# Optimizing a Trainium2 kernel written in Bass

```python
import numpy as np
import jax
import jax.numpy as jnp

def _softmax(x, axis=-1):
    return jax.nn.softmax(x, axis=axis)

def _gelu(x):
    return jax.nn.gelu(x, approximate=True)

def _silu(x):
    return jax.nn.silu(x)

def _sigmoid(x):
    return jax.nn.sigmoid(x)

def _layernorm(x, axis=-1, eps=1e-05):
    m = jnp.mean(x, axis=axis, keepdims=True)
    v = jnp.var(x, axis=axis, keepdims=True)
    return (x - m) / jnp.sqrt(v + eps)

def _scatter_add(tgt, idx, src, axis=0):
    return tgt.at[idx].add(src)

def _segment_sum(src, seg, n):
    return jax.ops.segment_sum(src, seg, n)
kernel_name = 'mk_macaron_d1_jaxref_r8_1ec511'

def setup_inputs(seed: int=0):
    np.random.seed(seed)
    _w = jnp.asarray

    def _L0_attn_setup():
        import jax, jax.numpy as jnp
        import numpy as np
        H_M, P_M, G_M, N_M, K_CONV, CHUNK = (128, 64, 8, 128, 4, 128)
        D_MODEL = 512
        D_INNER = H_M * P_M
        CONV_DIM = D_INNER + 2 * G_M * N_M
        PROJ_DIM = D_INNER + CONV_DIM + H_M
        EPS = 1e-05

        def segsum(x):
            l = x.shape[-1]
            xe = jnp.broadcast_to(x[..., None], x.shape + (l,))
            m1 = jnp.tril(jnp.ones((l, l), dtype=bool), -1)
            s = jnp.cumsum(jnp.where(m1, xe, 0.0), axis=-2)
            m2 = jnp.tril(jnp.ones((l, l), dtype=bool), 0)
            return jnp.where(m2, s, -jnp.inf)

        def causal_conv(x, w, bconv):
            k = w.shape[1]
            s = x.shape[1]
            xp = jnp.pad(x, ((0, 0), (k - 1, 0), (0, 0)))
            y = sum((xp[:, i:i + s, :] * w[:, i] for i in range(k)))
            return y + bconv
        key = jax.random.key(seed)
        ks = jax.random.split(key, 8)
        B_, S = (1, 256)
        sc = 0.02
        return {'x': jax.random.normal(ks[0], (B_, S, D_MODEL), dtype=jnp.float32), 'norm_w': jnp.ones((D_MODEL,), dtype=jnp.float32), 'in_proj_w': jax.random.normal(ks[1], (PROJ_DIM, D_MODEL), dtype=jnp.float32) * sc, 'conv_w': jax.random.normal(ks[2], (CONV_DIM, K_CONV), dtype=jnp.float32) * 0.2, 'conv_b': jnp.zeros((CONV_DIM,), dtype=jnp.float32), 'dt_bias': jax.random.uniform(ks[3], (H_M,), dtype=jnp.float32) * 0.1, 'A_log': jnp.log(1.0 + 15.0 * jax.random.uniform(ks[4], (H_M,), dtype=jnp.float32)), 'Dp': jnp.ones((H_M,), dtype=jnp.float32), 'gnorm_w': jnp.ones((D_INNER,), dtype=jnp.float32), 'out_proj_w': jax.random.normal(ks[5], (D_MODEL, D_INNER), dtype=jnp.float32) * sc}
    _L0_attn_in = _L0_attn_setup()

    def _L0_ffn_setup():
        import jax, jax.numpy as jnp
        import numpy as np
        ALPHA = 32
        R = 16
        SCALING = ALPHA / R
        key = jax.random.key(seed)
        k1, k2, k3, k4 = jax.random.split(key, 4)
        B_, S, D = (4, 256, 512)
        H, r, O = (8, R, 512)
        x = jax.random.normal(k1, (B_, S, D), dtype=jnp.float32)
        A = jax.random.normal(k2, (H, r, D), dtype=jnp.float32) * 0.02
        Bm = jax.random.normal(k3, (H, O, r), dtype=jnp.float32) * 0.02
        Wr = jax.random.normal(k4, (H, D), dtype=jnp.float32) * 0.02
        br = jnp.zeros((H,), dtype=jnp.float32)
        return {'x': x, 'A': A, 'B': Bm, 'Wr': Wr, 'br': br}
    _L0_ffn_in = _L0_ffn_setup()
    _d = {'L0_attn_x': _L0_attn_in['x'], 'L0_attn_norm_w': _L0_attn_in['norm_w'], 'L0_attn_in_proj_w': _L0_attn_in['in_proj_w'], 'L0_attn_conv_w': _L0_attn_in['conv_w'], 'L0_attn_conv_b': _L0_attn_in['conv_b'], 'L0_attn_dt_bias': _L0_attn_in['dt_bias'], 'L0_attn_A_log': _L0_attn_in['A_log'], 'L0_attn_Dp': _L0_attn_in['Dp'], 'L0_attn_gnorm_w': _L0_attn_in['gnorm_w'], 'L0_attn_out_proj_w': _L0_attn_in['out_proj_w'], 'L0_ffn_A': _L0_ffn_in['A'], 'L0_ffn_B': _L0_ffn_in['B'], 'L0_ffn_Wr': _L0_ffn_in['Wr'], 'L0_ffn_br': _L0_ffn_in['br']}
    _x0 = _d['L0_attn_x']
    _d['L0_attn_x'] = jax.random.normal(jax.random.fold_in(jax.random.key(seed), 1), (2, 512, 512), dtype=_x0.dtype)
    del _x0
    return _d

def reference(L0_attn_x, L0_attn_norm_w, L0_attn_in_proj_w, L0_attn_conv_w, L0_attn_conv_b, L0_attn_dt_bias, L0_attn_A_log, L0_attn_Dp, L0_attn_gnorm_w, L0_attn_out_proj_w, L0_ffn_A, L0_ffn_B, L0_ffn_Wr, L0_ffn_br):

    def _L0_attn_ref(x, norm_w, in_proj_w, conv_w, conv_b, dt_bias, A_log, Dp, gnorm_w, out_proj_w):
        import jax, jax.numpy as jnp
        import numpy as np
        H_M, P_M, G_M, N_M, K_CONV, CHUNK = (128, 64, 8, 128, 4, 128)
        D_MODEL = 512
        D_INNER = H_M * P_M
        CONV_DIM = D_INNER + 2 * G_M * N_M
        PROJ_DIM = D_INNER + CONV_DIM + H_M
        EPS = 1e-05

        def segsum(x):
            l = x.shape[-1]
            xe = jnp.broadcast_to(x[..., None], x.shape + (l,))
            m1 = jnp.tril(jnp.ones((l, l), dtype=bool), -1)
            s = jnp.cumsum(jnp.where(m1, xe, 0.0), axis=-2)
            m2 = jnp.tril(jnp.ones((l, l), dtype=bool), 0)
            return jnp.where(m2, s, -jnp.inf)

        def causal_conv(x, w, bconv):
            k = w.shape[1]
            s = x.shape[1]
            xp = jnp.pad(x, ((0, 0), (k - 1, 0), (0, 0)))
            y = sum((xp[:, i:i + s, :] * w[:, i] for i in range(k)))
            return y + bconv
        b, s, _ = x.shape
        residual = x
        h = x * jax.lax.rsqrt(jnp.mean(x * x, axis=-1, keepdims=True) + EPS) * norm_w
        proj = jnp.einsum('bsd,od->bso', h, in_proj_w)
        gate = proj[..., :D_INNER]
        hBC = proj[..., D_INNER:D_INNER + CONV_DIM]
        dt = proj[..., D_INNER + CONV_DIM:]
        hBC = jax.nn.silu(causal_conv(hBC, conv_w, conv_b))
        hid = hBC[..., :D_INNER].reshape(b, s, H_M, P_M)
        B = hBC[..., D_INNER:D_INNER + G_M * N_M].reshape(b, s, G_M, N_M)
        C = hBC[..., D_INNER + G_M * N_M:].reshape(b, s, G_M, N_M)
        dt = jax.nn.softplus(dt + dt_bias)
        A = -jnp.exp(A_log)
        pad = -s % CHUNK
        D_res = Dp[None, None, :, None] * hid
        hid_dt = hid * dt[..., None]
        A_full = A[None, None, :] * dt

        def padseq(t):
            return jnp.pad(t, [(0, 0), (0, pad)] + [(0, 0)] * (t.ndim - 2))
        hid_dt, A_full, Bp, Cp = (padseq(hid_dt), padseq(A_full), padseq(B), padseq(C))
        S = s + pad
        c, l = (S // CHUNK, CHUNK)
        hc = hid_dt.reshape(b, c, l, H_M, P_M)
        Ac = A_full.reshape(b, c, l, H_M).transpose(0, 3, 1, 2)
        rep = H_M // G_M
        Bh = jnp.repeat(Bp.reshape(b, c, l, G_M, N_M), rep, axis=3)
        Ch = jnp.repeat(Cp.reshape(b, c, l, G_M, N_M), rep, axis=3)
        A_cs = jnp.cumsum(Ac, axis=-1)
        L = jnp.exp(segsum(Ac))
        M = jnp.einsum('bcihn,bcjhn->bcijh', Ch, Bh) * jnp.transpose(L, (0, 2, 3, 4, 1))
        Y_diag = jnp.einsum('bcijh,bcjhp->bcihp', M, hc)
        decay_states = jnp.exp(A_cs[..., -1:] - A_cs)
        states = jnp.einsum('bclhn,bhcl,bclhp->bchpn', Bh, decay_states, hc)
        A_last = jnp.pad(A_cs[..., -1], ((0, 0), (0, 0), (1, 0)))
        decay_chunk = jnp.exp(segsum(A_last))
        states_cat = jnp.concatenate([jnp.zeros_like(states[:, :1]), states], axis=1)
        prev_states = jnp.einsum('bhij,bjhpn->bihpn', decay_chunk, states_cat)[:, :-1]
        Y_off = jnp.einsum('bclhn,bchpn,bhcl->bclhp', Ch, prev_states, jnp.exp(A_cs))
        y = (Y_diag + Y_off).reshape(b, S, H_M, P_M)[:, :s] + D_res
        y = y.reshape(b, s, D_INNER)
        yg = y * jax.nn.silu(gate)
        gsz = D_INNER // G_M
        ygr = yg.reshape(b, s, G_M, gsz)
        ygr = ygr * jax.lax.rsqrt(jnp.mean(ygr * ygr, axis=-1, keepdims=True) + EPS)
        y = ygr.reshape(b, s, D_INNER) * gnorm_w
        out = jnp.einsum('bsd,od->bso', y, out_proj_w)
        return residual + out

    def _L0_ffn_ref(x, A, B, Wr, br):
        import jax, jax.numpy as jnp
        import numpy as np
        ALPHA = 32
        R = 16
        SCALING = ALPHA / R
        H = A.shape[0]
        router_logits = jnp.einsum('bsd,hd->bsh', x, Wr) + br
        scores = H * jax.nn.softmax(router_logits, axis=-1)
        low = jnp.einsum('bsd,hrd->bshr', x, A)
        out = jnp.einsum('bshr,hor,bsh->bso', low, B, scores)
        return SCALING * out
    x = L0_attn_x
    x = x + 0.5 * _L0_ffn_ref(_layernorm(x, axis=-1), L0_ffn_A, L0_ffn_B, L0_ffn_Wr, L0_ffn_br)
    x = x + _L0_attn_ref(_layernorm(x, axis=-1), L0_attn_norm_w, L0_attn_in_proj_w, L0_attn_conv_w, L0_attn_conv_b, L0_attn_dt_bias, L0_attn_A_log, L0_attn_Dp, L0_attn_gnorm_w, L0_attn_out_proj_w)
    x = x + 0.5 * _L0_ffn_ref(_layernorm(x, axis=-1), L0_ffn_A, L0_ffn_B, L0_ffn_Wr, L0_ffn_br)
    return x

_drawn_inputs = setup_inputs


def setup_inputs(seed=0):
    import zlib

    import numpy as np

    out = dict(_drawn_inputs(seed))
    spreads = {'L0_attn_norm_w': (1.0, 0.2),
     'L0_attn_conv_b': (0.0, 0.1),
     'L0_attn_Dp': (1.0, 0.2),
     'L0_attn_gnorm_w': (1.0, 0.2),
     'L0_ffn_br': (0.0, 0.304)}
    factors = {'L0_attn_dt_bias': 8.0, 'L0_attn_A_log': 7.658}
    for name, (base, spread) in spreads.items():
        noise = np.random.default_rng([zlib.crc32(name.encode()), seed]).standard_normal(out[name].shape)
        drawn = base * np.exp(spread * noise) if base else spread * noise
        out[name] = jnp.asarray(drawn.astype(out[name].dtype))
    for name, factor in factors.items():
        out[name] = (out[name] * factor).astype(out[name].dtype)
    return out
```

```python
from contextlib import ExitStack

import concourse.bass as bass
from concourse import mybir

F32 = mybir.dt.float32
F32R = mybir.dt.float32r
BF16 = mybir.dt.bfloat16
ALU = mybir.AluOpType
ACT = mybir.ActivationFunctionType
AX = mybir.AxisListType

LN_EPS = 1e-5
RMS_EPS = 1e-5
EXP_FLOOR = -128.0


def macaron(nc, x, norm_w, in_proj_w, conv_w, conv_b, dt_bias, A_log, Dp, gnorm_w, out_proj_w,
            ffn_A, ffn_B, ffn_Wr, ffn_br, out):
    P = 128
    NB, S, DM = x.shape
    T = NB * S
    NCH = S // P
    NT = T // P
    KD = DM // P
    H = Dp.shape[0]
    DI = out_proj_w.shape[1]
    HP = DI // H
    CD, TAPS = conv_w.shape
    N = P
    G = (CD - DI) // (2 * N)
    TILES = DI // P
    TPG = TILES // G
    CT_ALL = CD // P
    FH, FR, _ = ffn_A.shape
    HR = FH * FR
    assert (P, H, HP, NT, S, DM) == (HR, P, P // 2, 8, 512, 512)
    FFN_SCALE = float(FH)

    x_d = x.rearrange("b (c p) d -> p (b c) d", p=P)
    out_d = out.rearrange("b (c p) d -> p (b c) d", p=P)
    A_d = ffn_A.rearrange("h r d -> (h r) d")
    B_d = ffn_B.rearrange("h (a p) r -> p a h r", p=P)
    outw_d = out_proj_w.rearrange("(a p) d -> p a d", p=P)
    HID0, B0, C0, DT0 = DI, 2 * DI, 2 * DI + G * N, DI + CD
    cs_d = nc.dram_tensor("cs_parts", [H, 3, T], BF16, kind="Internal").ap()
    ncs_d = nc.dram_tensor("ncs_parts", [H, 3, T], BF16, kind="Internal").ap()
    last_d = nc.dram_tensor("chunk_decay", [2 * NB, H], F32, kind="Internal").ap()

    with ExitStack() as ctx:
        sem = lambda name: ctx.enter_context(nc.semaphore(name))
        ps = lambda name, dt=F32: ctx.enter_context(nc.psum_tensor(name, [P, 2, 512], dt))

        size = nc.sbuf_usable_end - nc.sbuf_base - 160
        ctx.enter_context(nc.sbuf_tensor("arena", [P, size // 4], F32))
        end = nc.sbuf_base
        cursor = [(end - size // 4 * 4 + 31) // 32 * 32]
        widths = {F32: 4, F32R: 4, BF16: 2}

        def put(name, shape, dt, at=None):
            n = widths[dt]
            for k in shape[1:]:
                n *= k
            if at is None:
                at = cursor[0]
                cursor[0] += (n + 31) // 32 * 32
                assert cursor[0] <= end, (name, cursor[0], end)
            return nc.alloc_sbuf_tensor_at(name, shape, dt, offset=at), at

        HTh, _ = put("hT_hi", [P, KD, T], F32R)
        HTl, _ = put("hT_lo", [P, KD, T], F32R)
        XR, _ = put("residual", [P, NT, DM], F32)
        YG, yg_at = put("yg", [P, TPG, T], F32)
        YS, ys_at = put("yg_split", [P, 2, 2, 4, P], F32R)
        WOh, wo_at = put("wo_hi", [P, TPG, DM], F32R)
        WOl, _ = put("wo_lo", [P, TPG, DM], F32R)
        raw_h, _ = put("raw_hid", [P, KD, P], F32)
        raw_g, _ = put("raw_gate", [P, KD, P], F32)
        raw_o, _ = put("raw_out", [P, KD, P], F32)
        raw_b, _ = put("raw_bc", [P, KD, P], F32)
        WTh = put("wt_hid", [P, 2, KD, P], F32R)[0]
        WTg = put("wt_gate", [P, 2, KD, P], F32R)[0]
        WTb = put("wt_bc", [P, 2, KD, P], F32R, at=ys_at)[0]
        hidT, _ = put("hidT", [P, T], F32)
        sg, _ = put("silu_gate", [P, T], F32)
        hcA, _ = put("hid_dt_even", [P, NT, P], F32)
        hcB, _ = put("hid_dt_odd", [P, NT, P], F32)
        XD, _ = put("hid_dt_decay", [P, NB, NCH - 1, P], F32)
        LM, lm_at = put("scores", [P, 2, NB, NCH, P], F32)
        E, _ = put("decay_in", [P, NB, NCH, P], F32)
        CT, _ = put("C_T", [P, T], F32)
        BT, _ = put("B_T", [P, T], F32)
        GM, _ = put("CB_masked", [P, NT, P], F32)
        BTok, _ = put("B_tok", [P, NT, P], F32)
        dtk, _ = put("dt_tok", [P, NT, H], F32)
        dck, _ = put("decay_tok", [P, NT, H], F32)
        EL, _ = put("chunk_decays", [P, NB, 2, H], F32)
        ST, _ = put("states", [P, NB, NCH - 1, P], F32)
        SQ, _ = put("sum_sq", [P, T], F32)
        RP, _ = put("cs_by_chunk", [112, NT, P], BF16)
        LH, _ = put("cs_weights", [112, 2, P], BF16)
        CS, _ = put("cs_rows", [48, P], BF16)
        selE, _ = put("head_rows", [48, P], BF16)
        OH, _ = put("chunk_rows", [112, NT], BF16)
        OHf, _ = put("chunk_rows_f", [112, NT], F32)
        ident, _ = put("ident", [P, P], F32)
        causal, _ = put("causal", [P, P], F32)
        cw, _ = put("conv_w", [P, CT_ALL, TAPS], F32)
        cb, _ = put("conv_b", [P, CT_ALL], F32)
        Dc, _ = put("D_col", [P, TILES], F32)
        gw, _ = put("gnorm_col", [P, TILES], F32)
        nw, _ = put("norm_col", [P, KD], F32)
        dtb, _ = put("dt_bias", [P, 1], F32)
        negA, _ = put("neg_A", [P, 1], F32)
        ones, _ = put("ones", [P, 1], F32)
        half, _ = put("minus_half", [P, NT], F32)
        vs, _ = put("mean_sq", [P, NT], F32)
        rg, _ = put("rms_factor", [P, NT], F32)

        at = yg_at
        XH, _ = put("normed", [P, NT, DM], F32, at=at); at += NT * DM * 4
        TT, _ = put("normed_T", [P, 2, KD, P], F32, at=at); at += 2 * DM * 4
        A_raw, _ = put("A_raw", [P, DM], F32, at=at); at += DM * 4
        Wr_raw, _ = put("Wr_raw", [FH, DM], F32, at=at); at += DM * 4
        B_raw, _ = put("B_raw", [P, KD, FH, FR], F32, at=at); at += DM * 4
        AT, _ = put("A_T", [P, KD, HR + FH], F32, at=at); at += KD * (HR + FH) * 4
        assert at <= yg_at + TPG * T * 4
        at = lm_at
        BTm, _ = put("B_mix_T", [P, DM], F32, at=at); at += DM * 4
        low, _ = put("low", [P, NT, HR + FH], F32, at=at); at += NT * (HR + FH) * 4
        LS, _ = put("low_scored", [P, NT, HR], F32, at=at); at += NT * HR * 4
        LST, _ = put("low_scored_T", [P, NT, P], F32, at=at); at += NT * P * 4
        brb, _ = put("br_rows", [P, FH], F32, at=at); at += 32
        lg, _ = put("logits", [P, NT, FH], F32, at=at); at += NT * FH * 4
        pe_, _ = put("score_exp", [P, NT, FH], F32, at=at); at += NT * FH * 4
        pw, _ = put("score", [P, NT, FH], F32, at=at); at += NT * FH * 4
        mx, _ = put("row_max", [P, NT], F32, at=at); at += 32
        sm, _ = put("row_sum", [P, NT], F32, at=at); at += 32
        bst, _ = put("bn_st", [P, NT, 6], F32, at=at); at += NT * 24
        bag, _ = put("bn_ag", [P, NT, 2], F32, at=at); at += NT * 8
        rs, _ = put("ln_factor", [P, NT], F32, at=at); at += 32
        rv, _ = put("ln_var", [P, NT], F32, at=at); at += 32
        s2, _ = put("xn_sq", [P, NT], F32, at=at); at += 32
        at = yg_at
        dtS = []
        for k in range(7):
            dtS.append(put(f"dt_step{k}", [P, T], F32, at=at)[0]); at += T * 4
        parts = [put(f"cs_part{k}", [P, T], BF16, at=wo_at + k * T * 2)[0] for k in range(6)]
        at = wo_at + 6 * T * 2
        cwr, _ = put("conv_w_rows", [CT_ALL, P * TAPS], F32, at=at); at += P * TAPS * 4
        cbr, _ = put("conv_b_rows", [CT_ALL, P], F32, at=at); at += P * 4
        gwr, _ = put("gnorm_rows", [TILES, P], F32, at=at); at += P * 4
        nwr, _ = put("norm_rows", [KD, P], F32, at=at); at += P * 4
        Drow, _ = put("D_rows", [P, H], F32, at=at); at += H * 4
        assert at <= wo_at + TPG * DM * 4
        WTd = put("wt_dt", [P, 2, KD, P], F32R, at=wo_at + TPG * DM * 4)[0]

        psR, psP, psX, psD = ps("psR"), ps("psP"), ps("psX"), ps("psD")
        BANKS = {"R": psR, "P": psP, "X": psX, "D": psD}

        def family(tag):
            return ({b: [sem(f"{tag}_full_{b}{i}") for i in range(2)] for b in BANKS},
                    {b: [sem(f"{tag}_free_{b}{i}") for i in range(2)] for b in BANKS})

        o_full, o_free = family("once")
        t_full, t_free = family("tile")
        l_full, l_free = family("tail")
        PT = {"R": (4, 4), "P": (3, 3), "X": (3, 2), "D": (1, 1)}
        PL = {"R": (2, 1), "P": (2, 2), "X": (1, 1), "D": (5, 5)}

        x_in = sem("x_in"); tab_in = sem("tables_in"); ffw_in = sem("ffn_weights_in")
        rawh_in = sem("raw_hid_in"); rawg_in = sem("raw_gate_in"); rawo_in = sem("raw_out_in")
        rawb_in = sem("raw_bc_in")
        neg_in = sem("neg_cs_in"); cs_in = sem("cs_in"); last_in = sem("chunk_decay_in")
        scratch_out = sem("scratch_written"); y_out = sem("result_written")
        ident_ok = sem("identity_made"); const_ok = sem("constants_made"); pool_link = sem("pool_step")
        zero_ok = sem("hid_dt_cleared"); dve_link = sem("vector_step")
        ln_var = sem("ln_variance"); ln_fac = sem("ln_factor_made")
        xh_ok = sem("normed_made"); smx_in = sem("score_logits_made"); smx_exp = sem("score_exp_made")
        ls_ok = sem("low_scored_made"); xn_sq = sem("xn_squares_summed")
        h_ok = sem("h_made"); h_tmp = sem("h_T_scaled"); h_hi = sem("h_hi_made")
        wd_hi = sem("wt_dt_hi_made"); a_exp = sem("A_exp_made"); dt_act = sem("dt_scalar_step")
        cs_ok = sem("running_sums_made"); part_ok = sem("cs_part_made"); tok_ok = sem("dt_made")
        wth_hi = sem("wt_hid_hi_made"); wtg_hi = sem("wt_gate_hi_made"); wtb_hi = sem("wt_bc_hi_made")
        wo_hi = sem("wo_hi_made")
        tap_ok = sem("hid_tap_made"); conv_st = sem("hid_conv_step"); hid_ok = sem("hid_made")
        btap_ok = sem("bc_tap_made"); bconv_st = sem("bc_conv_step"); bc_ok = sem("bc_made")
        rp_ok = sem("cs_by_chunk_made"); exp_ok = sem("decay_exp_made"); m_ok = sem("scores_made")
        xd_ok = sem("hid_dt_decay_made"); st_step = sem("state_step")
        dh_ok = sem("D_hid_made"); ydiag_ok = sem("chunk_part_added"); yoff_ok = sem("state_part_made")
        pool_y = sem("y_step"); r_ok = sem("rms_factor_made"); sq_zero = sem("sum_sq_cleared")
        ys_hi = sem("ys_hi_made"); ys_ok = sem("ys_made"); ys_used = sem("ys_first_half_used")

        block = ctx.enter_context(nc.Block())

        def every(e, tile, tail):
            with e.Fori(0, G - 1) as g:
                with e.Fori(0, TPG) as s:
                    tile(TPG * g + s, s, g, False)
                tail(g, False)
            with e.Fori(0, TPG - 1) as s:
                tile(TPG * (G - 1) + s, s, G - 1, False)
            tile(TILES - 1, TPG - 1, G - 1, True)
            tail(G - 1, True)

        def apart(e):
            e.nop(nofuse=True)

        ONCE = {}
        seen = {(b, i): 0 for b in BANKS for i in range(2)}

        def use(name, b, i):
            ONCE[name] = (b, i, seen[b, i])
            seen[b, i] += 1

        def ffn_uses(f):
            use(f"A{f}", "R", 0); use(f"Wr{f}", "R", 1); use(f"B{f}", "P", 0)
            for k in range(NT):
                use(f"xT{f}{k}", "R", k % 2); use(f"low{f}{k}", "P", k % 2)
            for i in range(2):
                use(f"lsT{f}{i}", "X", i)
            for k in range(NT):
                use(f"ffn{f}{k}", "D", k % 2)

        use("tables", "D", 0)
        ffn_uses(0)
        for k in range(NT):
            use(f"hT{k}", "R", k % 2)
        use("WdT", "P", 0); use("dt0", "P", 0); use("dt1", "P", 1)
        for q in range(2):
            use(f"bcW{q}", "R", 0)
            for i in range(2):
                use(f"bc{q}{i}", "P", i)
        use("hW0", "P", 0); use("h0", "P", 0); use("h1", "P", 1); use("hW1", "P", 0); use("gW0", "P", 1)
        for i in range(2):
            use(f"dttok{i}", "R", i); use(f"dctok{i}", "X", i)
        for i in range(2):
            use(f"CB{i}", "D", i); use(f"Bt{i}", "X", i)
        before_loop = dict(seen)
        ffn_uses(1)

        def full(e, name):
            b, i, n = ONCE[name]
            e.wait_ge(o_full[b][i], n + 1)

        def free_sem(name):
            b, i, _ = ONCE[name]
            return o_free[b][i]

        def freed(e, name):
            b, i, n = ONCE[name]
            e.wait_ge(o_free[b][i], n + 1)

        def ready(e, name):
            b, i, n = ONCE[name]
            if n:
                e.wait_ge(o_free[b][i], n)

        def bank(name):
            b, i, _ = ONCE[name]
            return BANKS[b][:, i, :]

        @block.sync
        def _(sp):
            def ffn_weights():
                sp.dma_start(A_raw[:], A_d).then_inc(ffw_in, 16)
                sp.dma_start(Wr_raw[:], ffn_Wr).then_inc(ffw_in, 16)
                for a in range(KD):
                    sp.dma_start(B_raw[:, a], B_d[:, a]).then_inc(ffw_in, 16)
                sp.dma_start(brb[:], ffn_br.rearrange("(a h) -> a h", a=1).to_broadcast([P, FH])).then_inc(ffw_in, 16)

            def rows(dst, first, s):
                sp.dma_start(dst[:].rearrange("p a d -> p (a d)"),
                             in_proj_w[bass.ds(first, P), :]).then_inc(s, 16)

            def out_cols(t):
                sp.dma_start(raw_o[:], outw_d[:, :, bass.ds(t * P, P)]).then_inc(rawo_in, 16)

            def neg_rows(t):
                for h in range(2):
                    src = ncs_d[bass.ds(2 * t + h, 1)].rearrange("h q (c i) -> (h q c) i", c=NT)
                    sp.dma_start(LH[64 + 24 * h:88 + 24 * h, h, :], src).then_inc(neg_in, 16)

            def cs_rows(t):
                src = cs_d[bass.ds(2 * t, 2)].rearrange("h q (c i) -> (h q c) i", c=NT)
                sp.dma_start(CS[:], src).then_inc(cs_in, 16)

            for k in range(0, NT, 2):
                sp.dma_start(XR[:, k:k + 2], x_d[:, k:k + 2]).then_inc(x_in, 16)
            ffn_weights()
            for dst, src in (
                (cwr[:], conv_w.rearrange("(t p) k -> t (p k)", p=P)),
                (cbr[:], conv_b.rearrange("(t p) -> t p", p=P)),
                (gwr[:], gnorm_w.rearrange("(t p) -> t p", p=P)),
                (nwr[:], norm_w.rearrange("(t p) -> t p", p=P)),
                (dtb[:], dt_bias.rearrange("(h a) -> h a", a=1)),
                (negA[:], A_log.rearrange("(h a) -> h a", a=1)),
                (Drow[:], Dp.rearrange("(a h) -> a h", a=1).to_broadcast([P, H])),
            ):
                sp.dma_start(dst, src).then_inc(tab_in, 16)
            rows(raw_g, DT0, rawg_in)
            rows(raw_b, B0, rawb_in)
            rows(raw_h, HID0, rawh_in)
            sp.dma_start(raw_o[:], outw_d[:, :, 0:P]).then_inc(rawo_in, 16)
            full(sp, "WdT")
            rows(raw_g, 0, rawg_in)
            full(sp, "bcW0")
            rows(raw_b, C0, rawb_in)
            full(sp, "bcW1")
            rows(raw_b, B0 + P, rawb_in)
            full(sp, "hW0")
            rows(raw_h, HID0 + P, rawh_in)
            for q in range(6):
                sp.wait_ge(part_ok, q + 1)
                sp.dma_start((cs_d if q < 3 else ncs_d)[:, q % 3], parts[q][:]).then_inc(scratch_out, 16)
            sp.wait_ge(dt_act, 5)
            for b in range(NB):
                for c in range(2):
                    k = b * NCH + c + 1
                    sp.dma_start(last_d[2 * b + c].rearrange("(h a) -> h a", a=1),
                                 dtS[6][:, k:k + 1]).then_inc(scratch_out, 16)
            sp.wait_ge(scratch_out, 16 * 10)
            sp.dma_start(EL[:].rearrange("p b c h -> p (b c h)"),
                         last_d.rearrange("(a k) h -> a (k h)", a=1).to_broadcast([P, 2 * NB * H])).then_inc(last_in, 16)
            neg_rows(0)
            cs_rows(0)
            full(sp, "hW1")
            rows(raw_h, HID0 + 2 * P, rawh_in)
            full(sp, "gW0")
            rows(raw_g, P, rawg_in)

            def tile(t, s, g, last):
                if last:
                    return
                sp.wait_ge(t_full["X"][0], 3 * t + 1)
                out_cols(t + 1)
                sp.wait_ge(t_full["R"][1], 4 * t + 3)
                neg_rows(t + 1)
                sp.wait_ge(rp_ok, t + 1)
                cs_rows(t + 1)
                sp.wait_ge(t_full["P"][0], 3 * t + 3)
                rows(raw_h, HID0 + (t + 3) * P, rawh_in)
                sp.wait_ge(t_full["P"][1], 3 * t + 3)
                rows(raw_g, (t + 2) * P, rawg_in)

            def tail(g, last):
                if last:
                    return
                sp.wait_ge(l_full["R"][0], 2 * g + 1)
                rows(raw_b, C0 + (g + 1) * P, rawb_in)
                sp.wait_ge(l_full["R"][0], 2 * g + 2)
                rows(raw_b, B0 + (g + 2) * P, rawb_in)

            every(sp, tile, tail)
            sp.wait_ge(l_free["D"][1], 5 * (G - 1) + 4)
            ffn_weights()
            for k in range(NT):
                freed(sp, f"ffn1{k}")
                sp.dma_start(out_d[:, k], XR[:, k]).then_inc(y_out, 16)
            sp.wait_ge(y_out, 16 * NT)

        @block.tensor
        def _(pe):
            def transposes(name, blocks, out_ap=None):
                ready(pe, name)
                dst = bank(name) if out_ap is None else out_ap
                for k, a in enumerate(blocks):
                    w = a.shape[0]
                    last = pe.transpose(dst[0:a.shape[1], k * w:(k + 1) * w], a, ident[0:w, 0:w])
                b, i, _ = ONCE[name]
                last.then_inc(o_full[b][i], 1)

            def project(dst, wt, b):
                n = 0
                cols = slice(b * S, (b + 1) * S)
                for a in range(KD):
                    for w, h in ((wt[:, 0, a], HTh), (wt[:, 0, a], HTl), (wt[:, 1, a], HTh)):
                        last = pe.matmul(dst, w, h[:, a, cols], start=(n == 0), stop=(n == 3 * KD - 1))
                        n += 1
                return last

            def cb(psum, i):
                for c in range(NCH):
                    k = (i * NCH + c) * P
                    last = pe.matmul(psum[:, c * P:(c + 1) * P], BT[:, k:k + P], CT[:, k:k + P],
                                     start=True, stop=True)
                return last

            def b_tok(psum, i):
                for c in range(NCH):
                    k = (i * NCH + c) * P
                    last = pe.transpose(psum[:, c * P:(c + 1) * P], BT[:, k:k + P], ident[:])
                return last

            def w_blocks(raw):
                return [raw[:, a, :] for a in range(KD)]

            def ffn(f):
                pe.wait_ge(ffw_in, 16 * (3 + KD) * (f + 1))
                transposes(f"A{f}", [A_raw[:, a * P:(a + 1) * P] for a in range(KD)])
                transposes(f"Wr{f}", [Wr_raw[:, a * P:(a + 1) * P] for a in range(KD)])
                transposes(f"B{f}", [B_raw[:, a].rearrange("p h r -> p (h r)") for a in range(KD)])
                for k in range(NT + 1):
                    if k < NT:
                        pe.wait_ge(xh_ok, 2 * NT * f + k + 1)
                        transposes(f"xT{f}{k}", [XH[:, k, a * P:(a + 1) * P] for a in range(KD)])
                    if k:
                        j = k - 1
                        freed(pe, f"A{f}")
                        freed(pe, f"Wr{f}")
                        freed(pe, f"xT{f}{j}")
                        ready(pe, f"low{f}{j}")
                        for a in range(KD):
                            last = pe.matmul(bank(f"low{f}{j}")[:, 0:HR + FH], TT[:, j % 2, a], AT[:, a],
                                             start=(a == 0), stop=(a == KD - 1))
                        last.then_inc(o_full["P"][j % 2], 1)
                for i in range(2):
                    pe.wait_ge(ls_ok, f + 1)
                    transposes(f"lsT{f}{i}", [LS[:, 4 * i + c] for c in range(4)])
                for k in range(NT):
                    freed(pe, f"B{f}")
                    freed(pe, f"lsT{f}{k // 4}")
                    ready(pe, f"ffn{f}{k}")
                    pe.matmul(bank(f"ffn{f}{k}"), LST[:, k], BTm[:], start=True, stop=True
                              ).then_inc(o_full["D"][k % 2], 1)

            pe.wait_ge(ident_ok, 1)
            pe.wait_ge(tab_in, 16 * 7)
            at = 0
            for rows in [cwr[:, k::TAPS] for k in range(TAPS)] + [cbr[:], gwr[:], nwr[:]]:
                n = rows.shape[0]
                mm = pe.transpose(psD[:, 0, at:at + n], rows, ident[0:n, 0:n])
                at += n
            mm.then_inc(o_full["D"][0], 1)
            ffn(0)
            for k in range(NT):
                pe.wait_ge(h_ok, k + 1)
                transposes(f"hT{k}", [XH[:, k, a * P:(a + 1) * P] for a in range(KD)])
            pe.wait_ge(rawg_in, 16)
            transposes("WdT", w_blocks(raw_g))
            freed(pe, "WdT")
            for k in range(NT - 2, NT):
                freed(pe, f"hT{k}")
            for b in range(NB):
                ready(pe, f"dt{b}")
                project(bank(f"dt{b}"), WTd, b).then_inc(o_full["P"][b], 1)
            for q in range(2):
                pe.wait_ge(rawb_in, 16 * (q + 1))
                transposes(f"bcW{q}", w_blocks(raw_b))
                freed(pe, f"bcW{q}")
                for b in range(NB):
                    ready(pe, f"bc{q}{b}")
                    project(bank(f"bc{q}{b}"), WTb, b).then_inc(o_full["P"][b], 1)
            pe.wait_ge(rawh_in, 16)
            transposes("hW0", w_blocks(raw_h))
            freed(pe, "hW0")
            for b in range(NB):
                ready(pe, f"h{b}")
                project(bank(f"h{b}"), WTh, b).then_inc(o_full["P"][b], 1)
            pe.wait_ge(rawh_in, 32)
            transposes("hW1", w_blocks(raw_h))
            pe.wait_ge(rawg_in, 32)
            transposes("gW0", w_blocks(raw_g))
            pe.wait_ge(tok_ok, 1)
            for i in range(2):
                transposes(f"dttok{i}", [dtS[2][:, (4 * i + c) * P:(4 * i + c + 1) * P] for c in range(4)])
            pe.wait_ge(dt_act, 4)
            for i in range(2):
                transposes(f"dctok{i}", [dtS[5][:, (4 * i + c) * P:(4 * i + c + 1) * P] for c in range(4)])
            for i in range(2):
                pe.wait_ge(bc_ok, 4)
                ready(pe, f"CB{i}")
                cb(bank(f"CB{i}"), i).then_inc(o_full["D"][i], 1)
                ready(pe, f"Bt{i}")
                b_tok(bank(f"Bt{i}"), i).then_inc(o_full["X"][i], 1)
            for (b, i), n in before_loop.items():
                pe.wait_ge(o_free[b][i], n)
            pe.wait_ge(const_ok, 1)

            def tile(t, s, g, last):
                def fill(b, i, k):
                    pe.wait_ge(t_free[b][i], PT[b][i] * t + k)

                for b in range(NB):
                    pe.wait_ge(hid_ok, 2 * t + b + 1)
                    fill("R", b, 0)
                    for c in range(NCH):
                        k = (b * NCH + c) * P
                        mm = pe.transpose(psR[:, b, c * P:(c + 1) * P], hidT[:, k:k + P], ident[:])
                    mm.then_inc(t_full["R"][b], 1)

                def hid_next(b):
                    if not last:
                        fill("P", b, 0)
                        project(psP[:, b], WTh, b).then_inc(t_full["P"][b], 1)

                def decay(h):
                    for b in range(NB):
                        if h == 0 and b == 0:
                            pe.wait_ge(neg_in, 32 * (t + 1))
                            pe.wait_ge(rp_ok, t + 1)
                        fill("R", b, 1 + h)
                        pe.matmul(psR[:, b], LH[:, h], RP[:, NCH * b:NCH * (b + 1)].rearrange("k c i -> k (c i)"),
                                  start=True, stop=True).then_inc(t_full["R"][b], 1)

                gk = 0 if last else 1

                def gate(b):
                    fill("P", b, gk)
                    project(psP[:, b], WTg, b).then_inc(t_full["P"][b], 1)

                hid_next(0)
                decay(0)
                pe.wait_ge(rawo_in, 16 * (t + 1))
                fill("X", 0, 0)
                for a in range(KD):
                    mm = pe.transpose(psX[:, 0, a * P:(a + 1) * P], raw_o[:, a], ident[:])
                mm.then_inc(t_full["X"][0], 1)
                hid_next(1)
                decay(1)
                for b in range(NB):
                    fill("R", b, 3)
                    pe.matmul(psR[:, b], selE[:], RP[0:48, NCH * b:NCH * (b + 1)].rearrange("k c i -> k (c i)"),
                              start=True, stop=True).then_inc(t_full["R"][b], 1)
                gate(0)
                for b in range(NB):
                    pe.wait_ge(xd_ok, 4 * t + 2 * b + 2)
                    fill("X", b, 1 - b)
                    for c in range(NCH - 1):
                        mm = pe.matmul(psX[:, b, c * P:(c + 1) * P], BTok[:, b * NCH + c], XD[:, b, c],
                                       start=True, stop=True)
                    mm.then_inc(t_full["X"][b], 1)
                gate(1)
                for b in range(NB):
                    fill("D", b, 0)
                    pe.wait_ge(m_ok, 4 * t + 2 * b + 2)
                    for c in range(NCH):
                        pe.matmul(psD[:, b, c * P:(c + 1) * P], hcA[:, b * NCH + c], LM[:, 0, b, c],
                                  start=True, stop=False)
                        mm = pe.matmul(psD[:, b, c * P:(c + 1) * P], hcB[:, b * NCH + c], LM[:, 1, b, c],
                                       start=False, stop=True)
                    mm.then_inc(t_full["D"][b], 1)
                    if not last:
                        pe.wait_ge(rawg_in if b else rawh_in, 16 * (t + 3))
                        fill("P", b, 2)
                        for a in range(KD):
                            mm = pe.transpose(psP[:, b, a * P:(a + 1) * P], (raw_g if b else raw_h)[:, a], ident[:])
                        mm.then_inc(t_full["P"][b], 1)
                for b in range(NB):
                    fill("X", b, 2 - b)
                    if b == 0:
                        pe.wait_ge(t_free["X"][1], 2 * t + 1)
                    for c in range(NCH - 1):
                        k = (b * NCH + c + 1) * P
                        mm = pe.matmul(psX[:, b, c * P:(c + 1) * P], ST[:, b, c], CT[:, k:k + P],
                                       start=True, stop=True)
                    mm.then_inc(t_full["X"][b], 1)
                if not last:
                    pe.wait_ge(t_free["P"][1], 3 * t + 3)

            def tail(g, last):
                t1 = TPG * (g + 1)
                for b in ("R", "X", "D", "P"):
                    for i in range(2):
                        pe.wait_ge(t_free[b][i], PT[b][i] * t1 - (2 if last and b == "P" else 0))
                if not last:
                    for q in range(2):
                        pe.wait_ge(rawb_in, 16 * (2 * g + q + 3))
                        if q:
                            pe.wait_ge(l_free["R"][0], 2 * g + 1)
                        for a in range(KD):
                            mm = pe.transpose(psR[:, 0, a * P:(a + 1) * P], raw_b[:, a], ident[:])
                        mm.then_inc(l_full["R"][0], 1)
                        for b in range(NB):
                            pe.wait_ge(l_free["R"][0], 2 * g + q + 1)
                            if q:
                                pe.wait_ge(l_free["P"][b], 2 * g + 1)
                            project(psP[:, b], WTb, b).then_inc(l_full["P"][b], 1)
                pe.wait_ge(pool_y, 4 * t1)
                for k in range(NT):
                    mm = pe.matmul(psR[:, 1, k:k + 1], SQ[:, k * P:(k + 1) * P], ones[:], start=True, stop=True)
                mm.then_inc(l_full["R"][1], 1)
                for m in range(NT):
                    if m == 4 and not last:
                        pe.wait_ge(bc_ok, 4 * (g + 2))
                        for i in range(2):
                            pe.wait_ge(l_free["D"][i], 5 * g + 2)
                            cb(psD[:, i], i).then_inc(l_full["D"][i], 1)
                            b_tok(psX[:, i], i).then_inc(l_full["X"][i], 1)
                    k = m // 2 + (1 if m >= 4 and not last else 0)
                    if k:
                        pe.wait_ge(l_free["D"][m % 2], 5 * g + k)
                    n = 0
                    for hf in range(2):
                        pe.wait_ge(ys_ok, 2 * NT * g + 2 * m + hf + 1)
                        for j in range(4):
                            kt = 4 * hf + j
                            for y, w in ((YS[:, hf, 0, j], WOh), (YS[:, hf, 0, j], WOl), (YS[:, hf, 1, j], WOh)):
                                mm = pe.matmul(psD[:, m % 2], y, w[:, kt], start=(n == 0), stop=(n == 23))
                                n += 1
                                if n == 12:
                                    mm.then_inc(ys_used, 1)
                    mm.then_inc(l_full["D"][m % 2], 1)
                if not last:
                    for b in ("X", "D", "P", "R"):
                        for i in range(2):
                            pe.wait_ge(l_free[b][i], PL[b][i] * (g + 1))

            every(pe, tile, tail)
            pe.wait_ge(l_free["D"][0], 5 * (G - 1) + 4)
            pe.wait_ge(l_free["D"][1], 5 * (G - 1) + 4)
            ffn(1)

        @block.scalar
        def _(act):
            def tap(dst, src, ct, looped=False):
                if looped:
                    apart(act)
                return act.activation(dst, src, ACT.Identity, scale=cw[:, bass.ds(ct, 1), TAPS - 1],
                                      bias=cb[:, bass.ds(ct, 1)])

            def split_hi(dst, src):
                return act.activation(dst, src, ACT.Copy)

            def flat(w):
                return w.rearrange("p a c -> p (a c)")

            def ffn(f):
                full(act, f"A{f}")
                act.activation(AT[:, :, 0:HR], bank(f"A{f}").rearrange("p (a c) -> p a c", a=KD), ACT.Copy
                               ).then_inc(free_sem(f"A{f}"), 1)
                full(act, f"Wr{f}")
                act.activation(AT[:, :, HR:], bank(f"Wr{f}")[:, 0:KD * FH].rearrange("p (a c) -> p a c", a=KD),
                               ACT.Copy).then_inc(free_sem(f"Wr{f}"), 1)
                full(act, f"B{f}")
                act.activation(BTm[:], bank(f"B{f}"), ACT.Copy).then_inc(free_sem(f"B{f}"), 1)
                for k in range(NT):
                    full(act, f"xT{f}{k}")
                    if k >= 2:
                        full(act, f"low{f}{k - 2}")
                    act.activation(flat(TT[:, k % 2]), bank(f"xT{f}{k}"), ACT.Copy
                                   ).then_inc(free_sem(f"xT{f}{k}"), 1)
                act.wait_ge(smx_in, f + 1)
                act.activation(pe_[:], lg[:], ACT.Exp).then_inc(smx_exp, 1)
                for i in range(2):
                    full(act, f"lsT{f}{i}")
                    act.activation(flat(LST[:, 4 * i:4 * i + 4]), bank(f"lsT{f}{i}"),
                                   ACT.Copy).then_inc(free_sem(f"lsT{f}{i}"), 1)

            ffn(0)
            for k in range(NT):
                act.wait_ge(xh_ok, NT + k + 1)
                full(act, f"ffn0{NT - 1 - (k + 1) % 2}")
                if k >= 2:
                    act.wait_ge(xn_sq, k - 1)
                act.activation(flat(LST[:, 4 * (k % 2):4 * (k % 2) + 4]), XH[:, k], ACT.Square,
                               accum_out=s2[:, k:k + 1]).then_inc(xn_sq, 1)
            for k in range(NT):
                act.wait_ge(h_tmp, k + 1)
                act.activation(HTh[:, :, k * P:(k + 1) * P], TT[:, k % 2], ACT.Copy).then_inc(h_hi, 1)
            act.wait_ge(tab_in, 16 * 7)
            freed(act, "tables")
            act.activation(negA[:], negA[:], ACT.Exp).then_inc(a_exp, 1)
            full(act, "WdT")
            act.activation(flat(WTd[:, 0]), bank("WdT"), ACT.Copy).then_inc(wd_hi, 1)
            for b in range(NB):
                freed(act, f"dt{b}")
            act.activation(dtS[1][:], dtS[0][:], ACT.Abs).then_inc(dt_act, 1)
            act.wait_ge(dt_act, 1)
            act.activation(dtS[3][:], dtS[1][:], ACT.Exp, scale=-1.0).then_inc(dt_act, 1)
            act.wait_ge(dt_act, 2)
            act.activation(dtS[4][:], dtS[3][:], ACT.Ln, bias=1.0).then_inc(dt_act, 1)

            def bc_taps(q, b, src, ct, looped):
                dst = (BT, CT)[q]
                tap(dst[:, b * S:(b + 1) * S], src, ct, looped).then_inc(btap_ok, 1)

            def bc_silu(q, b):
                dst = (BT, CT)[q][:, b * S:(b + 1) * S]
                act.activation(dst, dst, ACT.Silu).then_inc(bc_ok, 1)

            for q in range(2):
                full(act, f"bcW{q}")
                act.activation(flat(WTb[:, 0]), bank(f"bcW{q}"), ACT.Copy).then_inc(wtb_hi, 1)
                for b in range(NB):
                    full(act, f"bc{q}{b}")
                    bc_taps(q, b, bank(f"bc{q}{b}"), TILES + G * q, False)
                if q == 0:
                    act.wait_ge(cs_ok, 1)
                    for k in range(NT):
                        e = act.activation(dtS[5][:, k * P:(k + 1) * P], dtS[4][:, k * P:(k + 1) * P], ACT.Exp,
                                           scale=-1.0, bias=dtS[4][:, (k + 1) * P - 1:(k + 1) * P])
                    e.then_inc(dt_act, 1)
                    act.activation(dtS[6][:, 0:NT], dtS[4][:, P - 1::P], ACT.Exp).then_inc(dt_act, 1)
            full(act, "hW0")
            act.activation(flat(WTh[:, 0]), bank("hW0"), ACT.Copy).then_inc(wth_hi, 1)
            for b in range(NB):
                full(act, f"h{b}")
                tap(hidT[:, b * S:(b + 1) * S], bank(f"h{b}"), 0).then_inc(tap_ok, 1)
            full(act, "hW1")
            act.activation(flat(WTh[:, 0]), bank("hW1"), ACT.Copy).then_inc(wth_hi, 1)
            full(act, "gW0")
            act.activation(flat(WTg[:, 0]), bank("gW0"), ACT.Copy).then_inc(wtg_hi, 1)
            for q in range(2):
                for b in range(NB):
                    freed(act, f"bc{q}{b}")
                    bc_silu(q, b)
            for b in range(NB):
                freed(act, f"h{b}")
                act.activation(hidT[:, b * S:(b + 1) * S], hidT[:, b * S:(b + 1) * S], ACT.Silu).then_inc(hid_ok, 1)
            act.wait_ge(last_in, 16)
            freed(act, "dttok1")
            freed(act, "dctok1")

            def tile(t, s, g, last):
                act.wait_ge(hid_ok, 2 * t + 2)
                act.wait_ge(ys_ok, 2 * NT * g)
                apart(act)
                act.activation(YG[:, bass.ds(s, 1), :].rearrange("p a t -> p (a t)"), hidT[:], ACT.Copy,
                               scale=Dc[:, bass.ds(t, 1)]).then_inc(dh_ok, 1)

                def tap_next(b):
                    if not last:
                        act.wait_ge(dh_ok, t + 1)
                        act.wait_ge(t_full["R"][b], 4 * t + 1)
                        act.wait_ge(t_full["P"][b], 3 * t + 1)
                        tap(hidT[:, b * S:(b + 1) * S], psP[:, b], t + 1, True).then_inc(tap_ok, 1)

                def decay_exp(h):
                    for b in range(NB):
                        act.wait_ge(t_free["R"][b], 4 * t + h + 2)
                        act.activation(flat(LM[:, h, b]), flat(LM[:, h, b]), ACT.Exp).then_inc(exp_ok, 1)

                tap_next(0)
                decay_exp(0)
                act.wait_ge(t_full["X"][0], 3 * t + 1)
                apart(act)
                act.activation(WOh[:, bass.ds(s, 1), :].rearrange("p a t -> p (a t)"), psX[:, 0], ACT.Copy,
                               scale=gw[:, bass.ds(t, 1)]).then_inc(wo_hi, 1)
                tap_next(1)
                decay_exp(1)
                for b in range(NB):
                    act.wait_ge(t_full["R"][b], 4 * t + 4)
                    act.wait_ge(pool_y, 4 * t)
                    act.activation(flat(E[:, b]), psR[:, b], ACT.Exp).then_inc(t_free["R"][b], 1)

                gk = 0 if last else 1

                def gate(b):
                    act.wait_ge(t_full["P"][b], 3 * t + gk + 1)
                    act.activation(sg[:, b * S:(b + 1) * S], psP[:, b], ACT.Silu).then_inc(t_free["P"][b], 1)

                gate(0)
                if not last:
                    for b in range(NB):
                        act.wait_ge(t_free["P"][b], 3 * t + 1)
                        act.activation(hidT[:, b * S:(b + 1) * S], hidT[:, b * S:(b + 1) * S], ACT.Silu
                                       ).then_inc(hid_ok, 1)
                gate(1)
                if not last:
                    act.wait_ge(t_full["P"][0], 3 * t + 3)
                    act.activation(flat(WTh[:, 0]), psP[:, 0], ACT.Copy).then_inc(wth_hi, 1)
                    act.wait_ge(t_full["P"][1], 3 * t + 3)
                    act.activation(flat(WTg[:, 0]), psP[:, 1], ACT.Copy).then_inc(wtg_hi, 1)

            def tail(g, last):
                def w_hi(q):
                    act.wait_ge(l_full["R"][0], 2 * g + q + 1)
                    act.activation(flat(WTb[:, 0]), psR[:, 0], ACT.Copy).then_inc(wtb_hi, 1)

                def taps(q):
                    for b in range(NB):
                        act.wait_ge(l_full["P"][b], 2 * g + q + 1)
                        bc_taps(q, b, psP[:, b], TILES + G * q + g + 1, True)

                def silus(q):
                    for b in range(NB):
                        act.wait_ge(l_free["P"][b], 2 * g + q + 1)
                        bc_silu(q, b)

                if not last:
                    w_hi(0)
                    taps(0)
                    w_hi(1)
                    act.wait_ge(t_full["X"][1], 2 * TPG * (g + 1))
                    taps(1)
                act.wait_ge(pool_y, 4 * TPG * (g + 1))
                for m in range(NT):
                    for hf in range(2):
                        if m and hf == 0:
                            act.wait_ge(ys_used, NT * g + m)
                        if m and hf == 1:
                            k = (m - 1) // 2 + (1 if m - 1 >= 4 and not last else 0)
                            act.wait_ge(l_full["D"][(m - 1) % 2], 5 * g + k + 1)
                        act.activation(YS[:, hf, 0], YG[:, 4 * hf:4 * hf + 4, m * P:(m + 1) * P], ACT.Copy
                                       ).then_inc(ys_hi, 1)
                    if m == 0 and not last:
                        silus(0)
                        silus(1)

            every(act, tile, tail)
            ffn(1)

        @block.vector
        def _(dve):
            steps = [0]

            def link(ins):
                steps[0] += 1
                ins.then_inc(dve_link, 1)
                dve.wait_ge(dve_link, steps[0])

            def layer_norm(n):
                for k in range(NT):
                    last = dve.bn_stats(bst[:, k], XR[:, k])
                link(last)
                for k in range(NT):
                    last = dve.bn_aggr(bag[:, k], bst[:, k])
                link(last)
                dve.tensor_scalar(rv[:], bag[:, :, 1], LN_EPS, None, ALU.add).then_inc(ln_var, 1)
                dve.wait_ge(ln_fac, (1, 2, 4)[n])
                for k in range(NT):
                    dve.tensor_scalar(XH[:, k], XR[:, k], bag[:, k, 0:1], rs[:, k:k + 1], ALU.subtract, ALU.mult
                                      ).then_inc(xh_ok, 1)

            def ffn(f):
                for k in range(NT):
                    full(dve, f"low{f}{k}")
                    dve.tensor_copy(low[:, k], bank(f"low{f}{k}")[:, 0:HR + FH]).then_inc(free_sem(f"low{f}{k}"), 1)
                for k in (NT - 2, NT - 1):
                    freed(dve, f"low{f}{k}")
                wide = [P, NT, FH]
                dve.wait_ge(ffw_in, 16 * (3 + KD) * (f + 1))
                link(dve.tensor_tensor(lg[:], low[:, :, HR:], brb[:].unsqueeze(1).to_broadcast(wide), ALU.add))
                link(dve.tensor_reduce(mx[:], lg[:], AX.X, ALU.max))
                dve.tensor_tensor(lg[:], lg[:], mx[:].unsqueeze(2).to_broadcast(wide), ALU.subtract
                                  ).then_inc(smx_in, 1)
                dve.wait_ge(smx_exp, f + 1)
                link(dve.tensor_reduce(sm[:], pe_[:], AX.X, ALU.add))
                link(dve.reciprocal(mx[:], sm[:]))
                link(dve.scalar_tensor_tensor(out=pw[:], in0=pe_[:], scalar=FFN_SCALE,
                                              in1=mx[:].unsqueeze(2).to_broadcast(wide), op0=ALU.mult, op1=ALU.mult))
                for k in range(NT):
                    last = dve.tensor_tensor(LS[:, k].rearrange("p (h r) -> p h r", h=FH),
                                             low[:, k, 0:HR].rearrange("p (h r) -> p h r", h=FH),
                                             pw[:, k].unsqueeze(2).to_broadcast([P, FH, FR]), ALU.mult)
                last.then_inc(ls_ok, 1)
                for k in range(NT):
                    full(dve, f"ffn{f}{k}")
                    dve.tensor_tensor(XR[:, k], XR[:, k], bank(f"ffn{f}{k}"), ALU.add
                                      ).then_inc(free_sem(f"ffn{f}{k}"), 1)
                for k in (NT - 2, NT - 1):
                    freed(dve, f"ffn{f}{k}")

            def conv(step, n, dst, src, ct, done):
                for d in range(1, TAPS):
                    if d > 1:
                        dve.wait_ge(step, n + d - 1)
                    dve.scalar_tensor_tensor(out=dst[:, d:S], in0=src[:, 0:S - d],
                                             scalar=cw[:, bass.ds(ct, 1), TAPS - 1 - d], in1=dst[:, d:S],
                                             op0=ALU.mult, op1=ALU.add
                                             ).then_inc(done if d == TAPS - 1 else step, 1)

            def split_lo(dst, src, hi, done):
                dve.tensor_tensor(dst.rearrange("p a c -> p (a c)"), src,
                                  hi.rearrange("p a c -> p (a c)").bitcast(F32), ALU.subtract).then_inc(done, 1)

            dve.memset(hcA[:], 0.0)
            dve.memset(hcB[:], 0.0).then_inc(zero_ok, 1)
            dve.wait_ge(x_in, 16 * NT // 2)
            layer_norm(0)
            full(dve, "tables")
            n = TAPS * CT_ALL
            dve.tensor_copy(cw[:].rearrange("p t k -> p k t"), bank("tables")[:, 0:n].rearrange("p (k t) -> p k t", k=TAPS))
            for dst in (cb, gw, nw):
                last = dve.tensor_copy(dst[:], bank("tables")[:, n:n + dst.shape[1]])
                n += dst.shape[1]
            for h in range(2):
                last = dve.tensor_copy(Dc[h * HP:(h + 1) * HP, :], Drow[h * HP:(h + 1) * HP, h::2])
            last.then_inc(free_sem("tables"), 1)
            freed(dve, "tables")
            ffn(0)
            layer_norm(1)
            dve.wait_ge(xh_ok, 2 * NT)
            for k in range(NT):
                last = dve.tensor_tensor(XR[:, k], XR[:, k], XH[:, k], ALU.add)
            dve.wait_ge(xn_sq, NT)
            dve.tensor_scalar(rv[:], s2[:], 1.0 / DM, RMS_EPS, ALU.mult, ALU.add).then_inc(ln_var, 1)
            dve.wait_ge(ln_fac, 3)
            for k in range(NT):
                dve.tensor_scalar(XH[:, k], XH[:, k], rs[:, k:k + 1], None, ALU.mult).then_inc(h_ok, 1)
            dve.wait_ge(tab_in, 16 * 7)
            for k in range(NT + 1):
                if k < NT:
                    full(dve, f"hT{k}")
                    dve.tensor_tensor(TT[:, k % 2], bank(f"hT{k}").rearrange("p (a c) -> p a c", a=KD),
                                      nw[:].unsqueeze(2).to_broadcast([P, KD, P]), ALU.mult).then_inc(h_tmp, 1)
                if k:
                    j = k - 1
                    dve.wait_ge(h_hi, j + 1)
                    dve.tensor_tensor(HTl[:, :, j * P:(j + 1) * P], TT[:, j % 2],
                                      HTh[:, :, j * P:(j + 1) * P].bitcast(F32), ALU.subtract
                                      ).then_inc(free_sem(f"hT{j}"), 1)
            full(dve, "WdT")
            dve.wait_ge(wd_hi, 1)
            split_lo(WTd[:, 1], bank("WdT"), WTd[:, 0], free_sem("WdT"))
            for b in range(NB):
                full(dve, f"dt{b}")
                dve.tensor_scalar(dtS[0][:, b * S:(b + 1) * S], bank(f"dt{b}"), dtb[:], None, ALU.add
                                  ).then_inc(free_sem(f"dt{b}"), 1)

            def bc_first(q):
                full(dve, f"bcW{q}")
                dve.wait_ge(wtb_hi, q + 1)
                split_lo(WTb[:, 1], bank(f"bcW{q}"), WTb[:, 0], free_sem(f"bcW{q}"))

            def bc_conv_first(q):
                for b in range(NB):
                    dve.wait_ge(btap_ok, 2 * q + b + 1)
                    conv(bconv_st, 2 * (2 * q + b), (BT, CT)[q][:, b * S:(b + 1) * S], bank(f"bc{q}{b}"),
                         TILES + G * q, free_sem(f"bc{q}{b}"))

            bc_first(0)
            dve.wait_ge(dt_act, 3)
            dve.wait_ge(a_exp, 1)
            link(dve.tensor_scalar(negA[:], negA[:], -1.0, None, ALU.mult))
            for b in range(NB):
                freed(dve, f"dt{b}")
            dve.scalar_tensor_tensor(out=dtS[2][:], in0=dtS[0][:], scalar=0.0, in1=dtS[4][:], op0=ALU.max,
                                     op1=ALU.add).then_inc(tok_ok, 1)
            dve.wait_ge(tok_ok, 1)
            link(dve.tensor_scalar(dtS[1][:], dtS[2][:], negA[:], EXP_FLOOR, ALU.mult, ALU.max))
            link(dve.memset(dtS[3][:], 1.0))
            link(dve.memset(dtS[3][:, 0::P], 0.0))
            dve.tensor_tensor_scan(dtS[4][:], dtS[3][:], dtS[1][:], 0.0, ALU.mult, ALU.add).then_inc(cs_ok, 1)
            dve.wait_ge(cs_ok, 1)
            rest = dtS[4]
            for q in range(3):
                dve.tensor_copy(parts[q][:], rest[:]).then_inc(part_ok, 1)
                dve.wait_ge(part_ok, q + 1)
                if q < 2:
                    nxt = (dtS[3], dtS[1])[q]
                    link(dve.tensor_tensor(nxt[:], rest[:], parts[q][:], ALU.subtract))
                    rest = nxt
            for q in range(3):
                dve.tensor_scalar(parts[3 + q][:], parts[q][:], -1.0, None, ALU.mult).then_inc(part_ok, 1)
            bc_conv_first(0)
            bc_first(1)
            bc_conv_first(1)
            full(dve, "hW0")
            dve.wait_ge(wth_hi, 1)
            split_lo(WTh[:, 1], bank("hW0"), WTh[:, 0], free_sem("hW0"))
            for b in range(NB):
                dve.wait_ge(tap_ok, b + 1)
                conv(conv_st, 2 * b, hidT[:, b * S:(b + 1) * S], bank(f"h{b}"), 0, free_sem(f"h{b}"))
            full(dve, "hW1")
            dve.wait_ge(wth_hi, 2)
            split_lo(WTh[:, 1], bank("hW1"), WTh[:, 0], free_sem("hW1"))
            full(dve, "gW0")
            dve.wait_ge(wtg_hi, 1)
            split_lo(WTg[:, 1], bank("gW0"), WTg[:, 0], free_sem("gW0"))
            for name, dst in (("dttok", dtk), ("dctok", dck)):
                for i in range(2):
                    full(dve, f"{name}{i}")
                    dve.tensor_copy(dst[:, 4 * i:4 * i + 4], bank(f"{name}{i}").rearrange("p (c h) -> p c h", c=4)
                                    ).then_inc(free_sem(f"{name}{i}"), 1)

            def mask_cb(psum, i, done):
                dve.tensor_tensor(GM[:, 4 * i:4 * i + 4], psum.rearrange("p (c i) -> p c i", c=NCH),
                                  causal[:].unsqueeze(1).to_broadcast([P, NCH, P]), ALU.mult).then_inc(done, 1)

            def copy_b(psum, i, done):
                dve.tensor_copy(BTok[:, 4 * i:4 * i + 4], psum.rearrange("p (c i) -> p c i", c=NCH)
                                ).then_inc(done, 1)

            dve.wait_ge(const_ok, 1)
            for i in range(2):
                full(dve, f"CB{i}")
                mask_cb(bank(f"CB{i}"), i, free_sem(f"CB{i}"))
                full(dve, f"Bt{i}")
                copy_b(bank(f"Bt{i}"), i, free_sem(f"Bt{i}"))
            dve.wait_ge(last_in, 16)
            dve.wait_ge(zero_ok, 1)

            def tile(t, s, g, last):
                dve.wait_ge(xd_ok, 4 * t)
                for b in range(NB):
                    dve.wait_ge(t_full["D"][b], t)
                    dve.wait_ge(t_full["R"][b], 4 * t + 1)
                    src = psR[:, b].rearrange("p (c i) -> p c i", c=NCH)
                    ch = slice(b * NCH, (b + 1) * NCH)
                    for h, dst in enumerate((hcA, hcB)):
                        cols = slice(h * HP, (h + 1) * HP)
                        last_i = dve.tensor_tensor(dst[:, ch, cols], src[:, :, cols],
                                                   dtk[:, ch, bass.ds(2 * t + h, 1)].to_broadcast([P, NCH, HP]),
                                                   ALU.mult)
                    last_i.then_inc(t_free["R"][b], 1)

                def clamp(h):
                    for b in range(NB):
                        dve.wait_ge(t_full["R"][b], 4 * t + h + 2)
                        dve.tensor_scalar(LM[:, h, b].rearrange("p c i -> p (c i)"), psR[:, b], 0.0, None, ALU.min
                                          ).then_inc(t_free["R"][b], 1)

                def conv_next(b):
                    if not last:
                        dve.wait_ge(tap_ok, 2 * t + b + 3)
                        conv(conv_st, 4 * t + 4 + 2 * b, hidT[:, b * S:(b + 1) * S], psP[:, b], t + 1,
                             t_free["P"][b])

                clamp(0)
                conv_next(0)
                clamp(1)
                dve.wait_ge(wo_hi, t + 1)
                dve.scalar_tensor_tensor(out=WOl[:, bass.ds(s, 1), :].rearrange("p a t -> p (a t)"), in0=psX[:, 0],
                                         scalar=gw[:, bass.ds(t, 1)],
                                         in1=WOh[:, bass.ds(s, 1), :].rearrange("p a t -> p (a t)").bitcast(F32),
                                         op0=ALU.mult, op1=ALU.subtract).then_inc(t_free["X"][0], 1)
                for b in range(NB):
                    for h in range(2):
                        dve.wait_ge(exp_ok, 4 * t + (3 if h == 0 and b else 1 + 2 * h + b))
                        dve.tensor_tensor(LM[:, h, b], LM[:, h, b], GM[:, b * NCH:(b + 1) * NCH], ALU.mult
                                          ).then_inc(m_ok, 1)
                conv_next(1)
                dve.wait_ge(t_full["X"][0], 3 * t + 2)
                dve.wait_ge(t_full["X"][1], 2 * t + 1)
                halves = lambda a: a.rearrange("p b (h q) -> p b h q", h=2)
                dve.tensor_copy(ST[:, :, 0], psX[:, :, 0:P]).then_inc(st_step, 1)
                for c in range(1, NCH - 1):
                    dve.wait_ge(st_step, 4 * t + 2 * c - 1)
                    dve.tensor_tensor(halves(ST[:, :, c]), halves(ST[:, :, c - 1]),
                                      EL[:, :, c - 1, bass.ds(2 * t, 2)].unsqueeze(3).to_broadcast([P, NB, 2, HP]),
                                      ALU.mult).then_inc(st_step, 1)
                    dve.wait_ge(st_step, 4 * t + 2 * c)
                    if c < NCH - 2:
                        dve.tensor_tensor(ST[:, :, c], ST[:, :, c], psX[:, :, c * P:(c + 1) * P], ALU.add
                                          ).then_inc(st_step, 1)
                    else:
                        for b in range(NB):
                            dve.tensor_tensor(ST[:, b, c], ST[:, b, c], psX[:, b, c * P:(c + 1) * P], ALU.add
                                              ).then_inc(t_free["X"][b], 1)
                dve.wait_ge(dh_ok, t + 1)
                for b in range(NB):
                    dve.wait_ge(t_full["D"][b], t + 1)
                    y = YG[:, bass.ds(s, 1), b * S:(b + 1) * S].rearrange("p a t -> p (a t)")
                    dve.tensor_tensor(y, y, psD[:, b], ALU.add).then_inc(t_free["D"][b], 1)
                    if not last:
                        dve.wait_ge(wtg_hi if b else wth_hi, t + 3 - b)
                        w = WTg if b else WTh
                        split_lo(w[:, 1], psP[:, b], w[:, 0], t_free["P"][b])
                for b in range(NB):
                    dve.wait_ge(t_full["X"][b], PT["X"][b] * t + 3 - b)
                    dve.wait_ge(t_free["R"][b], 4 * t + 4)
                    dve.tensor_tensor(E[:, b, 1:NCH], E[:, b, 1:NCH],
                                      psX[:, b, 0:(NCH - 1) * P].rearrange("p (c i) -> p c i", c=NCH - 1), ALU.mult
                                      ).then_inc(t_free["X"][b], 1)

            def tail(g, last):
                def w_lo(q):
                    dve.wait_ge(wtb_hi, 2 * g + q + 3)
                    split_lo(WTb[:, 1], psR[:, 0], WTb[:, 0], l_free["R"][0])

                def convs(q):
                    for b in range(NB):
                        dve.wait_ge(btap_ok, 4 * (g + 1) + 2 * q + b + 1)
                        conv(bconv_st, 8 * (g + 1) + 2 * (2 * q + b), (BT, CT)[q][:, b * S:(b + 1) * S], psP[:, b],
                             TILES + G * q + g + 1, l_free["P"][b])

                if not last:
                    w_lo(0)
                    convs(0)
                    w_lo(1)
                    convs(1)
                dve.wait_ge(l_full["R"][1], g + 1)
                dve.tensor_scalar(vs[:], psR[:, 1, 0:NT], float(G) / DI, RMS_EPS, ALU.mult, ALU.add
                                  ).then_inc(l_free["R"][1], 1)

                def add(m):
                    k = m // 2 + (1 if m >= 4 and not last else 0)
                    dve.wait_ge(l_full["D"][m % 2], 5 * g + k + 1)
                    dve.scalar_tensor_tensor(out=XR[:, m], in0=psD[:, m % 2], scalar=rg[:, m:m + 1], in1=XR[:, m],
                                             op0=ALU.mult, op1=ALU.add).then_inc(l_free["D"][m % 2], 1)

                for m in range(NT):
                    for hf in range(2):
                        dve.wait_ge(ys_hi, 2 * NT * g + 2 * m + hf + 1)
                        dve.tensor_tensor(YS[:, hf, 1], YG[:, 4 * hf:4 * hf + 4, m * P:(m + 1) * P],
                                          YS[:, hf, 0].bitcast(F32), ALU.subtract).then_inc(ys_ok, 1)
                    if m == 1:
                        dve.wait_ge(r_ok, g + 1)
                    if m:
                        add(m - 1)
                    if m == 4 and not last:
                        for i in range(2):
                            dve.wait_ge(l_full["D"][i], 5 * g + 3)
                            mask_cb(psD[:, i], i, l_free["D"][i])
                            dve.wait_ge(l_full["X"][i], g + 1)
                            copy_b(psX[:, i], i, l_free["X"][i])
                add(NT - 1)

            every(dve, tile, tail)
            for i in range(2):
                dve.wait_ge(l_free["D"][i], 5 * (G - 1) + 4)
            layer_norm(2)
            ffn(1)

        @block.gpsimd
        def _(pool):
            steps = [0]

            def link(ins):
                steps[0] += 1
                ins.then_inc(pool_link, 1)
                pool.wait_ge(pool_link, steps[0])

            link(pool.memset(ident[:], 0.0))
            pool.affine_select(out=ident[:], in_=ident[:], compare_op=ALU.not_equal, fill=1.0, base=0,
                               pattern=[[-1, P]], channel_multiplier=1).then_inc(ident_ok, 1)
            link(pool.memset(half[:], -0.5))

            def inv_sqrt(dst, src, n, var, made):
                pool.wait_ge(var, n)
                pool.tensor_tensor(dst[:], src[:], half[:], ALU.pow).then_inc(made, 1)

            inv_sqrt(rs, rv, 1, ln_var, ln_fac)
            pool.memset(ones[:], 1.0)
            link(pool.memset(causal[:], 1.0))
            link(pool.affine_select(out=causal[:], in_=causal[:], compare_op=ALU.is_ge, fill=0.0, base=0,
                                    pattern=[[1, P]], channel_multiplier=-1))
            link(pool.memset(OHf[:], 0.0))
            for m in (0, 1, 2, 3, 4, 5, 8, 9, 10, 11, 12, 13):
                link(pool.affine_select(out=OHf[:], in_=OHf[:], compare_op=ALU.not_equal, fill=1.0, base=-NT * m,
                                        pattern=[[-1, NT]], channel_multiplier=1))
            link(pool.tensor_copy(OH[:], OHf[:]))
            link(pool.tensor_copy(RP[:], OH[:].unsqueeze(2).to_broadcast([112, NT, P])))
            link(pool.memset(LH[:], 0.0))
            link(pool.memset(LH[0:48], 1.0))
            link(pool.memset(selE[:], 1.0))
            for h, (mul, base) in enumerate(((-1, 23), (1, -24))):
                link(pool.affine_select(out=LH[0:48, h], in_=LH[0:48, h], compare_op=ALU.is_ge, fill=0.0,
                                        base=base, pattern=[[0, P]], channel_multiplier=mul))
                cols = slice(h * HP, (h + 1) * HP)
                link(pool.affine_select(out=selE[:, cols], in_=selE[:, cols], compare_op=ALU.is_ge, fill=0.0,
                                        base=base, pattern=[[0, HP]], channel_multiplier=mul))
            pool.memset(SQ[:], 0.0).then_inc(sq_zero, 1)
            pool.wait_ge(sq_zero, 1)
            pool.memset(vs[:], 1.0).then_inc(const_ok, 1)
            inv_sqrt(rs, rv, 2, ln_var, ln_fac)
            inv_sqrt(rs, rv, 3, ln_var, ln_fac)

            def by_chunk(t):
                pool.wait_ge(cs_in, 16 * (t + 1))
                pool.tensor_tensor(RP[0:48], CS[:].unsqueeze(1).to_broadcast([48, NT, P]),
                                   OH[0:48].unsqueeze(2).to_broadcast([48, NT, P]), ALU.mult).then_inc(rp_ok, 1)

            by_chunk(0)

            def tile(t, s, g, last):
                for b in range(NB):
                    pool.wait_ge(t_full["X"][b], PT["X"][b] * t)
                    pool.wait_ge(t_free["R"][b], 4 * t + 1)
                    apart(pool)
                    ch = slice(b * NCH, b * NCH + NCH - 1)
                    for h, src in enumerate((hcA, hcB)):
                        cols = slice(h * HP, (h + 1) * HP)
                        pool.tensor_tensor(XD[:, b, :, cols], src[:, ch, cols],
                                           dck[:, ch, bass.ds(2 * t + h, 1)].to_broadcast([P, NCH - 1, HP]),
                                           ALU.mult).then_inc(xd_ok, 1)
                if not last:
                    for b in range(NB):
                        pool.wait_ge(t_full["R"][b], 4 * t + 4)
                    by_chunk(t + 1)
                y4 = YG[:, bass.ds(s, 1), :].rearrange("p a (b c i) -> p (a b) c i", b=NB, c=NCH)
                y = YG[:, bass.ds(s, 1), :].rearrange("p a t -> p (a t)")
                flatE = E[:].rearrange("p b c i -> p (b c i)")
                for b in range(NB):
                    pool.wait_ge(t_free["X"][b], PT["X"][b] * t + 3 - b)
                    pool.wait_ge(t_free["D"][b], t + 1)
                apart(pool)
                pool.tensor_tensor(y4[:, :, 1:NCH], y4[:, :, 1:NCH], E[:, :, 1:NCH], ALU.add).then_inc(pool_y, 1)
                for b in range(NB):
                    pool.wait_ge(t_free["P"][b], 3 * t + (1 if last else 2))
                pool.wait_ge(pool_y, 4 * t + 1)
                apart(pool)
                pool.tensor_tensor(y, y, sg[:], ALU.mult).then_inc(pool_y, 1)
                pool.wait_ge(pool_y, 4 * t + 2)
                apart(pool)
                pool.tensor_tensor(flatE, y, y, ALU.mult).then_inc(pool_y, 1)
                pool.wait_ge(pool_y, 4 * t + 3)
                pool.wait_ge(sq_zero, g + 1)
                pool.tensor_tensor(SQ[:], SQ[:], flatE, ALU.add).then_inc(pool_y, 1)

            def tail(g, last):
                pool.wait_ge(l_full["R"][1], g + 1)
                apart(pool)
                pool.memset(SQ[:], 0.0).then_inc(sq_zero, 1)
                inv_sqrt(rg, vs, g + 1, l_free["R"][1], r_ok)

            every(pool, tile, tail)
            inv_sqrt(rs, rv, 4, ln_var, ln_fac)


_ORDER = ["x", "norm_w", "in_proj_w", "conv_w", "conv_b", "dt_bias", "A_log", "Dp", "gnorm_w", "out_proj_w",
          "A", "B", "Wr", "br"]


def kernel(L0_attn_x, L0_attn_norm_w, L0_attn_in_proj_w, L0_attn_conv_w, L0_attn_conv_b, L0_attn_dt_bias,
           L0_attn_A_log, L0_attn_Dp, L0_attn_gnorm_w, L0_attn_out_proj_w, L0_ffn_A, L0_ffn_B, L0_ffn_Wr,
           L0_ffn_br):
    import numpy as np
    import concourse.bacc as bacc
    from concourse.bass_utils import run_bass_kernel_spmd

    given = [L0_attn_x, L0_attn_norm_w, L0_attn_in_proj_w, L0_attn_conv_w, L0_attn_conv_b, L0_attn_dt_bias,
             L0_attn_A_log, L0_attn_Dp, L0_attn_gnorm_w, L0_attn_out_proj_w, L0_ffn_A, L0_ffn_B, L0_ffn_Wr,
             L0_ffn_br]
    nc = bacc.Bacc("TRN2", target_bir_lowering=False, num_devices=1)
    arrays, args = {}, []
    for name, a in zip(_ORDER, given):
        a = np.ascontiguousarray(a)
        arrays[f"in_{name}"] = a
        args.append(nc.dram_tensor(f"in_{name}", a.shape, mybir.dt.from_np(a.dtype), kind="ExternalInput").ap())
    y = nc.dram_tensor("out_y", given[0].shape, F32, kind="ExternalOutput").ap()
    macaron(nc, *args, y)
    r = run_bass_kernel_spmd(nc, [arrays], core_ids=[0])
    return r.results[0]["out_y"]
```

```python
from contextlib import ExitStack

import concourse.bass as bass
from concourse import mybir

F32 = mybir.dt.float32
F32R = mybir.dt.float32r
ALU = mybir.AluOpType
ACT = mybir.ActivationFunctionType
AX = mybir.AxisListType

LN_EPS = 1e-5
RMS_EPS = 1e-5
EXP_FLOOR = -128.0


def macaron(nc, x, norm_w, in_proj_w, conv_w, conv_b, dt_bias, A_log, Dp, gnorm_w, out_proj_w,
            ffn_A, ffn_B, ffn_Wr, ffn_br, out):
    P = 128
    NB, S, DM = x.shape
    T = NB * S
    NCH = S // P
    NT = T // P
    KD = DM // P
    H = Dp.shape[0]
    DI = out_proj_w.shape[1]
    HP = DI // H
    CD, TAPS = conv_w.shape
    N = P
    G = (CD - DI) // (2 * N)
    TILES = DI // P
    TPG = TILES // G
    CT_ALL = CD // P
    FH, FR, _ = ffn_A.shape
    HR = FH * FR
    assert (P, H, HP, NT, S, DM) == (HR, P, P // 2, 8, 512, 512)
    FFN_SCALE = float(FH)

    x_d = x.rearrange("b (c p) d -> p (b c) d", p=P)
    out_d = out.rearrange("b (c p) d -> p (b c) d", p=P)
    A_d = ffn_A.rearrange("h r d -> (h r) d")
    B_d = ffn_B.rearrange("h (a p) r -> p a h r", p=P)
    outw_d = out_proj_w.rearrange("(a p) d -> p a d", p=P)
    HID0, B0, C0, DT0 = DI, 2 * DI, 2 * DI + G * N, DI + CD
    cs_d = nc.dram_tensor("running_sums", [H, T], F32, kind="Internal").ap()
    last_d = nc.dram_tensor("chunk_decay", [2 * NB, H], F32, kind="Internal").ap()

    with ExitStack() as ctx:
        sem = lambda name: ctx.enter_context(nc.semaphore(name))
        ps = lambda name, dt=F32: ctx.enter_context(nc.psum_tensor(name, [P, 2, 512], dt))

        size = nc.sbuf_usable_end - nc.sbuf_base - 160
        ctx.enter_context(nc.sbuf_tensor("arena", [P, size // 4], F32))
        end = nc.sbuf_base
        cursor = [(end - size // 4 * 4 + 31) // 32 * 32]
        widths = {F32: 4, F32R: 4}

        def put(name, shape, dt, at=None):
            n = widths[dt]
            for k in shape[1:]:
                n *= k
            if at is None:
                at = cursor[0]
                cursor[0] += (n + 31) // 32 * 32
                assert cursor[0] <= end, (name, cursor[0], end)
            return nc.alloc_sbuf_tensor_at(name, shape, dt, offset=at), at

        HTh, _ = put("hT_hi", [P, KD, T], F32R)
        HTl, _ = put("hT_lo", [P, KD, T], F32R)
        XR, _ = put("residual", [P, NT, DM], F32)
        YG, yg_at = put("yg", [P, TPG, T], F32)
        YS, ys_at = put("yg_split", [P, 2, 2, 4, P], F32R)
        WOh, wo_at = put("wo_hi", [P, TPG, DM], F32R)
        WOl, _ = put("wo_lo", [P, TPG, DM], F32R)
        raw_h, _ = put("raw_hid", [P, KD, P], F32)
        raw_g, _ = put("raw_gate", [P, KD, P], F32)
        raw_o, _ = put("raw_out", [P, KD, P], F32)
        WTh = put("wt_hid", [P, 2, KD, P], F32R)[0]
        WTg = put("wt_gate", [P, 2, KD, P], F32R)[0]
        hidT, _ = put("hidT", [P, T], F32)
        sg, _ = put("silu_gate", [P, T], F32)
        hcA, _ = put("hid_dt_even", [P, NT, P], F32)
        hcB, _ = put("hid_dt_odd", [P, NT, P], F32)
        XD, xd_at = put("hid_dt_decay", [P, NB, NCH - 1, P], F32)
        ST, _ = put("states", [P, NB, NCH - 1, P], F32, at=xd_at)
        CSB, _ = put("cs_rows", [P, NT, P], F32)
        LM, lm_at = put("scores", [P, 2, NB, NCH, P], F32)
        WTbc = put("wt_bc", [P, 2, 2, KD, P], F32R, at=lm_at)[0]
        E, _ = put("decay_in", [P, NB, NCH, P], F32)
        CT, _ = put("C_T", [P, T], F32)
        BT, bt_at = put("B_T", [P, T], F32)
        raw_c = put("raw_c", [P, KD, P], F32, at=bt_at)[0]
        raw_b = put("raw_b", [P, KD, P], F32, at=bt_at + DM * 4)[0]
        GM, _ = put("CB_masked", [P, NT, P], F32)
        BTok, _ = put("B_tok", [P, NT, P], F32)
        dtk, _ = put("dt_tok", [P, NT, H], F32)
        dck, _ = put("decay_tok", [P, NT, H], F32)
        ctk, _ = put("cs_tok", [P, NT, H], F32)
        EL, _ = put("chunk_decays", [P, NB, 2, H], F32)
        SQ, _ = put("sum_sq", [P, T], F32)
        ident, _ = put("ident", [P, P], F32)
        causal, _ = put("causal", [P, P], F32)
        cw, _ = put("conv_w", [P, CT_ALL, TAPS], F32)
        cb, _ = put("conv_b", [P, CT_ALL], F32)
        Dc, _ = put("D_col", [P, TILES], F32)
        gw, _ = put("gnorm_col", [P, TILES], F32)
        nw, _ = put("norm_col", [P, KD], F32)
        dtb, _ = put("dt_bias", [P, 1], F32)
        negA, _ = put("neg_A", [P, 1], F32)
        ones, _ = put("ones", [P, 1], F32)
        half, _ = put("minus_half", [P, NT], F32)
        vs, _ = put("mean_sq", [P, NT], F32)
        rg, _ = put("rms_factor", [P, NT], F32)

        at = yg_at
        XH, _ = put("normed", [P, NT, DM], F32, at=at); at += NT * DM * 4
        TT, _ = put("normed_T", [P, 2, KD, P], F32, at=at); at += 2 * DM * 4
        A_raw, _ = put("A_raw", [P, DM], F32, at=at); at += DM * 4
        Wr_raw, _ = put("Wr_raw", [FH, DM], F32, at=at); at += DM * 4
        B_raw, _ = put("B_raw", [P, KD, FH, FR], F32, at=at); at += DM * 4
        AT, _ = put("A_T", [P, KD, HR + FH], F32, at=at); at += KD * (HR + FH) * 4
        assert at <= yg_at + TPG * T * 4
        at = lm_at
        BTm, _ = put("B_mix_T", [P, DM], F32, at=at); at += DM * 4
        low, _ = put("low", [P, NT, HR + FH], F32, at=at); at += NT * (HR + FH) * 4
        LS, _ = put("low_scored", [P, NT, HR], F32, at=at); at += NT * HR * 4
        LST, _ = put("low_scored_T", [P, NT, P], F32, at=at); at += NT * P * 4
        brb, _ = put("br_rows", [P, FH], F32, at=at); at += 32
        lg, _ = put("logits", [P, NT, FH], F32, at=at); at += NT * FH * 4
        pe_, _ = put("score_exp", [P, NT, FH], F32, at=at); at += NT * FH * 4
        pw, _ = put("score", [P, NT, FH], F32, at=at); at += NT * FH * 4
        mx, _ = put("row_max", [P, NT], F32, at=at); at += 32
        sm, _ = put("row_sum", [P, NT], F32, at=at); at += 32
        bst, _ = put("bn_st", [P, NT, 6], F32, at=at); at += NT * 24
        bag, _ = put("bn_ag", [P, NT, 2], F32, at=at); at += NT * 8
        rs, _ = put("ln_factor", [P, NT], F32, at=at); at += 32
        rv, _ = put("ln_var", [P, NT], F32, at=at); at += 32
        s2, _ = put("xn_sq", [P, NT], F32, at=at); at += 32
        at = yg_at
        dtS = []
        for k in range(7):
            dtS.append(put(f"dt_step{k}", [P, T], F32, at=at)[0]); at += T * 4
        at = wo_at
        cwr, _ = put("conv_w_rows", [CT_ALL, P * TAPS], F32, at=at); at += P * TAPS * 4
        cbr, _ = put("conv_b_rows", [CT_ALL, P], F32, at=at); at += P * 4
        gwr, _ = put("gnorm_rows", [TILES, P], F32, at=at); at += P * 4
        nwr, _ = put("norm_rows", [KD, P], F32, at=at); at += P * 4
        Drow, _ = put("D_rows", [P, H], F32, at=at); at += H * 4
        assert at <= wo_at + TPG * DM * 4
        at = wo_at + TPG * DM * 4
        WTd = put("wt_dt", [P, 2, KD, P], F32R, at=at)[0]; at += 2 * DM * 4
        WTf = []
        for k in range(2):
            WTf.append(put(f"wt_bc_first{k}", [P, 2, KD, P], F32R, at=at)[0]); at += 2 * DM * 4
        raw_f = []
        for k in range(2):
            raw_f.append(put(f"raw_bc_first{k}", [P, KD, P], F32, at=at)[0]); at += DM * 4
        assert at <= wo_at + 2 * TPG * DM * 4

        psR, psP, psX, psD = ps("psR"), ps("psP"), ps("psX"), ps("psD")
        BANKS = {"R": psR, "P": psP, "X": psX, "D": psD}

        def family(tag):
            return ({b: [sem(f"{tag}_full_{b}{i}") for i in range(2)] for b in BANKS},
                    {b: [sem(f"{tag}_free_{b}{i}") for i in range(2)] for b in BANKS})

        o_full, o_free = family("once")
        t_full, t_free = o_full, o_free
        l_full, l_free = family("tail")
        PT = {"R": (1, 1), "P": (3, 3), "X": (3, 2), "D": (1, 1)}
        PL = {"R": (1, 2), "P": (2, 2), "X": (1, 1), "D": (5, 5)}
        Y0, XD0, YS0 = 4, 1, 1

        x_in = sem("x_in"); tab_in = sem("tables_in"); ffw_in = sem("ffn_weights_in")
        rawh_in = sem("raw_hid_in"); rawg_in = sem("raw_gate_in"); rawo_in = sem("raw_out_in")
        rawb_in = sem("raw_bc_in"); rawc_in = sem("raw_c_in")
        cs_in = sem("cs_rows_in"); last_in = sem("chunk_decay_in")
        scratch_out = sem("scratch_written"); y_out = sem("result_written")
        ident_ok = sem("identity_made"); const_ok = sem("constants_made"); pool_link = sem("pool_step")
        zero_ok = sem("hid_dt_cleared"); dve_link = sem("vector_step")
        ln_var = sem("ln_variance"); ln_fac = sem("ln_factor_made")
        xh_ok = sem("normed_made"); smx_in = sem("score_logits_made"); smx_exp = sem("score_exp_made")
        ls_ok = sem("low_scored_made"); xn_sq = sem("xn_squares_summed")
        h_ok = sem("h_made"); h_tmp = sem("h_T_scaled"); h_hi = sem("h_hi_made")
        wd_hi = sem("wt_dt_hi_made"); a_exp = sem("A_exp_made"); dt_act = sem("dt_scalar_step")
        cs_ok = sem("running_sums_made"); tok_ok = sem("dt_made")
        wth_hi = sem("wt_hid_hi_made"); wtg_hi = sem("wt_gate_hi_made"); wtb_hi = sem("wt_bc_hi_made")
        wo_hi = sem("wo_hi_made")
        tap_ok = sem("hid_tap_made"); conv_st = sem("hid_conv_step"); hid_ok = sem("hid_made")
        btap_ok = sem("bc_tap_made"); bconv_st = sem("bc_conv_step"); bc_ok = sem("bc_made")
        dif_ok = sem("exponents_made"); e_ok = sem("decay_in_made"); exp_ok = sem("decay_exp_made"); m_ok = sem("scores_made")
        xd_ok = sem("hid_dt_decay_made"); st_step = sem("state_step")
        dh_ok = sem("D_hid_made")
        pool_y = sem("y_step"); r_ok = sem("rms_factor_made"); sq_zero = sem("sum_sq_cleared")
        ys_hi = sem("ys_hi_made"); ys_ok = sem("ys_made"); ys_used = sem("ys_first_half_used")

        block = ctx.enter_context(nc.Block())

        def every(e, tile, tail):
            def group(g, last):
                tile(TPG * g, 0, g, first=True, end=False, last=False)
                with e.Fori(1, TPG - 1) as s:
                    tile(TPG * g + s, s, g, first=False, end=False, last=False)
                tile(TPG * g + TPG - 1, TPG - 1, g, first=False, end=not last, last=last)
                tail(g, last)

            with e.Fori(0, G - 1) as g:
                group(g, False)
            group(G - 1, True)

        def apart(e):
            e.nop(nofuse=True)

        ONCE = {}
        seen = {(b, i): 0 for b in BANKS for i in range(2)}

        def use(name, b, i):
            ONCE[name] = (b, i, seen[b, i])
            seen[b, i] += 1

        def ffn_uses(f):
            use(f"A{f}", "R", 0); use(f"Wr{f}", "R", 1); use(f"B{f}", "P", 0)
            for k in range(NT):
                use(f"xT{f}{k}", "R", k % 2); use(f"low{f}{k}", "P", k % 2)
            for i in range(2):
                use(f"lsT{f}{i}", "X", i)
            for k in range(NT):
                use(f"ffn{f}{k}", "D", k % 2)

        use("tables", "D", 0)
        ffn_uses(0)
        for k in range(NT):
            use(f"hT{k}", "R", k % 2)
        use("WdT", "P", 0); use("dt0", "P", 0); use("dt1", "P", 1)
        for q in range(2):
            use(f"bcW{q}", "R", 0)
            for i in range(2):
                use(f"bc{q}{i}", "P", i)
        use("hW0", "P", 0); use("h0", "P", 0); use("h1", "P", 1); use("hW1", "P", 0); use("gW0", "P", 1)
        for i in range(2):
            use(f"dttok{i}", "R", i); use(f"cstok{i}", "D", i); use(f"dctok{i}", "X", i)
        for i in range(2):
            use(f"CB{i}", "D", i); use(f"Bt{i}", "X", i)
        before_loop = dict(seen)
        BASE = {b: [seen[b, i] for i in range(2)] for b in BANKS}
        for b, i in seen:
            seen[b, i] += PT[b][i] * TILES - (2 if b == "P" else 0)
        ffn_uses(1)

        def full(e, name):
            b, i, n = ONCE[name]
            e.wait_ge(o_full[b][i], n + 1)

        def free_sem(name):
            b, i, _ = ONCE[name]
            return o_free[b][i]

        def freed(e, name):
            b, i, n = ONCE[name]
            e.wait_ge(o_free[b][i], n + 1)

        def ready(e, name):
            b, i, n = ONCE[name]
            if n:
                e.wait_ge(o_free[b][i], n)

        def bank(name):
            b, i, _ = ONCE[name]
            return BANKS[b][:, i, :]

        @block.sync
        def _(sp):
            def ffn_weights():
                sp.dma_start(A_raw[:], A_d).then_inc(ffw_in, 16)
                sp.dma_start(Wr_raw[:], ffn_Wr).then_inc(ffw_in, 16)
                for a in range(KD):
                    sp.dma_start(B_raw[:, a], B_d[:, a]).then_inc(ffw_in, 16)
                sp.dma_start(brb[:], ffn_br.rearrange("(a h) -> a h", a=1).to_broadcast([P, FH])).then_inc(ffw_in, 16)

            def rows(dst, first, s):
                sp.dma_start(dst[:].rearrange("p a d -> p (a d)"),
                             in_proj_w[bass.ds(first, P), :]).then_inc(s, 16)

            def out_cols(t):
                sp.dma_start(raw_o[:], outw_d[:, :, bass.ds(t * P, P)]).then_inc(rawo_in, 16)

            def cs_rows(head):
                sp.dma_start(CSB[:].rearrange("p c i -> p (c i)"), cs_d[bass.ds(head, 1)].to_broadcast([P, T])
                             ).then_inc(cs_in, 16)

            for k in range(0, NT, 2):
                sp.dma_start(XR[:, k:k + 2], x_d[:, k:k + 2]).then_inc(x_in, 16)
            ffn_weights()
            for dst, src in (
                (cwr[:], conv_w.rearrange("(t p) k -> t (p k)", p=P)),
                (cbr[:], conv_b.rearrange("(t p) -> t p", p=P)),
                (gwr[:], gnorm_w.rearrange("(t p) -> t p", p=P)),
                (nwr[:], norm_w.rearrange("(t p) -> t p", p=P)),
                (dtb[:], dt_bias.rearrange("(h a) -> h a", a=1)),
                (negA[:], A_log.rearrange("(h a) -> h a", a=1)),
                (Drow[:], Dp.rearrange("(a h) -> a h", a=1).to_broadcast([P, H])),
            ):
                sp.dma_start(dst, src).then_inc(tab_in, 16)
            rows(raw_g, DT0, rawg_in)
            rows(raw_f[0], B0, rawb_in)
            rows(raw_f[1], C0, rawc_in)
            rows(raw_h, HID0, rawh_in)
            sp.dma_start(raw_o[:], outw_d[:, :, 0:P]).then_inc(rawo_in, 16)
            full(sp, "WdT")
            rows(raw_g, 0, rawg_in)
            full(sp, "hW0")
            rows(raw_h, HID0 + P, rawh_in)
            sp.wait_ge(cs_ok, 1)
            sp.dma_start(cs_d, dtS[4][:]).then_inc(scratch_out, 16)
            sp.wait_ge(dt_act, 5)
            for b in range(NB):
                for c in range(2):
                    k = b * NCH + c + 1
                    sp.dma_start(last_d[2 * b + c].rearrange("(h a) -> h a", a=1),
                                 dtS[6][:, k:k + 1]).then_inc(scratch_out, 16)
            sp.wait_ge(scratch_out, 16 * (1 + 2 * NB))
            cs_rows(0)
            sp.dma_start(EL[:].rearrange("p b c h -> p (b c h)"),
                         last_d.rearrange("(a k) h -> a (k h)", a=1).to_broadcast([P, 2 * NB * H])).then_inc(last_in, 16)
            full(sp, "hW1")
            rows(raw_h, HID0 + 2 * P, rawh_in)
            full(sp, "gW0")
            rows(raw_g, P, rawg_in)

            full(sp, "CB1")
            full(sp, "Bt1")
            rows(raw_b, B0 + P, rawb_in)
            rows(raw_c, C0 + P, rawc_in)

            def tile(t, s, g, first, end, last):
                def next_head(h):
                    sp.wait_ge(dif_ok, 4 * t + 2 * h + 2)
                    apart(sp)
                    sp.wait_ge(e_ok, 2 * t + h + 1)
                    apart(sp)
                    cs_rows(2 * t + h + 1)

                next_head(0)
                if last:
                    return
                sp.wait_ge(t_full["X"][0], BASE["X"][0] + 3 * t + 1)
                out_cols(t + 1)
                next_head(1)
                sp.wait_ge(t_full["P"][0], BASE["P"][0] + 3 * t + 3)
                rows(raw_h, HID0 + (t + 3) * P, rawh_in)
                sp.wait_ge(t_full["P"][1], BASE["P"][1] + 3 * t + 3)
                rows(raw_g, (t + 2) * P, rawg_in)

            def tail(g, last):
                if last:
                    return
                sp.wait_ge(l_full["D"][1], 5 * g + 3)
                apart(sp)
                sp.wait_ge(l_full["X"][1], g + 1)
                rows(raw_b, B0 + (g + 2) * P, rawb_in)
                rows(raw_c, C0 + (g + 2) * P, rawc_in)

            every(sp, tile, tail)
            sp.wait_ge(l_free["D"][1], 5 * (G - 1) + 4)
            ffn_weights()
            for k in range(NT):
                freed(sp, f"ffn1{k}")
                sp.dma_start(out_d[:, k], XR[:, k]).then_inc(y_out, 16)
            sp.wait_ge(y_out, 16 * NT)

        @block.tensor
        def _(pe):
            def transposes(name, blocks, out_ap=None):
                ready(pe, name)
                dst = bank(name) if out_ap is None else out_ap
                for k, a in enumerate(blocks):
                    w = a.shape[0]
                    last = pe.transpose(dst[0:a.shape[1], k * w:(k + 1) * w], a, ident[0:w, 0:w])
                b, i, _ = ONCE[name]
                last.then_inc(o_full[b][i], 1)

            def project(dst, wt, b):
                n = 0
                cols = slice(b * S, (b + 1) * S)
                for a in range(KD):
                    for w, h in ((wt[:, 0, a], HTh), (wt[:, 0, a], HTl), (wt[:, 1, a], HTh)):
                        last = pe.matmul(dst, w, h[:, a, cols], start=(n == 0), stop=(n == 3 * KD - 1))
                        n += 1
                return last

            def cb(psum, i):
                for c in range(NCH):
                    k = (i * NCH + c) * P
                    last = pe.matmul(psum[:, c * P:(c + 1) * P], BT[:, k:k + P], CT[:, k:k + P],
                                     start=True, stop=True)
                return last

            def b_tok(psum, i):
                for c in range(NCH):
                    k = (i * NCH + c) * P
                    last = pe.transpose(psum[:, c * P:(c + 1) * P], BT[:, k:k + P], ident[:])
                return last

            def w_blocks(raw):
                return [raw[:, a, :] for a in range(KD)]

            def ffn(f):
                pe.wait_ge(ffw_in, 16 * (3 + KD) * (f + 1))
                transposes(f"A{f}", [A_raw[:, a * P:(a + 1) * P] for a in range(KD)])
                transposes(f"Wr{f}", [Wr_raw[:, a * P:(a + 1) * P] for a in range(KD)])
                transposes(f"B{f}", [B_raw[:, a].rearrange("p h r -> p (h r)") for a in range(KD)])
                for k in range(NT + 1):
                    if k < NT:
                        pe.wait_ge(xh_ok, 2 * NT * f + k + 1)
                        transposes(f"xT{f}{k}", [XH[:, k, a * P:(a + 1) * P] for a in range(KD)])
                    if k:
                        j = k - 1
                        freed(pe, f"A{f}")
                        freed(pe, f"Wr{f}")
                        freed(pe, f"xT{f}{j}")
                        ready(pe, f"low{f}{j}")
                        for a in range(KD):
                            last = pe.matmul(bank(f"low{f}{j}")[:, 0:HR + FH], TT[:, j % 2, a], AT[:, a],
                                             start=(a == 0), stop=(a == KD - 1))
                        last.then_inc(o_full["P"][j % 2], 1)
                for i in range(2):
                    pe.wait_ge(ls_ok, f + 1)
                    transposes(f"lsT{f}{i}", [LS[:, 4 * i + c] for c in range(4)])
                for k in range(NT):
                    freed(pe, f"B{f}")
                    freed(pe, f"lsT{f}{k // 4}")
                    ready(pe, f"ffn{f}{k}")
                    pe.matmul(bank(f"ffn{f}{k}"), LST[:, k], BTm[:], start=True, stop=True
                              ).then_inc(o_full["D"][k % 2], 1)

            pe.wait_ge(ident_ok, 1)
            pe.wait_ge(tab_in, 16 * 7)
            at = 0
            for rows in [cwr[:, k::TAPS] for k in range(TAPS)] + [cbr[:], gwr[:], nwr[:]]:
                n = rows.shape[0]
                mm = pe.transpose(psD[:, 0, at:at + n], rows, ident[0:n, 0:n])
                at += n
            mm.then_inc(o_full["D"][0], 1)
            ffn(0)
            for k in range(NT):
                pe.wait_ge(h_ok, k + 1)
                transposes(f"hT{k}", [XH[:, k, a * P:(a + 1) * P] for a in range(KD)])
            pe.wait_ge(rawg_in, 16)
            transposes("WdT", w_blocks(raw_g))
            freed(pe, "WdT")
            for k in range(NT - 2, NT):
                freed(pe, f"hT{k}")
            for b in range(NB):
                ready(pe, f"dt{b}")
                project(bank(f"dt{b}"), WTd, b).then_inc(o_full["P"][b], 1)
            for q in range(2):
                pe.wait_ge((rawb_in, rawc_in)[q], 16)
                transposes(f"bcW{q}", w_blocks(raw_f[q]))
                freed(pe, f"bcW{q}")
                for b in range(NB):
                    ready(pe, f"bc{q}{b}")
                    project(bank(f"bc{q}{b}"), WTf[q], b).then_inc(o_full["P"][b], 1)
            pe.wait_ge(rawh_in, 16)
            transposes("hW0", w_blocks(raw_h))
            freed(pe, "hW0")
            for b in range(NB):
                ready(pe, f"h{b}")
                project(bank(f"h{b}"), WTh, b).then_inc(o_full["P"][b], 1)
            pe.wait_ge(rawh_in, 32)
            transposes("hW1", w_blocks(raw_h))
            pe.wait_ge(rawg_in, 32)
            transposes("gW0", w_blocks(raw_g))
            pe.wait_ge(tok_ok, 1)
            for i in range(2):
                transposes(f"dttok{i}", [dtS[2][:, (4 * i + c) * P:(4 * i + c + 1) * P] for c in range(4)])
            pe.wait_ge(cs_ok, 1)
            for i in range(2):
                transposes(f"cstok{i}", [dtS[4][:, (4 * i + c) * P:(4 * i + c + 1) * P] for c in range(4)])
            pe.wait_ge(dt_act, 4)
            for i in range(2):
                transposes(f"dctok{i}", [dtS[5][:, (4 * i + c) * P:(4 * i + c + 1) * P] for c in range(4)])
            for i in range(2):
                pe.wait_ge(bc_ok, 4)
                ready(pe, f"CB{i}")
                cb(bank(f"CB{i}"), i).then_inc(o_full["D"][i], 1)
                ready(pe, f"Bt{i}")
                b_tok(bank(f"Bt{i}"), i).then_inc(o_full["X"][i], 1)
            for (b, i), n in before_loop.items():
                pe.wait_ge(o_free[b][i], n)
            pe.wait_ge(const_ok, 1)

            def tile(t, s, g, first, end, last):
                def fill(b, i, k):
                    pe.wait_ge(t_free[b][i], BASE[b][i] + PT[b][i] * t + k)

                for b in range(NB):
                    pe.wait_ge(hid_ok, 2 * t + b + 1)
                    fill("R", b, 0)
                    for c in range(NCH):
                        k = (b * NCH + c) * P
                        mm = pe.transpose(psR[:, b, c * P:(c + 1) * P], hidT[:, k:k + P], ident[:])
                    mm.then_inc(t_full["R"][b], 1)

                def hid_next(b):
                    fill("P", b, 0)
                    if not last:
                        project(psP[:, b], WTh, b).then_inc(t_full["P"][b], 1)

                gk = 0 if last else 1

                def gate(b):
                    fill("P", b, gk)
                    project(psP[:, b], WTg, b).then_inc(t_full["P"][b], 1)

                hid_next(0)
                pe.wait_ge(rawo_in, 16 * (t + 1))
                fill("X", 0, 0)
                for a in range(KD):
                    mm = pe.transpose(psX[:, 0, a * P:(a + 1) * P], raw_o[:, a], ident[:])
                mm.then_inc(t_full["X"][0], 1)
                hid_next(1)
                for b in (1, 0):
                    pe.wait_ge(xd_ok, XD0 + 4 * t + 2 * b + 2)
                    fill("X", b, 1 - b)
                    for c in range(NCH - 1):
                        mm = pe.matmul(psX[:, b, c * P:(c + 1) * P], BTok[:, b * NCH + c], XD[:, b, c],
                                       start=True, stop=True)
                    mm.then_inc(t_full["X"][b], 1)
                gate(0)
                gate(1)
                for b in range(NB):
                    fill("D", b, 0)
                    pe.wait_ge(m_ok, 4 * t + b + 3)
                    for c in range(NCH):
                        pe.matmul(psD[:, b, c * P:(c + 1) * P], hcA[:, b * NCH + c], LM[:, 0, b, c],
                                  start=True, stop=False)
                        mm = pe.matmul(psD[:, b, c * P:(c + 1) * P], hcB[:, b * NCH + c], LM[:, 1, b, c],
                                       start=False, stop=True)
                    mm.then_inc(t_full["D"][b], 1)
                    if not last:
                        pe.wait_ge(rawg_in if b else rawh_in, 16 * (t + 3))
                        fill("P", b, 2)
                        for a in range(KD):
                            mm = pe.transpose(psP[:, b, a * P:(a + 1) * P], (raw_g if b else raw_h)[:, a], ident[:])
                        mm.then_inc(t_full["P"][b], 1)
                if end:
                    for i, raw, arrived in ((0, raw_b, rawb_in), (1, raw_c, rawc_in)):
                        pe.wait_ge(arrived, 16 * (g + 2))
                        fill("R", i, 1)
                        for a in range(KD):
                            mm = pe.transpose(psR[:, i, a * P:(a + 1) * P], raw[:, a], ident[:])
                        mm.then_inc(l_full["R"][i], 1)
                for b in range(NB):
                    fill("X", b, 2 - b)
                    if b == 0:
                        fill("X", 1, 1)
                    for c in range(NCH - 1):
                        k = (b * NCH + c + 1) * P
                        mm = pe.matmul(psX[:, b, c * P:(c + 1) * P], ST[:, b, c], CT[:, k:k + P],
                                       start=True, stop=True)
                    mm.then_inc(t_full["X"][b], 1)

            def tail(g, last):
                def ended(b, i):
                    pe.wait_ge(t_free[b][i], BASE[b][i] + PT[b][i] * TPG * (g + 1) - (2 if last and b == "P" else 0))

                def d_use(m):
                    return m // 2 + (1 if m >= 4 and not last else 0)

                def share(m, hf):
                    if hf == 0:
                        if m < 2:
                            ended("D", m)
                        else:
                            pe.wait_ge(l_free["D"][m % 2], 5 * g + d_use(m))
                    pe.wait_ge(ys_ok, YS0 + 2 * NT * g + 2 * m + hf + 1)
                    n = 0
                    for j in range(4):
                        kt = 4 * hf + j
                        for y, w in ((YS[:, hf, 0, j], WOh), (YS[:, hf, 0, j], WOl), (YS[:, hf, 1, j], WOh)):
                            mm = pe.matmul(psD[:, m % 2], y, w[:, kt], start=(hf == 0 and n == 0),
                                           stop=(hf == 1 and n == 11))
                            n += 1
                    mm.then_inc(l_full["D"][m % 2] if hf else ys_used, 1)

                def b_or_c(q, b):
                    if q == 0:
                        if b == 0:
                            pe.wait_ge(l_free["R"][0], g + 1)
                        ended("P", b)
                    else:
                        if b == 0:
                            pe.wait_ge(l_free["R"][1], 2 * g + 1)
                        pe.wait_ge(l_free["P"][b], 2 * g + 1)
                    project(psP[:, b], WTbc[:, q], b).then_inc(l_full["P"][b], 1)

                def squares():
                    if last:
                        ended("R", 1)
                    pe.wait_ge(pool_y, Y0 + 4 * TPG * (g + 1))
                    for k in range(NT):
                        mm = pe.matmul(psR[:, 1, k:k + 1], SQ[:, k * P:(k + 1) * P], ones[:], start=True, stop=True)
                    mm.then_inc(l_full["R"][1], 1)

                ended("X", 0)
                share(0, 0)
                if last:
                    share(0, 1)
                    squares()
                else:
                    for b in range(NB):
                        b_or_c(0, b)
                    share(0, 1)
                    b_or_c(1, 0)
                    squares()
                    b_or_c(1, 1)
                for m in range(1, NT):
                    if m == 4 and not last:
                        pe.wait_ge(bc_ok, 4 * (g + 2))
                        pe.wait_ge(l_free["D"][0], 5 * g + 2)
                        cb(psD[:, 0], 0).then_inc(l_full["D"][0], 1)
                        for i in range(2):
                            ended("X", i)
                            b_tok(psX[:, i], i).then_inc(l_full["X"][i], 1)
                        pe.wait_ge(l_free["D"][1], 5 * g + 2)
                        cb(psD[:, 1], 1).then_inc(l_full["D"][1], 1)
                    share(m, 0)
                    share(m, 1)
                if not last:
                    for b, i in (("X", 0), ("X", 1), ("P", 0), ("P", 1), ("R", 0), ("R", 1)):
                        pe.wait_ge(l_free[b][i], PL[b][i] * (g + 1))

            every(pe, tile, tail)
            pe.wait_ge(l_free["D"][0], 5 * (G - 1) + 4)
            pe.wait_ge(l_free["D"][1], 5 * (G - 1) + 4)
            ffn(1)

        @block.scalar
        def _(act):
            def tap(dst, src, ct, looped=False):
                if looped:
                    apart(act)
                return act.activation(dst, src, ACT.Identity, scale=cw[:, bass.ds(ct, 1), TAPS - 1],
                                      bias=cb[:, bass.ds(ct, 1)])

            def split_hi(dst, src):
                return act.activation(dst, src, ACT.Copy)

            def flat(w):
                return w.rearrange("p a c -> p (a c)")

            def ffn(f):
                full(act, f"A{f}")
                act.activation(AT[:, :, 0:HR], bank(f"A{f}").rearrange("p (a c) -> p a c", a=KD), ACT.Copy
                               ).then_inc(free_sem(f"A{f}"), 1)
                full(act, f"Wr{f}")
                act.activation(AT[:, :, HR:], bank(f"Wr{f}")[:, 0:KD * FH].rearrange("p (a c) -> p a c", a=KD),
                               ACT.Copy).then_inc(free_sem(f"Wr{f}"), 1)
                full(act, f"B{f}")
                act.activation(BTm[:], bank(f"B{f}"), ACT.Copy).then_inc(free_sem(f"B{f}"), 1)
                for k in range(NT):
                    full(act, f"xT{f}{k}")
                    if k >= 2:
                        full(act, f"low{f}{k - 2}")
                    act.activation(flat(TT[:, k % 2]), bank(f"xT{f}{k}"), ACT.Copy
                                   ).then_inc(free_sem(f"xT{f}{k}"), 1)
                act.wait_ge(smx_in, f + 1)
                act.activation(pe_[:], lg[:], ACT.Exp).then_inc(smx_exp, 1)
                for i in range(2):
                    full(act, f"lsT{f}{i}")
                    act.activation(flat(LST[:, 4 * i:4 * i + 4]), bank(f"lsT{f}{i}"),
                                   ACT.Copy).then_inc(free_sem(f"lsT{f}{i}"), 1)

            ffn(0)
            for k in range(NT):
                act.wait_ge(xh_ok, NT + k + 1)
                full(act, f"ffn0{NT - 1 - (k + 1) % 2}")
                if k >= 2:
                    act.wait_ge(xn_sq, k - 1)
                act.activation(flat(LST[:, 4 * (k % 2):4 * (k % 2) + 4]), XH[:, k], ACT.Square,
                               accum_out=s2[:, k:k + 1]).then_inc(xn_sq, 1)
            for k in range(NT):
                act.wait_ge(h_tmp, k + 1)
                act.activation(HTh[:, :, k * P:(k + 1) * P], TT[:, k % 2], ACT.Copy).then_inc(h_hi, 1)
            act.wait_ge(tab_in, 16 * 7)
            freed(act, "tables")
            act.activation(negA[:], negA[:], ACT.Exp).then_inc(a_exp, 1)
            full(act, "WdT")
            act.activation(flat(WTd[:, 0]), bank("WdT"), ACT.Copy).then_inc(wd_hi, 1)
            for b in range(NB):
                freed(act, f"dt{b}")
            act.activation(dtS[1][:], dtS[0][:], ACT.Abs).then_inc(dt_act, 1)
            act.wait_ge(dt_act, 1)
            act.activation(dtS[3][:], dtS[1][:], ACT.Exp, scale=-1.0).then_inc(dt_act, 1)
            act.wait_ge(dt_act, 2)
            act.activation(dtS[4][:], dtS[3][:], ACT.Ln, bias=1.0).then_inc(dt_act, 1)

            def bc_taps(q, b, src, ct, looped):
                dst = (BT, CT)[q]
                tap(dst[:, b * S:(b + 1) * S], src, ct, looped).then_inc(btap_ok, 1)

            def bc_silu(q, b):
                dst = (BT, CT)[q][:, b * S:(b + 1) * S]
                act.activation(dst, dst, ACT.Silu).then_inc(bc_ok, 1)

            for q in range(2):
                full(act, f"bcW{q}")
                act.activation(flat(WTf[q][:, 0]), bank(f"bcW{q}"), ACT.Copy).then_inc(wtb_hi, 1)
                for b in range(NB):
                    full(act, f"bc{q}{b}")
                    bc_taps(q, b, bank(f"bc{q}{b}"), TILES + G * q, False)
                if q == 0:
                    act.wait_ge(cs_ok, 1)
                    for k in range(NT):
                        e = act.activation(dtS[5][:, k * P:(k + 1) * P], dtS[4][:, k * P:(k + 1) * P], ACT.Exp,
                                           scale=-1.0, bias=dtS[4][:, (k + 1) * P - 1:(k + 1) * P])
                    e.then_inc(dt_act, 1)
                    act.activation(dtS[6][:, 0:NT], dtS[4][:, P - 1::P], ACT.Exp).then_inc(dt_act, 1)
            full(act, "hW0")
            act.activation(flat(WTh[:, 0]), bank("hW0"), ACT.Copy).then_inc(wth_hi, 1)
            for b in range(NB):
                full(act, f"h{b}")
                tap(hidT[:, b * S:(b + 1) * S], bank(f"h{b}"), 0).then_inc(tap_ok, 1)
            full(act, "hW1")
            act.activation(flat(WTh[:, 0]), bank("hW1"), ACT.Copy).then_inc(wth_hi, 1)
            full(act, "gW0")
            act.activation(flat(WTg[:, 0]), bank("gW0"), ACT.Copy).then_inc(wtg_hi, 1)
            for q in range(2):
                for b in range(NB):
                    freed(act, f"bc{q}{b}")
                    bc_silu(q, b)
            for b in range(NB):
                freed(act, f"h{b}")
                act.activation(hidT[:, b * S:(b + 1) * S], hidT[:, b * S:(b + 1) * S], ACT.Silu).then_inc(hid_ok, 1)
            act.wait_ge(last_in, 16)
            act.wait_ge(scratch_out, 16 * (1 + 2 * NB))
            freed(act, "dttok1")
            freed(act, "cstok1")
            freed(act, "dctok1")

            def share_hi(g, m, hf, last):
                if m and hf == 0:
                    act.wait_ge(ys_used, NT * g + m)
                if m and hf == 1:
                    k = (m - 1) // 2 + (1 if m - 1 >= 4 and not last else 0)
                    act.wait_ge(l_full["D"][(m - 1) % 2], 5 * g + k + 1)
                act.activation(YS[:, hf, 0], YG[:, 4 * hf:4 * hf + 4, m * P:(m + 1) * P], ACT.Copy
                               ).then_inc(ys_hi, 1)

            def tile(t, s, g, first, end, last):
                act.wait_ge(hid_ok, 2 * t + 2)
                act.wait_ge(ys_ok, YS0 + 2 * NT * g)
                apart(act)
                act.activation(YG[:, bass.ds(s, 1), :].rearrange("p a t -> p (a t)"), hidT[:], ACT.Copy,
                               scale=Dc[:, bass.ds(t, 1)]).then_inc(dh_ok, 1)

                def tap_next(b):
                    if not last:
                        act.wait_ge(dh_ok, t + 1)
                        act.wait_ge(t_full["R"][b], BASE["R"][b] + t + 1)
                        act.wait_ge(t_full["P"][b], BASE["P"][b] + 3 * t + 1)
                        tap(hidT[:, b * S:(b + 1) * S], psP[:, b], t + 1, True).then_inc(tap_ok, 1)

                def decay_exp(h):
                    for b in range(NB):
                        act.wait_ge(dif_ok, 4 * t + 2 * h + b + 1)
                        act.activation(flat(LM[:, h, b]), flat(LM[:, h, b]), ACT.Exp).then_inc(exp_ok, 1)

                def decay_in(h):
                    act.wait_ge(cs_in, 16 * (2 * t + h + 1))
                    act.wait_ge(pool_y, Y0 + 4 * t - 3)
                    rows = slice(h * HP, (h + 1) * HP)
                    cs = CSB[rows].rearrange("p (b c) i -> p b c i", b=NB)
                    act.activation(E[rows, :, 1:NCH], cs[:, :, 1:NCH], ACT.Exp).then_inc(e_ok, 1)

                gk = 0 if last else 1

                def gate(b):
                    act.wait_ge(t_full["P"][b], BASE["P"][b] + 3 * t + gk + 1)
                    act.activation(sg[:, b * S:(b + 1) * S], psP[:, b], ACT.Silu).then_inc(t_free["P"][b], 1)

                decay_in(0)
                tap_next(0)
                act.wait_ge(t_full["X"][0], BASE["X"][0] + 3 * t + 1)
                apart(act)
                act.activation(WOh[:, bass.ds(s, 1), :].rearrange("p a t -> p (a t)"), psX[:, 0], ACT.Copy,
                               scale=gw[:, bass.ds(t, 1)]).then_inc(wo_hi, 1)
                decay_exp(0)
                tap_next(1)
                decay_in(1)
                decay_exp(1)
                if end or last:
                    share_hi(g, 0, 0, last)
                act.wait_ge(pool_y, Y0 + 4 * t)
                gate(0)
                if not last:
                    for b in range(NB):
                        act.wait_ge(t_free["P"][b], BASE["P"][b] + 3 * t + 1)
                        act.activation(hidT[:, b * S:(b + 1) * S], hidT[:, b * S:(b + 1) * S], ACT.Silu
                                       ).then_inc(hid_ok, 1)
                gate(1)
                if not last:
                    act.wait_ge(t_full["P"][0], BASE["P"][0] + 3 * t + 3)
                    act.activation(flat(WTh[:, 0]), psP[:, 0], ACT.Copy).then_inc(wth_hi, 1)
                    act.wait_ge(t_full["P"][1], BASE["P"][1] + 3 * t + 3)
                    act.activation(flat(WTg[:, 0]), psP[:, 1], ACT.Copy).then_inc(wtg_hi, 1)

            def tail(g, last):
                def taps(q, b):
                    act.wait_ge(l_full["P"][b], 2 * g + q + 1)
                    bc_taps(q, b, psP[:, b], TILES + G * q + g + 1, True)

                def silus(q):
                    for b in range(NB):
                        act.wait_ge(l_free["P"][b], 2 * g + q + 1)
                        bc_silu(q, b)

                if not last:
                    act.wait_ge(t_full["D"][1], BASE["D"][1] + TPG * (g + 1))
                    for i in range(2):
                        act.wait_ge(l_full["R"][i], PL["R"][i] * g + 1)
                        act.activation(flat(WTbc[:, i, 0]), psR[:, i], ACT.Copy).then_inc(wtb_hi, 1)
                act.wait_ge(pool_y, Y0 + 4 * TPG * (g + 1) - 2)
                share_hi(g, 0, 1, last)
                if not last:
                    taps(0, 0)
                share_hi(g, 1, 0, last)
                if not last:
                    taps(0, 1)
                    act.wait_ge(t_full["X"][1], BASE["X"][1] + 2 * TPG * (g + 1))
                    taps(1, 0)
                share_hi(g, 1, 1, last)
                if not last:
                    taps(1, 1)
                if not last:
                    silus(0)
                    silus(1)
                for m in range(2, NT):
                    share_hi(g, m, 0, last)
                    share_hi(g, m, 1, last)

            every(act, tile, tail)
            ffn(1)

        @block.vector
        def _(dve):
            steps = [0]

            def link(ins):
                steps[0] += 1
                ins.then_inc(dve_link, 1)
                dve.wait_ge(dve_link, steps[0])

            def layer_norm(n):
                for k in range(NT):
                    last = dve.bn_stats(bst[:, k], XR[:, k])
                link(last)
                for k in range(NT):
                    last = dve.bn_aggr(bag[:, k], bst[:, k])
                link(last)
                dve.tensor_scalar(rv[:], bag[:, :, 1], LN_EPS, None, ALU.add).then_inc(ln_var, 1)
                dve.wait_ge(ln_fac, (1, 2, 4)[n])
                for k in range(NT):
                    dve.tensor_scalar(XH[:, k], XR[:, k], bag[:, k, 0:1], rs[:, k:k + 1], ALU.subtract, ALU.mult
                                      ).then_inc(xh_ok, 1)

            def ffn(f):
                for k in range(NT):
                    full(dve, f"low{f}{k}")
                    dve.tensor_copy(low[:, k], bank(f"low{f}{k}")[:, 0:HR + FH]).then_inc(free_sem(f"low{f}{k}"), 1)
                for k in (NT - 2, NT - 1):
                    freed(dve, f"low{f}{k}")
                wide = [P, NT, FH]
                dve.wait_ge(ffw_in, 16 * (3 + KD) * (f + 1))
                link(dve.tensor_tensor(lg[:], low[:, :, HR:], brb[:].unsqueeze(1).to_broadcast(wide), ALU.add))
                link(dve.tensor_reduce(mx[:], lg[:], AX.X, ALU.max))
                dve.tensor_tensor(lg[:], lg[:], mx[:].unsqueeze(2).to_broadcast(wide), ALU.subtract
                                  ).then_inc(smx_in, 1)
                dve.wait_ge(smx_exp, f + 1)
                link(dve.tensor_reduce(sm[:], pe_[:], AX.X, ALU.add))
                link(dve.reciprocal(mx[:], sm[:]))
                link(dve.scalar_tensor_tensor(out=pw[:], in0=pe_[:], scalar=FFN_SCALE,
                                              in1=mx[:].unsqueeze(2).to_broadcast(wide), op0=ALU.mult, op1=ALU.mult))
                for k in range(NT):
                    last = dve.tensor_tensor(LS[:, k].rearrange("p (h r) -> p h r", h=FH),
                                             low[:, k, 0:HR].rearrange("p (h r) -> p h r", h=FH),
                                             pw[:, k].unsqueeze(2).to_broadcast([P, FH, FR]), ALU.mult)
                last.then_inc(ls_ok, 1)
                for k in range(NT):
                    full(dve, f"ffn{f}{k}")
                    dve.tensor_tensor(XR[:, k], XR[:, k], bank(f"ffn{f}{k}"), ALU.add
                                      ).then_inc(free_sem(f"ffn{f}{k}"), 1)
                for k in (NT - 2, NT - 1):
                    freed(dve, f"ffn{f}{k}")

            def conv_tap(step, n, dst, src, ct, done, d):
                if d > 1:
                    dve.wait_ge(step, n + d - 1)
                dve.scalar_tensor_tensor(out=dst[:, d:S], in0=src[:, 0:S - d],
                                         scalar=cw[:, bass.ds(ct, 1), TAPS - 1 - d], in1=dst[:, d:S],
                                         op0=ALU.mult, op1=ALU.add
                                         ).then_inc(done if d == TAPS - 1 else step, 1)

            def conv(step, n, dst, src, ct, done):
                for d in range(1, TAPS):
                    conv_tap(step, n, dst, src, ct, done, d)

            def split_lo(dst, src, hi, done):
                dve.tensor_tensor(dst.rearrange("p a c -> p (a c)"), src,
                                  hi.rearrange("p a c -> p (a c)").bitcast(F32), ALU.subtract).then_inc(done, 1)

            dve.memset(hcA[:], 0.0).then_inc(ys_ok, 1)
            dve.memset(hcB[:], 0.0).then_inc(zero_ok, 1)
            dve.wait_ge(x_in, 16 * NT // 2)
            layer_norm(0)
            full(dve, "tables")
            n = TAPS * CT_ALL
            dve.tensor_copy(cw[:].rearrange("p t k -> p k t"), bank("tables")[:, 0:n].rearrange("p (k t) -> p k t", k=TAPS))
            for dst in (cb, gw, nw):
                last = dve.tensor_copy(dst[:], bank("tables")[:, n:n + dst.shape[1]])
                n += dst.shape[1]
            for h in range(2):
                last = dve.tensor_copy(Dc[h * HP:(h + 1) * HP, :], Drow[h * HP:(h + 1) * HP, h::2])
            last.then_inc(free_sem("tables"), 1)
            freed(dve, "tables")
            ffn(0)
            layer_norm(1)
            dve.wait_ge(xh_ok, 2 * NT)
            for k in range(NT):
                last = dve.tensor_tensor(XR[:, k], XR[:, k], XH[:, k], ALU.add)
            dve.wait_ge(xn_sq, NT)
            dve.tensor_scalar(rv[:], s2[:], 1.0 / DM, RMS_EPS, ALU.mult, ALU.add).then_inc(ln_var, 1)
            dve.wait_ge(ln_fac, 3)
            for k in range(NT):
                dve.tensor_scalar(XH[:, k], XH[:, k], rs[:, k:k + 1], None, ALU.mult).then_inc(h_ok, 1)
            dve.wait_ge(tab_in, 16 * 7)
            for k in range(NT + 1):
                if k < NT:
                    full(dve, f"hT{k}")
                    dve.tensor_tensor(TT[:, k % 2], bank(f"hT{k}").rearrange("p (a c) -> p a c", a=KD),
                                      nw[:].unsqueeze(2).to_broadcast([P, KD, P]), ALU.mult).then_inc(h_tmp, 1)
                if k:
                    j = k - 1
                    dve.wait_ge(h_hi, j + 1)
                    dve.tensor_tensor(HTl[:, :, j * P:(j + 1) * P], TT[:, j % 2],
                                      HTh[:, :, j * P:(j + 1) * P].bitcast(F32), ALU.subtract
                                      ).then_inc(free_sem(f"hT{j}"), 1)
            full(dve, "WdT")
            dve.wait_ge(wd_hi, 1)
            split_lo(WTd[:, 1], bank("WdT"), WTd[:, 0], free_sem("WdT"))
            for b in range(NB):
                full(dve, f"dt{b}")
                dve.tensor_scalar(dtS[0][:, b * S:(b + 1) * S], bank(f"dt{b}"), dtb[:], None, ALU.add
                                  ).then_inc(free_sem(f"dt{b}"), 1)

            def bc_first(q):
                full(dve, f"bcW{q}")
                dve.wait_ge(wtb_hi, q + 1)
                split_lo(WTf[q][:, 1], bank(f"bcW{q}"), WTf[q][:, 0], free_sem(f"bcW{q}"))

            def bc_conv_first(q):
                for b in range(NB):
                    dve.wait_ge(btap_ok, 2 * q + b + 1)
                    conv(bconv_st, 2 * (2 * q + b), (BT, CT)[q][:, b * S:(b + 1) * S], bank(f"bc{q}{b}"),
                         TILES + G * q, free_sem(f"bc{q}{b}"))

            bc_first(0)
            dve.wait_ge(dt_act, 3)
            dve.wait_ge(a_exp, 1)
            link(dve.tensor_scalar(negA[:], negA[:], -1.0, None, ALU.mult))
            for b in range(NB):
                freed(dve, f"dt{b}")
            dve.scalar_tensor_tensor(out=dtS[2][:], in0=dtS[0][:], scalar=0.0, in1=dtS[4][:], op0=ALU.max,
                                     op1=ALU.add).then_inc(tok_ok, 1)
            dve.wait_ge(tok_ok, 1)
            link(dve.tensor_scalar(dtS[1][:], dtS[2][:], negA[:], EXP_FLOOR, ALU.mult, ALU.max))
            link(dve.memset(dtS[3][:], 1.0))
            link(dve.memset(dtS[3][:, 0::P], 0.0))
            dve.tensor_tensor_scan(dtS[4][:], dtS[3][:], dtS[1][:], 0.0, ALU.mult, ALU.add).then_inc(cs_ok, 1)
            bc_conv_first(0)
            bc_first(1)
            bc_conv_first(1)
            full(dve, "hW0")
            dve.wait_ge(wth_hi, 1)
            split_lo(WTh[:, 1], bank("hW0"), WTh[:, 0], free_sem("hW0"))
            for b in range(NB):
                dve.wait_ge(tap_ok, b + 1)
                conv(conv_st, 2 * b, hidT[:, b * S:(b + 1) * S], bank(f"h{b}"), 0, free_sem(f"h{b}"))
            full(dve, "hW1")
            dve.wait_ge(wth_hi, 2)
            split_lo(WTh[:, 1], bank("hW1"), WTh[:, 0], free_sem("hW1"))
            full(dve, "gW0")
            dve.wait_ge(wtg_hi, 1)
            split_lo(WTg[:, 1], bank("gW0"), WTg[:, 0], free_sem("gW0"))
            for name, dst in (("dttok", dtk), ("cstok", ctk), ("dctok", dck)):
                for i in range(2):
                    full(dve, f"{name}{i}")
                    dve.tensor_copy(dst[:, 4 * i:4 * i + 4], bank(f"{name}{i}").rearrange("p (c h) -> p c h", c=4)
                                    ).then_inc(free_sem(f"{name}{i}"), 1)

            def mask_cb(psum, i, done):
                dve.tensor_tensor(GM[:, 4 * i:4 * i + 4], psum.rearrange("p (c i) -> p c i", c=NCH),
                                  causal[:].unsqueeze(1).to_broadcast([P, NCH, P]), ALU.mult).then_inc(done, 1)

            def copy_b(psum, i, done):
                dve.tensor_copy(BTok[:, 4 * i:4 * i + 4], psum.rearrange("p (c i) -> p c i", c=NCH)
                                ).then_inc(done, 1)

            dve.wait_ge(const_ok, 1)
            for i in range(2):
                full(dve, f"CB{i}")
                mask_cb(bank(f"CB{i}"), i, free_sem(f"CB{i}"))
                full(dve, f"Bt{i}")
                copy_b(bank(f"Bt{i}"), i, free_sem(f"Bt{i}"))
            dve.wait_ge(last_in, 16)
            dve.wait_ge(zero_ok, 1)

            def share_lo(g, m, hf):
                dve.wait_ge(ys_hi, 2 * NT * g + 2 * m + hf + 1)
                dve.tensor_tensor(YS[:, hf, 1], YG[:, 4 * hf:4 * hf + 4, m * P:(m + 1) * P],
                                  YS[:, hf, 0].bitcast(F32), ALU.subtract).then_inc(ys_ok, 1)

            def tile(t, s, g, first, end, last):
                dve.wait_ge(xd_ok, XD0 + 4 * t)
                for b in range(NB):
                    dve.wait_ge(t_full["D"][b], BASE["D"][b] + t)
                    dve.wait_ge(t_full["R"][b], BASE["R"][b] + t + 1)
                    src = psR[:, b].rearrange("p (c i) -> p c i", c=NCH)
                    ch = slice(b * NCH, (b + 1) * NCH)
                    for h, dst in enumerate((hcA, hcB)):
                        cols = slice(h * HP, (h + 1) * HP)
                        last_i = dve.tensor_tensor(dst[:, ch, cols], src[:, :, cols],
                                                   dtk[:, ch, bass.ds(2 * t + h, 1)].to_broadcast([P, NCH, HP]),
                                                   ALU.mult)
                    last_i.then_inc(t_free["R"][b], 1)

                def exponents(h, b):
                    if b == 0:
                        dve.wait_ge(cs_in, 16 * (2 * t + h + 1))
                    for c in range(NCH):
                        k = b * NCH + c
                        last_i = dve.tensor_scalar(LM[:, h, b, c], CSB[:, k], ctk[:, k, bass.ds(2 * t + h, 1)], 0.0,
                                                   ALU.subtract, ALU.min)
                    last_i.then_inc(dif_ok, 1)

                def conv_next(b, d):
                    if not last:
                        if d == 1:
                            dve.wait_ge(tap_ok, 2 * t + b + 3)
                        conv_tap(conv_st, 4 * t + 4 + 2 * b, hidT[:, b * S:(b + 1) * S], psP[:, b], t + 1,
                                 t_free["P"][b], d)

                def score(h, b):
                    dve.wait_ge(exp_ok, 4 * t + 2 * h + b + 1)
                    dve.tensor_tensor(LM[:, h, b], LM[:, h, b], GM[:, b * NCH:(b + 1) * NCH], ALU.mult
                                      ).then_inc(m_ok, 1)

                exponents(0, 0)
                exponents(0, 1)
                conv_next(0, 1)
                conv_next(0, 2)
                dve.wait_ge(wo_hi, t + 1)
                dve.scalar_tensor_tensor(out=WOl[:, bass.ds(s, 1), :].rearrange("p a t -> p (a t)"), in0=psX[:, 0],
                                         scalar=gw[:, bass.ds(t, 1)],
                                         in1=WOh[:, bass.ds(s, 1), :].rearrange("p a t -> p (a t)").bitcast(F32),
                                         op0=ALU.mult, op1=ALU.subtract).then_inc(t_free["X"][0], 1)
                conv_next(0, 3)
                conv_next(1, 1)
                score(0, 0)
                conv_next(1, 2)
                score(0, 1)
                conv_next(1, 3)
                exponents(1, 0)
                exponents(1, 1)
                score(1, 0)
                score(1, 1)
                if end or last:
                    share_lo(g, 0, 0)
                dve.wait_ge(t_full["X"][0], BASE["X"][0] + 3 * t + 2)
                dve.wait_ge(t_full["X"][1], BASE["X"][1] + 2 * t + 1)
                halves = lambda a: a.rearrange("p b (h q) -> p b h q", h=2)
                dve.tensor_copy(ST[:, :, 0], psX[:, :, 0:P]).then_inc(st_step, 1)
                for c in range(1, NCH - 1):
                    dve.wait_ge(st_step, 4 * t + 2 * c - 1)
                    dve.tensor_tensor(halves(ST[:, :, c]), halves(ST[:, :, c - 1]),
                                      EL[:, :, c - 1, bass.ds(2 * t, 2)].unsqueeze(3).to_broadcast([P, NB, 2, HP]),
                                      ALU.mult).then_inc(st_step, 1)
                    dve.wait_ge(st_step, 4 * t + 2 * c)
                    if c < NCH - 2:
                        dve.tensor_tensor(ST[:, :, c], ST[:, :, c], psX[:, :, c * P:(c + 1) * P], ALU.add
                                          ).then_inc(st_step, 1)
                    else:
                        for b in range(NB):
                            dve.tensor_tensor(ST[:, b, c], ST[:, b, c], psX[:, b, c * P:(c + 1) * P], ALU.add
                                              ).then_inc(t_free["X"][b], 1)
                dve.wait_ge(dh_ok, t + 1)
                for b in range(NB):
                    dve.wait_ge(t_full["D"][b], BASE["D"][b] + t + 1)
                    y = YG[:, bass.ds(s, 1), b * S:(b + 1) * S].rearrange("p a t -> p (a t)")
                    dve.tensor_tensor(y, y, psD[:, b], ALU.add).then_inc(t_free["D"][b], 1)
                    if not last:
                        dve.wait_ge(wtg_hi if b else wth_hi, t + 3 - b)
                        w = WTg if b else WTh
                        split_lo(w[:, 1], psP[:, b], w[:, 0], t_free["P"][b])
                for b in range(NB):
                    dve.wait_ge(t_full["X"][b], BASE["X"][b] + PT["X"][b] * t + 3 - b)
                    dve.wait_ge(e_ok, 2 * t + 2)
                    dve.tensor_tensor(E[:, b, 1:NCH], E[:, b, 1:NCH],
                                      psX[:, b, 0:(NCH - 1) * P].rearrange("p (c i) -> p c i", c=NCH - 1), ALU.mult
                                      ).then_inc(t_free["X"][b], 1)

            def tail(g, last):
                def bc_conv(q, b):
                    dve.wait_ge(btap_ok, 4 * (g + 1) + 2 * q + b + 1)
                    for d in range(1, TAPS):
                        conv_tap(bconv_st, 8 * (g + 1) + 2 * (2 * q + b), (BT, CT)[q][:, b * S:(b + 1) * S],
                                 psP[:, b], TILES + G * q + g + 1, l_free["P"][b], d)

                def mean_squares():
                    k = PL["R"][1] * g + (1 if last else 2)
                    dve.wait_ge(l_full["R"][1], k)
                    dve.tensor_scalar(vs[:], psR[:, 1, 0:NT], float(G) / DI, RMS_EPS, ALU.mult, ALU.add
                                      ).then_inc(l_free["R"][1], 1)

                def add(m):
                    k = m // 2 + (1 if m >= 4 and not last else 0)
                    dve.wait_ge(l_full["D"][m % 2], 5 * g + k + 1)
                    dve.scalar_tensor_tensor(out=XR[:, m], in0=psD[:, m % 2], scalar=rg[:, m:m + 1], in1=XR[:, m],
                                             op0=ALU.mult, op1=ALU.add).then_inc(l_free["D"][m % 2], 1)

                if not last:
                    for q in range(2):
                        dve.wait_ge(wtb_hi, 2 * g + q + 3)
                        split_lo(WTbc[:, q, 1], psR[:, q], WTbc[:, q, 0], l_free["R"][q])
                share_lo(g, 0, 1)
                if not last:
                    bc_conv(0, 0)
                share_lo(g, 1, 0)
                if not last:
                    bc_conv(0, 1)
                    bc_conv(1, 0)
                share_lo(g, 1, 1)
                mean_squares()
                if not last:
                    bc_conv(1, 1)
                dve.wait_ge(r_ok, g + 1)
                add(0)
                for m in range(2, NT):
                    share_lo(g, m, 0)
                    add(m - 1)
                    share_lo(g, m, 1)
                    if m == 4 and not last:
                        dve.wait_ge(l_full["D"][0], 5 * g + 3)
                        mask_cb(psD[:, 0], 0, l_free["D"][0])
                        for i in range(2):
                            dve.wait_ge(l_full["X"][i], g + 1)
                            copy_b(psX[:, i], i, l_free["X"][i])
                        dve.wait_ge(l_full["D"][1], 5 * g + 3)
                        mask_cb(psD[:, 1], 1, l_free["D"][1])
                add(NT - 1)

            every(dve, tile, tail)
            for i in range(2):
                dve.wait_ge(l_free["D"][i], 5 * (G - 1) + 4)
            layer_norm(2)
            ffn(1)

        @block.gpsimd
        def _(pool):
            steps = [0]

            def link(ins):
                steps[0] += 1
                ins.then_inc(pool_link, 1)
                pool.wait_ge(pool_link, steps[0])

            link(pool.memset(ident[:], 0.0))
            pool.affine_select(out=ident[:], in_=ident[:], compare_op=ALU.not_equal, fill=1.0, base=0,
                               pattern=[[-1, P]], channel_multiplier=1).then_inc(ident_ok, 1)
            link(pool.memset(half[:], -0.5))

            def inv_sqrt(dst, src, n, var, made):
                pool.wait_ge(var, n)
                pool.tensor_tensor(dst[:], src[:], half[:], ALU.pow).then_inc(made, 1)

            inv_sqrt(rs, rv, 1, ln_var, ln_fac)
            pool.memset(ones[:], 1.0)
            link(pool.memset(causal[:], 1.0))
            link(pool.affine_select(out=causal[:], in_=causal[:], compare_op=ALU.is_ge, fill=0.0, base=0,
                                    pattern=[[1, P]], channel_multiplier=-1))
            pool.memset(SQ[:], 0.0).then_inc(sq_zero, 1)
            pool.wait_ge(sq_zero, 1)
            for k in range(Y0):
                pool.memset(rg[:, k:k + 1], 1.0).then_inc(pool_y, 1)
            pool.memset(rg[:, Y0:Y0 + 1], 1.0).then_inc(xd_ok, 1)
            pool.memset(vs[:], 1.0).then_inc(const_ok, 1)
            inv_sqrt(rs, rv, 2, ln_var, ln_fac)
            inv_sqrt(rs, rv, 3, ln_var, ln_fac)

            def state_part(t, s):
                y4 = YG[:, bass.ds(s, 1), :].rearrange("p a (b c i) -> p (a b) c i", b=NB, c=NCH)
                for b in range(NB):
                    pool.wait_ge(t_free["X"][b], BASE["X"][b] + PT["X"][b] * (t + 1))
                    pool.wait_ge(t_free["D"][b], BASE["D"][b] + t + 1)
                apart(pool)
                pool.tensor_tensor(y4[:, :, 1:NCH], y4[:, :, 1:NCH], E[:, :, 1:NCH], ALU.add).then_inc(pool_y, 1)

            def gated(t, s, last):
                y = YG[:, bass.ds(s, 1), :].rearrange("p a t -> p (a t)")
                for b in range(NB):
                    pool.wait_ge(t_free["P"][b], BASE["P"][b] + 3 * t + (1 if last else 2))
                pool.wait_ge(pool_y, Y0 + 4 * t + 1)
                apart(pool)
                pool.tensor_tensor(y, y, sg[:], ALU.mult).then_inc(pool_y, 1)

            def squared(t, s, g):
                y = YG[:, bass.ds(s, 1), :].rearrange("p a t -> p (a t)")
                pool.wait_ge(pool_y, Y0 + 4 * t + 2)
                apart(pool)
                pool.tensor_tensor(sg[:], y, y, ALU.mult).then_inc(pool_y, 1)
                pool.wait_ge(pool_y, Y0 + 4 * t + 3)
                pool.wait_ge(sq_zero, g + 1)
                pool.tensor_tensor(SQ[:], SQ[:], sg[:], ALU.add).then_inc(pool_y, 1)

            def tile(t, s, g, first, end, last):
                if not first:
                    state_part(t - 1, s - 1)
                for b in range(NB):
                    pool.wait_ge(t_full["X"][b], BASE["X"][b] + PT["X"][b] * t)
                    pool.wait_ge(t_free["R"][b], BASE["R"][b] + t + 1)
                    apart(pool)
                    ch = slice(b * NCH, b * NCH + NCH - 1)
                    for h, src in enumerate((hcA, hcB)):
                        cols = slice(h * HP, (h + 1) * HP)
                        pool.tensor_tensor(XD[:, b, :, cols], src[:, ch, cols],
                                           dck[:, ch, bass.ds(2 * t + h, 1)].to_broadcast([P, NCH - 1, HP]),
                                           ALU.mult).then_inc(xd_ok, 1)
                if not first:
                    gated(t - 1, s - 1, False)
                    squared(t - 1, s - 1, g)

            def tail(g, last):
                t = TPG * g + TPG - 1
                state_part(t, TPG - 1)
                gated(t, TPG - 1, last)
                squared(t, TPG - 1, g)
                k = PL["R"][1] * g + (1 if last else 2)
                pool.wait_ge(l_full["R"][1], k)
                inv_sqrt(rg, vs, k, l_free["R"][1], r_ok)
                apart(pool)
                pool.memset(SQ[:], 0.0).then_inc(sq_zero, 1)

            every(pool, tile, tail)
            inv_sqrt(rs, rv, 4, ln_var, ln_fac)


_ORDER = ["x", "norm_w", "in_proj_w", "conv_w", "conv_b", "dt_bias", "A_log", "Dp", "gnorm_w", "out_proj_w",
          "A", "B", "Wr", "br"]


def kernel(L0_attn_x, L0_attn_norm_w, L0_attn_in_proj_w, L0_attn_conv_w, L0_attn_conv_b, L0_attn_dt_bias,
           L0_attn_A_log, L0_attn_Dp, L0_attn_gnorm_w, L0_attn_out_proj_w, L0_ffn_A, L0_ffn_B, L0_ffn_Wr,
           L0_ffn_br):
    import numpy as np
    import concourse.bacc as bacc
    from concourse.bass_utils import run_bass_kernel_spmd

    given = [L0_attn_x, L0_attn_norm_w, L0_attn_in_proj_w, L0_attn_conv_w, L0_attn_conv_b, L0_attn_dt_bias,
             L0_attn_A_log, L0_attn_Dp, L0_attn_gnorm_w, L0_attn_out_proj_w, L0_ffn_A, L0_ffn_B, L0_ffn_Wr,
             L0_ffn_br]
    nc = bacc.Bacc("TRN2", target_bir_lowering=False, num_devices=1)
    arrays, args = {}, []
    for name, a in zip(_ORDER, given):
        a = np.ascontiguousarray(a)
        arrays[f"in_{name}"] = a
        args.append(nc.dram_tensor(f"in_{name}", a.shape, mybir.dt.from_np(a.dtype), kind="ExternalInput").ap())
    y = nc.dram_tensor("out_y", given[0].shape, F32, kind="ExternalOutput").ap()
    macaron(nc, *args, y)
    r = run_bass_kernel_spmd(nc, [arrays], core_ids=[0])
    return r.results[0]["out_y"]
```

```python
from contextlib import ExitStack

import concourse.bass as bass
from concourse import mybir

F32 = mybir.dt.float32
F32R = mybir.dt.float32r
ALU = mybir.AluOpType
ACT = mybir.ActivationFunctionType
AX = mybir.AxisListType

LN_EPS = 1e-5
RMS_EPS = 1e-5
EXP_FLOOR = -128.0


def macaron(nc, x, norm_w, in_proj_w, conv_w, conv_b, dt_bias, A_log, Dp, gnorm_w, out_proj_w,
            ffn_A, ffn_B, ffn_Wr, ffn_br, out):
    P = 128
    NB, S, DM = x.shape
    T = NB * S
    NCH = S // P
    NT = T // P
    KD = DM // P
    H = Dp.shape[0]
    DI = out_proj_w.shape[1]
    HP = DI // H
    CD, TAPS = conv_w.shape
    N = P
    G = (CD - DI) // (2 * N)
    TILES = DI // P
    TPG = TILES // G
    CT_ALL = CD // P
    FH, FR, _ = ffn_A.shape
    HR = FH * FR
    assert (P, H, HP, NT, S, DM) == (HR, P, P // 2, 8, 512, 512)
    FFN_SCALE = float(FH)

    x_d = x.rearrange("b (c p) d -> p (b c) d", p=P)
    out_d = out.rearrange("b (c p) d -> p (b c) d", p=P)
    A_d = ffn_A.rearrange("h r d -> (h r) d")
    B_d = ffn_B.rearrange("h (a p) r -> p a h r", p=P)
    outw_d = out_proj_w.rearrange("(a p) d -> p a d", p=P)
    HID0, B0, C0, DT0 = DI, 2 * DI, 2 * DI + G * N, DI + CD
    cs_d = nc.dram_tensor("running_sums", [H, T], F32, kind="Internal").ap()
    last_d = nc.dram_tensor("chunk_decay", [2 * NB, H], F32, kind="Internal").ap()

    with ExitStack() as ctx:
        sem = lambda name: ctx.enter_context(nc.semaphore(name))
        ps = lambda name, dt=F32: ctx.enter_context(nc.psum_tensor(name, [P, 2, 512], dt))

        size = nc.sbuf_usable_end - nc.sbuf_base - 160
        ctx.enter_context(nc.sbuf_tensor("arena", [P, size // 4], F32))
        end = nc.sbuf_base
        cursor = [(end - size // 4 * 4 + 31) // 32 * 32]
        widths = {F32: 4, F32R: 4}

        def put(name, shape, dt, at=None):
            n = widths[dt]
            for k in shape[1:]:
                n *= k
            if at is None:
                at = cursor[0]
                cursor[0] += (n + 31) // 32 * 32
                assert cursor[0] <= end, (name, cursor[0], end)
            return nc.alloc_sbuf_tensor_at(name, shape, dt, offset=at), at

        HTh, ht_at = put("hT_hi", [P, KD, T], F32R)
        HTl, _ = put("hT_lo", [P, KD, T], F32R)
        XR, _ = put("residual", [P, NT, DM], F32)
        YG, yg_at = put("yg", [P, TPG, T], F32)
        YS, ys_at = put("yg_split", [P, 2, 2, 4, P], F32R)
        WOh, wo_at = put("wo_hi", [P, TPG, DM], F32R)
        WOl, _ = put("wo_lo", [P, TPG, DM], F32R)
        raw_h, _ = put("raw_hid", [P, KD, P], F32)
        raw_g, _ = put("raw_gate", [P, KD, P], F32)
        raw_o, _ = put("raw_out", [P, KD, P], F32)
        WTh = put("wt_hid", [P, 2, KD, P], F32R)[0]
        WTg = put("wt_gate", [P, 2, KD, P], F32R)[0]
        hidT, _ = put("hidT", [P, T], F32)
        sg, _ = put("silu_gate", [P, T], F32)
        HC, _ = put("hid_dt", [P, NT, P], F32)
        XD, xd_at = put("hid_dt_decay", [P, NB, NCH - 1, P], F32)
        ST, _ = put("states", [P, NB, NCH - 1, P], F32, at=xd_at)
        CSB, csb_at = put("cs_rows", [P, NT, P], F32)
        LM, lm_at = put("scores", [P, 2, NB, NCH, P], F32)
        WTbc = put("wt_bc", [P, 2, 2, KD, P], F32R, at=lm_at)[0]
        E, _ = put("decay_in", [P, NB, NCH, P], F32)
        CT, _ = put("C_T", [P, T], F32)
        BT, bt_at = put("B_T", [P, T], F32)
        raw_c = put("raw_c", [P, KD, P], F32, at=bt_at)[0]
        raw_b = put("raw_b", [P, KD, P], F32, at=bt_at + DM * 4)[0]
        GM, _ = put("CB_masked", [P, NT, P], F32)
        BTok, _ = put("B_tok", [P, NT, P], F32)
        dtk, _ = put("dt_tok", [P, NT, H], F32)
        dck, _ = put("decay_tok", [P, NT, H], F32)
        ctk, _ = put("cs_tok", [P, NT, H], F32)
        EL, _ = put("chunk_decays", [P, NB, 2, H], F32)
        SQ, _ = put("sum_sq", [P, T], F32)
        YQ, _ = put("yg_squared", [P, T], F32)
        ident, _ = put("ident", [P, P], F32)
        causal, _ = put("causal", [P, P], F32)
        cw, _ = put("conv_w", [P, CT_ALL, TAPS], F32)
        cb, _ = put("conv_b", [P, CT_ALL], F32)
        Dc, _ = put("D_col", [P, TILES], F32)
        gw, _ = put("gnorm_col", [P, TILES], F32)
        dtb, _ = put("dt_bias", [P, 1], F32)
        negA, _ = put("neg_A", [P, 1], F32)
        ones, _ = put("ones", [P, 1], F32)
        half, _ = put("minus_half", [P, NT], F32)
        vs, _ = put("mean_sq", [P, NT], F32)
        rg, _ = put("rms_factor", [P, NT], F32)

        nwB, _ = put("norm_rows", [P, DM], F32, at=csb_at)

        class Mixture:
            def __init__(self, tag, at, size):
                end = at + size
                self.XH, _ = put(f"normed{tag}", [P, NT, DM], F32, at=at); at += NT * DM * 4
                self.TT, _ = put(f"normed_T{tag}", [P, 2, KD, P], F32, at=at); at += 2 * DM * 4
                self.A_raw, _ = put(f"A_raw{tag}", [P, DM], F32, at=at); at += DM * 4
                self.Wr_raw, _ = put(f"Wr_raw{tag}", [FH, DM], F32, at=at); at += DM * 4
                self.B_raw, _ = put(f"B_raw{tag}", [P, KD, FH, FR], F32, at=at); at += DM * 4
                self.AT, _ = put(f"A_T{tag}", [P, KD, HR + FH], F32, at=at); at += KD * (HR + FH) * 4
                assert at <= end

        MX = (Mixture("_first", yg_at, TPG * T * 4), Mixture("_second", ht_at, 2 * KD * T * 4))
        at = lm_at
        BTm, _ = put("B_mix_T", [P, DM], F32, at=at); at += DM * 4
        low, _ = put("low", [P, NT, HR + FH], F32, at=at); at += NT * (HR + FH) * 4
        LS, _ = put("low_scored", [P, NT, HR], F32, at=at); at += NT * HR * 4
        LST, _ = put("low_scored_T", [P, NT, P], F32, at=at); at += NT * P * 4
        brb, _ = put("br_rows", [P, FH], F32, at=at); at += 32
        lg, _ = put("logits", [P, NT, FH], F32, at=at); at += NT * FH * 4
        pe_, _ = put("score_exp", [P, NT, FH], F32, at=at); at += NT * FH * 4
        pw, _ = put("score", [P, NT, FH], F32, at=at); at += NT * FH * 4
        mx, _ = put("row_max", [P, NT], F32, at=at); at += 32
        sm, _ = put("row_sum", [P, NT], F32, at=at); at += 32
        bst, _ = put("bn_st", [P, NT, 6], F32, at=at); at += NT * 24
        bag, _ = put("bn_ag", [P, NT, 2], F32, at=at); at += NT * 8
        rs, _ = put("ln_factor", [P, NT], F32, at=at); at += 32
        rv, _ = put("ln_var", [P, NT], F32, at=at); at += 32
        s2, _ = put("xn_sq", [P, NT], F32, at=at); at += 32
        dtS = [put(f"dt_step{k}", [P, T], F32, at=yg_at + place * T * 4)[0]
               for k, place in enumerate((4, 5, 6, 7, 0, 1, 2))]
        HN, _ = put("mixer_in", [P, NT, DM], F32, at=wo_at)
        at = wo_at
        cwr, _ = put("conv_w_rows", [CT_ALL, P * TAPS], F32, at=at); at += P * TAPS * 4
        cbr, _ = put("conv_b_rows", [CT_ALL, P], F32, at=at); at += P * 4
        gwr, _ = put("gnorm_rows", [TILES, P], F32, at=at); at += P * 4
        Drow, _ = put("D_rows", [P, H], F32, at=at); at += H * 4
        assert at <= wo_at + TPG * DM * 4
        at = wo_at + TPG * DM * 4
        WTd = put("wt_dt", [P, 2, KD, P], F32R, at=at)[0]; at += 2 * DM * 4
        WTf = []
        for k in range(2):
            WTf.append(put(f"wt_bc_first{k}", [P, 2, KD, P], F32R, at=at)[0]); at += 2 * DM * 4
        raw_f = []
        for k in range(2):
            raw_f.append(put(f"raw_bc_first{k}", [P, KD, P], F32, at=at)[0]); at += DM * 4
        assert at <= wo_at + 2 * TPG * DM * 4

        psR, psP, psX, psD = ps("psR"), ps("psP"), ps("psX"), ps("psD")
        BANKS = {"R": psR, "P": psP, "X": psX, "D": psD}

        def family(tag):
            return ({b: [sem(f"{tag}_full_{b}{i}") for i in range(2)] for b in BANKS},
                    {b: [sem(f"{tag}_free_{b}{i}") for i in range(2)] for b in BANKS})

        o_full, o_free = family("once")
        t_full, t_free = o_full, o_free
        l_full, l_free = family("tail")
        PT = {"R": (1, 1), "P": (3, 3), "X": (3, 2), "D": (1, 1)}
        PL = {"R": (1, 2), "P": (2, 2), "X": (1, 1), "D": (5, 5)}
        Y0, XD0, YS0 = 4, 1, 1

        x_in = [sem(f"x_in{i}") for i in range(2)]; nw_in = sem("norm_w_in"); tab_in = sem("tables_in"); ffw_in = sem("ffn_weights_in")
        rawh_in = sem("raw_hid_in"); rawg_in = sem("raw_gate_in"); rawo_in = sem("raw_out_in")
        rawb_in = sem("raw_bc_in"); rawc_in = sem("raw_c_in")
        cs_in = sem("cs_rows_in"); last_in = sem("chunk_decay_in")
        scratch_out = sem("scratch_written"); y_out = sem("result_written")
        ident_ok = sem("identity_made"); const_ok = sem("constants_made"); pool_link = sem("pool_step")
        dve_link = sem("vector_step")
        ln_var = sem("ln_variance"); ln_fac = sem("ln_factor_made")
        xh_ok = sem("normed_made"); smx_in = sem("score_logits_made"); smx_exp = sem("score_exp_made")
        ls_ok = sem("low_scored_made"); xn_sq = sem("xn_squares_summed")
        h_ok = sem("h_made"); xr_ok = sem("residual_and_normed_added"); h_hi = sem("h_hi_made")
        wd_hi = sem("wt_dt_hi_made"); a_exp = sem("A_exp_made"); dt_act = sem("dt_scalar_step")
        cs_ok = sem("running_sums_made"); tok_ok = sem("dt_made")
        wth_hi = sem("wt_hid_hi_made"); wtg_hi = sem("wt_gate_hi_made"); wtb_hi = sem("wt_bc_hi_made")
        wo_hi = sem("wo_hi_made")
        tap_ok = sem("hid_tap_made"); conv_st = sem("hid_conv_step"); hid_ok = sem("hid_made")
        btap_ok = sem("bc_tap_made"); bconv_st = sem("bc_conv_step"); bc_ok = sem("bc_made")
        dif_ok = sem("exponents_made"); e_ok = sem("decay_in_made"); exp_ok = sem("decay_exp_made"); 
        m_ok = [sem(f"scores_made_head{h}") for h in range(2)]
        xd_ok = sem("hid_dt_decay_made"); st_step = sem("state_step")
        dh_ok = sem("D_hid_made")
        pool_y = sem("y_step"); r_ok = sem("rms_factor_made"); sq_zero = sem("sum_sq_cleared")
        ys_hi = sem("ys_hi_made"); ys_ok = sem("ys_made"); ys_used = sem("ys_first_half_used")

        block = ctx.enter_context(nc.Block())

        def every(e, tile, tail):
            def group(g, last):
                tile(TPG * g, 0, g, first=True, end=False, last=False)
                with e.Fori(1, TPG - 1) as s:
                    tile(TPG * g + s, s, g, first=False, end=False, last=False)
                tile(TPG * g + TPG - 1, TPG - 1, g, first=False, end=not last, last=last)
                tail(g, last)

            with e.Fori(0, G - 1) as g:
                group(g, False)
            group(G - 1, True)

        def apart(e):
            e.nop(nofuse=True)

        ONCE = {}
        seen = {(b, i): 0 for b in BANKS for i in range(2)}

        def use(name, b, i):
            ONCE[name] = (b, i, seen[b, i])
            seen[b, i] += 1

        def ffn_weight_uses(f):
            use(f"A{f}", "R", 0); use(f"Wr{f}", "R", 1); use(f"B{f}", "P", 0)

        def ffn_uses(f):
            for k in range(NT):
                use(f"xT{f}{k}", "R", k % 2); use(f"low{f}{k}", "P", k % 2)
            for i in range(2):
                use(f"lsT{f}{i}", "X", i)
            for k in range(NT):
                use(f"ffn{f}{k}", "D", k % 2)

        use("tables", "D", 0); use("WdT", "P", 0); use("bcW0", "P", 1); use("bcW1", "R", 0)
        ffn_weight_uses(0)
        ffn_uses(0)
        use("hW0", "P", 0); use("gW0", "P", 1)
        for k in range(NT):
            use(f"hT{k}", "RX"[k % 4 // 2], k % 2)
        for i in range(2):
            use(f"dt{i}", "P", i); use(f"bc0{i}", "D", i); use(f"bc1{i}", "X", i)
        for i in range(2):
            use(f"h{i}", "P", i)
        use("hW1", "P", 0)
        for i in range(2):
            use(f"dttok{i}", "R", i); use(f"cstok{i}", "D", i); use(f"dctok{i}", "X", i)
        for i in range(2):
            use(f"CB{i}", "D", i); use(f"Bt{i}", "X", i)
        before_loop = dict(seen)
        BASE = {b: [seen[b, i] for i in range(2)] for b in BANKS}
        for b, i in seen:
            seen[b, i] += PT[b][i] * TILES - (2 if b == "P" else 0)
        ffn_weight_uses(1)
        ffn_uses(1)

        def full(e, name):
            b, i, n = ONCE[name]
            e.wait_ge(o_full[b][i], n + 1)

        def free_sem(name):
            b, i, _ = ONCE[name]
            return o_free[b][i]

        def freed(e, name):
            b, i, n = ONCE[name]
            e.wait_ge(o_free[b][i], n + 1)

        def ready(e, name):
            b, i, n = ONCE[name]
            if n:
                e.wait_ge(o_free[b][i], n)

        def bank(name):
            b, i, _ = ONCE[name]
            return BANKS[b][:, i, :]

        @block.sync
        def _(sp):
            def ffn_weights(f):
                m = MX[f]
                sp.dma_start(m.A_raw[:], A_d).then_inc(ffw_in, 16)
                sp.dma_start(m.Wr_raw[:], ffn_Wr).then_inc(ffw_in, 16)
                for a in range(KD):
                    sp.dma_start(m.B_raw[:, a], B_d[:, a]).then_inc(ffw_in, 16)
                sp.dma_start(brb[:], ffn_br.rearrange("(a h) -> a h", a=1).to_broadcast([P, FH])).then_inc(ffw_in, 16)

            def rows(dst, first, s):
                sp.dma_start(dst[:].rearrange("p a d -> p (a d)"),
                             in_proj_w[bass.ds(first, P), :]).then_inc(s, 16)

            def out_cols(t):
                sp.dma_start(raw_o[:], outw_d[:, :, bass.ds(t * P, P)]).then_inc(rawo_in, 16)

            def cs_rows(head):
                sp.dma_start(CSB[:].rearrange("p c i -> p (c i)"), cs_d[bass.ds(head, 1)].to_broadcast([P, T])
                             ).then_inc(cs_in, 16)

            for k in range(0, NT, 2):
                sp.dma_start(XR[:, k:k + 2], x_d[:, k:k + 2]).then_inc(x_in[k // 4], 16)
            rows(raw_g, DT0, rawg_in)
            rows(raw_f[0], B0, rawb_in)
            rows(raw_f[1], C0, rawc_in)
            ffn_weights(0)
            for dst, src in (
                (cwr[:], conv_w.rearrange("(t p) k -> t (p k)", p=P)),
                (cbr[:], conv_b.rearrange("(t p) -> t p", p=P)),
                (gwr[:], gnorm_w.rearrange("(t p) -> t p", p=P)),
                (dtb[:], dt_bias.rearrange("(h a) -> h a", a=1)),
                (negA[:], A_log.rearrange("(h a) -> h a", a=1)),
                (Drow[:], Dp.rearrange("(a h) -> a h", a=1).to_broadcast([P, H])),
            ):
                sp.dma_start(dst, src).then_inc(tab_in, 16)
            sp.dma_start(nwB[:], norm_w.rearrange("(a d) -> a d", a=1).to_broadcast([P, DM])).then_inc(nw_in, 16)
            rows(raw_h, HID0, rawh_in)
            sp.dma_start(raw_o[:], outw_d[:, :, 0:P]).then_inc(rawo_in, 16)
            full(sp, "WdT")
            rows(raw_g, 0, rawg_in)
            full(sp, "hW0")
            rows(raw_h, HID0 + P, rawh_in)
            full(sp, "gW0")
            rows(raw_g, P, rawg_in)
            sp.wait_ge(cs_ok, 1)
            sp.dma_start(cs_d, dtS[4][:]).then_inc(scratch_out, 16)
            sp.wait_ge(dt_act, 5)
            for b in range(NB):
                for c in range(2):
                    k = b * NCH + c + 1
                    sp.dma_start(last_d[2 * b + c].rearrange("(h a) -> h a", a=1),
                                 dtS[6][:, k:k + 1]).then_inc(scratch_out, 16)
            sp.wait_ge(scratch_out, 16 * (1 + 2 * NB))
            sp.wait_ge(h_ok, NT)
            cs_rows(0)
            sp.dma_start(EL[:].rearrange("p b c h -> p (b c h)"),
                         last_d.rearrange("(a k) h -> a (k h)", a=1).to_broadcast([P, 2 * NB * H])).then_inc(last_in, 16)
            full(sp, "hW1")
            rows(raw_h, HID0 + 2 * P, rawh_in)
            full(sp, "CB1")
            full(sp, "Bt1")
            rows(raw_b, B0 + P, rawb_in)
            rows(raw_c, C0 + P, rawc_in)

            def tile(t, s, g, first, end, last):
                def next_head(h):
                    sp.wait_ge(dif_ok, 4 * t + 2 * h + 2)
                    apart(sp)
                    sp.wait_ge(e_ok, 2 * t + h + 1)
                    apart(sp)
                    cs_rows(2 * t + h + 1)

                next_head(0)
                if last:
                    return
                sp.wait_ge(t_full["X"][0], BASE["X"][0] + 3 * t + 1)
                out_cols(t + 1)
                next_head(1)
                sp.wait_ge(t_full["P"][0], BASE["P"][0] + 3 * t + 3)
                rows(raw_h, HID0 + (t + 3) * P, rawh_in)
                sp.wait_ge(t_full["P"][1], BASE["P"][1] + 3 * t + 3)
                rows(raw_g, (t + 2) * P, rawg_in)

            def tail(g, last):
                if last:
                    sp.wait_ge(t_full["X"][1], BASE["X"][1] + PT["X"][1] * TILES)
                    ffn_weights(1)
                    return
                sp.wait_ge(l_full["D"][1], 5 * g + 3)
                apart(sp)
                sp.wait_ge(l_full["X"][1], g + 1)
                rows(raw_b, B0 + (g + 2) * P, rawb_in)
                rows(raw_c, C0 + (g + 2) * P, rawc_in)

            every(sp, tile, tail)
            for k in range(NT):
                freed(sp, f"ffn1{k}")
                sp.dma_start(out_d[:, k], XR[:, k]).then_inc(y_out, 16)
            sp.wait_ge(y_out, 16 * NT)

        @block.tensor
        def _(pe):
            def transposes(name, blocks, out_ap=None):
                ready(pe, name)
                dst = bank(name) if out_ap is None else out_ap
                for k, a in enumerate(blocks):
                    w = a.shape[0]
                    last = pe.transpose(dst[0:a.shape[1], k * w:(k + 1) * w], a, ident[0:w, 0:w])
                b, i, _ = ONCE[name]
                last.then_inc(o_full[b][i], 1)

            def project(dst, wt, b):
                n = 0
                cols = slice(b * S, (b + 1) * S)
                for a in range(KD):
                    for w, h in ((wt[:, 0, a], HTh), (wt[:, 0, a], HTl), (wt[:, 1, a], HTh)):
                        last = pe.matmul(dst, w, h[:, a, cols], start=(n == 0), stop=(n == 3 * KD - 1))
                        n += 1
                return last

            def cb(psum, i):
                for c in range(NCH):
                    k = (i * NCH + c) * P
                    last = pe.matmul(psum[:, c * P:(c + 1) * P], BT[:, k:k + P], CT[:, k:k + P],
                                     start=True, stop=True)
                return last

            def b_tok(psum, i):
                for c in range(NCH):
                    k = (i * NCH + c) * P
                    last = pe.transpose(psum[:, c * P:(c + 1) * P], BT[:, k:k + P], ident[:])
                return last

            def w_blocks(raw):
                return [raw[:, a, :] for a in range(KD)]

            def ffn_weights(f):
                m = MX[f]
                pe.wait_ge(ffw_in, 16 * (3 + KD) * (f + 1))
                transposes(f"A{f}", [m.A_raw[:, a * P:(a + 1) * P] for a in range(KD)])
                transposes(f"Wr{f}", [m.Wr_raw[:, a * P:(a + 1) * P] for a in range(KD)])
                transposes(f"B{f}", [m.B_raw[:, a].rearrange("p h r -> p (h r)") for a in range(KD)])

            def ffn(f):
                m = MX[f]
                for k in range(NT + 1):
                    if k < NT:
                        pe.wait_ge(xh_ok, 2 * NT * f + k + 1)
                        transposes(f"xT{f}{k}", [m.XH[:, k, a * P:(a + 1) * P] for a in range(KD)])
                    if k:
                        j = k - 1
                        freed(pe, f"A{f}")
                        freed(pe, f"Wr{f}")
                        freed(pe, f"xT{f}{j}")
                        ready(pe, f"low{f}{j}")
                        for a in range(KD):
                            last = pe.matmul(bank(f"low{f}{j}")[:, 0:HR + FH], m.TT[:, j % 2, a], m.AT[:, a],
                                             start=(a == 0), stop=(a == KD - 1))
                        last.then_inc(o_full["P"][j % 2], 1)
                for k in range(NT):
                    i = k // 4
                    if k % 4 == 0:
                        pe.wait_ge(ls_ok, 2 * f + i + 1)
                        transposes(f"lsT{f}{i}", [LS[:, 4 * i + c] for c in range(4)])
                        freed(pe, f"B{f}")
                        freed(pe, f"lsT{f}{i}")
                    ready(pe, f"ffn{f}{k}")
                    pe.matmul(bank(f"ffn{f}{k}"), LST[:, k], BTm[:], start=True, stop=True
                              ).then_inc(o_full["D"][k % 2], 1)

            pe.wait_ge(ident_ok, 1)
            pe.wait_ge(rawg_in, 16)
            transposes("WdT", w_blocks(raw_g))
            for q in range(2):
                pe.wait_ge((rawb_in, rawc_in)[q], 16)
                transposes(f"bcW{q}", w_blocks(raw_f[q]))
            pe.wait_ge(tab_in, 16 * 6)
            at = 0
            for rows in [cwr[:, k::TAPS] for k in range(TAPS)] + [cbr[:], gwr[:]]:
                n = rows.shape[0]
                mm = pe.transpose(psD[:, 0, at:at + n], rows, ident[0:n, 0:n])
                at += n
            mm.then_inc(o_full["D"][0], 1)
            ffn_weights(0)
            ffn(0)
            pe.wait_ge(rawh_in, 16)
            transposes("hW0", w_blocks(raw_h))
            pe.wait_ge(rawg_in, 32)
            transposes("gW0", w_blocks(raw_g))
            for k in range(NT):
                pe.wait_ge(h_ok, k + 1)
                transposes(f"hT{k}", [HN[:, k, a * P:(a + 1) * P] for a in range(KD)])

            def first(name, wt, b):
                ready(pe, name)
                i = ONCE[name]
                project(bank(name), wt, b).then_inc(o_full[i[0]][i[1]], 1)

            freed(pe, "WdT")
            freed(pe, "bcW0")
            for b in range(NB):
                for k in range(NCH * b, NCH * (b + 1)):
                    freed(pe, f"hT{k}")
                first(f"dt{b}", WTd, b)
                first(f"bc0{b}", WTf[0], b)
            freed(pe, "bcW1")
            for b in range(NB):
                first(f"bc1{b}", WTf[1], b)
            freed(pe, "hW0")
            for b in range(NB):
                first(f"h{b}", WTh, b)
            pe.wait_ge(rawh_in, 32)
            transposes("hW1", w_blocks(raw_h))
            for name, src, made, n in (("dttok", dtS[2], tok_ok, 1), ("cstok", dtS[4], cs_ok, 1),
                                       ("dctok", dtS[5], dt_act, 4)):
                pe.wait_ge(made, n)
                for i in range(2):
                    transposes(f"{name}{i}", [src[:, (4 * i + c) * P:(4 * i + c + 1) * P] for c in range(4)])
            for i in range(2):
                pe.wait_ge(bc_ok, 4)
                ready(pe, f"CB{i}")
                cb(bank(f"CB{i}"), i).then_inc(o_full["D"][i], 1)
                ready(pe, f"Bt{i}")
                b_tok(bank(f"Bt{i}"), i).then_inc(o_full["X"][i], 1)
            for (b, i), n in before_loop.items():
                pe.wait_ge(o_free[b][i], n)
            pe.wait_ge(const_ok, 1)

            def tile(t, s, g, first, end, last):
                def fill(b, i, k):
                    pe.wait_ge(t_free[b][i], BASE[b][i] + PT[b][i] * t + k)

                for b in range(NB):
                    pe.wait_ge(hid_ok, 2 * t + b + 1)
                    fill("R", b, 0)
                    for c in range(NCH):
                        k = (b * NCH + c) * P
                        mm = pe.transpose(psR[:, b, c * P:(c + 1) * P], hidT[:, k:k + P], ident[:])
                    mm.then_inc(t_full["R"][b], 1)

                def hid_next(b):
                    fill("P", b, 0)
                    if not last:
                        project(psP[:, b], WTh, b).then_inc(t_full["P"][b], 1)

                gk = 0 if last else 1

                def gate(b):
                    fill("P", b, gk)
                    project(psP[:, b], WTg, b).then_inc(t_full["P"][b], 1)

                hid_next(0)
                pe.wait_ge(rawo_in, 16 * (t + 1))
                fill("X", 0, 0)
                for a in range(KD):
                    mm = pe.transpose(psX[:, 0, a * P:(a + 1) * P], raw_o[:, a], ident[:])
                mm.then_inc(t_full["X"][0], 1)
                hid_next(1)
                if last:
                    gate(0)
                    gate(1)
                for b in (1, 0):
                    pe.wait_ge(xd_ok, XD0 + 2 * t + b + 1)
                    fill("X", b, 1 - b)
                    for c in range(NCH - 1):
                        mm = pe.matmul(psX[:, b, c * P:(c + 1) * P], BTok[:, b * NCH + c], XD[:, b, c],
                                       start=True, stop=True)
                    mm.then_inc(t_full["X"][b], 1)
                if not last:
                    gate(0)
                    gate(1)
                for b in range(NB):
                    fill("D", b, 0)
                    for h in range(2):
                        pe.wait_ge(m_ok[h], 2 * t + b + 1)
                    for c in range(NCH):
                        for h in range(2):
                            rows = slice(h * HP, (h + 1) * HP)
                            mm = pe.matmul(psD[rows, b, c * P:(c + 1) * P], HC[:, b * NCH + c, rows],
                                           LM[:, h, b, c], start=True, stop=True)
                    mm.then_inc(t_full["D"][b], 1)
                if not last:
                    for b, raw, arrived in ((0, raw_h, rawh_in), (1, raw_g, rawg_in)):
                        pe.wait_ge(arrived, 16 * (t + 3))
                        fill("P", b, 2)
                        for a in range(KD):
                            mm = pe.transpose(psP[:, b, a * P:(a + 1) * P], raw[:, a], ident[:])
                        mm.then_inc(t_full["P"][b], 1)
                if end:
                    for i, raw, arrived in ((0, raw_b, rawb_in), (1, raw_c, rawc_in)):
                        pe.wait_ge(arrived, 16 * (g + 2))
                        fill("R", i, 1)
                        for a in range(KD):
                            mm = pe.transpose(psR[:, i, a * P:(a + 1) * P], raw[:, a], ident[:])
                        mm.then_inc(l_full["R"][i], 1)
                for b in range(NB):
                    fill("X", b, 2 - b)
                    if b == 0:
                        fill("X", 1, 1)
                    for c in range(NCH - 1):
                        k = (b * NCH + c + 1) * P
                        mm = pe.matmul(psX[:, b, c * P:(c + 1) * P], ST[:, b, c], CT[:, k:k + P],
                                       start=True, stop=True)
                    mm.then_inc(t_full["X"][b], 1)

            def tail(g, last):
                def ended(b, i):
                    pe.wait_ge(t_free[b][i], BASE[b][i] + PT[b][i] * TPG * (g + 1) - (2 if last and b == "P" else 0))

                def d_use(m):
                    return m // 2 + (1 if m >= 4 and not last else 0)

                def share(m, hf):
                    if hf == 0:
                        if m < 2:
                            ended("D", m)
                        else:
                            pe.wait_ge(l_free["D"][m % 2], 5 * g + d_use(m))
                    pe.wait_ge(ys_ok, YS0 + 2 * NT * g + 2 * m + hf + 1)
                    n = 0
                    for j in range(4):
                        kt = 4 * hf + j
                        for y, w in ((YS[:, hf, 0, j], WOh), (YS[:, hf, 0, j], WOl), (YS[:, hf, 1, j], WOh)):
                            mm = pe.matmul(psD[:, m % 2], y, w[:, kt], start=(hf == 0 and n == 0),
                                           stop=(hf == 1 and n == 11))
                            n += 1
                    mm.then_inc(l_full["D"][m % 2] if hf else ys_used, 1)

                def b_or_c(q, b):
                    if q == 0:
                        if b == 0:
                            pe.wait_ge(l_free["R"][0], g + 1)
                        ended("P", b)
                    else:
                        if b == 0:
                            pe.wait_ge(l_free["R"][1], 2 * g + 1)
                        pe.wait_ge(l_free["P"][b], 2 * g + 1)
                    project(psP[:, b], WTbc[:, q], b).then_inc(l_full["P"][b], 1)

                def squares():
                    if last:
                        ended("R", 1)
                    pe.wait_ge(pool_y, Y0 + 4 * TPG * (g + 1))
                    for k in range(NT):
                        mm = pe.matmul(psR[:, 1, k:k + 1], SQ[:, k * P:(k + 1) * P], ones[:], start=True, stop=True)
                    mm.then_inc(l_full["R"][1], 1)

                ended("X", 0)
                share(0, 0)
                if last:
                    share(0, 1)
                    squares()
                else:
                    for b in range(NB):
                        b_or_c(0, b)
                    share(0, 1)
                    b_or_c(1, 0)
                    squares()
                    b_or_c(1, 1)
                for m in range(1, NT):
                    if m == 4 and not last:
                        pe.wait_ge(bc_ok, 4 * (g + 2))
                        pe.wait_ge(l_free["D"][0], 5 * g + 2)
                        cb(psD[:, 0], 0).then_inc(l_full["D"][0], 1)
                        for i in range(2):
                            ended("X", i)
                            b_tok(psX[:, i], i).then_inc(l_full["X"][i], 1)
                        pe.wait_ge(l_free["D"][1], 5 * g + 2)
                        cb(psD[:, 1], 1).then_inc(l_full["D"][1], 1)
                    if m == 4 and last:
                        pe.wait_ge(l_free["R"][1], PL["R"][1] * g + 1)
                        ffn_weights(1)
                    share(m, 0)
                    share(m, 1)
                if not last:
                    for b, i in (("X", 0), ("X", 1), ("P", 0), ("P", 1), ("R", 0), ("R", 1)):
                        pe.wait_ge(l_free[b][i], PL[b][i] * (g + 1))

            every(pe, tile, tail)
            pe.wait_ge(l_free["D"][0], 5 * (G - 1) + 4)
            pe.wait_ge(l_free["D"][1], 5 * (G - 1) + 4)
            ffn(1)

        @block.scalar
        def _(act):
            def tap(dst, src, ct, looped=False):
                if looped:
                    apart(act)
                return act.activation(dst, src, ACT.Identity, scale=cw[:, bass.ds(ct, 1), TAPS - 1],
                                      bias=cb[:, bass.ds(ct, 1)])

            def split_hi(dst, src):
                return act.activation(dst, src, ACT.Copy)

            def flat(w):
                return w.rearrange("p a c -> p (a c)")

            def ffn_weights(f):
                m = MX[f]
                full(act, f"A{f}")
                act.activation(m.AT[:, :, 0:HR], bank(f"A{f}").rearrange("p (a c) -> p a c", a=KD), ACT.Copy
                               ).then_inc(free_sem(f"A{f}"), 1)
                full(act, f"Wr{f}")
                act.activation(m.AT[:, :, HR:], bank(f"Wr{f}")[:, 0:KD * FH].rearrange("p (a c) -> p a c", a=KD),
                               ACT.Copy).then_inc(free_sem(f"Wr{f}"), 1)
                full(act, f"B{f}")
                act.activation(BTm[:], bank(f"B{f}"), ACT.Copy).then_inc(free_sem(f"B{f}"), 1)

            def ffn(f):
                def score_exp(i):
                    act.wait_ge(smx_in, 2 * f + i + 1)
                    act.activation(pe_[:, 4 * i:4 * i + 4], lg[:, 4 * i:4 * i + 4], ACT.Exp).then_inc(smx_exp, 1)

                for k in range(NT):
                    full(act, f"xT{f}{k}")
                    if k >= 2:
                        full(act, f"low{f}{k - 2}")
                    act.activation(flat(MX[f].TT[:, k % 2]), bank(f"xT{f}{k}"), ACT.Copy
                                   ).then_inc(free_sem(f"xT{f}{k}"), 1)
                    if k == 5:
                        score_exp(0)
                score_exp(1)
                for i in range(2):
                    full(act, f"lsT{f}{i}")
                    act.activation(flat(LST[:, 4 * i:4 * i + 4]), bank(f"lsT{f}{i}"),
                                   ACT.Copy).then_inc(free_sem(f"lsT{f}{i}"), 1)

            def hi(name, wt, made):
                full(act, name)
                act.activation(flat(wt[:, 0]), bank(name), ACT.Copy).then_inc(made, 1)

            hi("WdT", WTd, wd_hi)
            for q in range(2):
                hi(f"bcW{q}", WTf[q], wtb_hi)
            ffn_weights(0)
            ffn(0)
            hi("hW0", WTh, wth_hi)
            hi("gW0", WTg, wtg_hi)
            for k in range(NT):
                act.wait_ge(xh_ok, NT + k + 1)
                full(act, f"ffn0{NT - 1 - (k + 1) % 2}")
                if k >= 2:
                    act.wait_ge(xn_sq, k - 1)
                act.activation(flat(LST[:, 4 * (k % 2):4 * (k % 2) + 4]), MX[0].XH[:, k], ACT.Square,
                               accum_out=s2[:, k:k + 1]).then_inc(xn_sq, 1)
            for k in range(NT):
                full(act, f"hT{k}")
                act.activation(HTh[:, :, k * P:(k + 1) * P], bank(f"hT{k}").rearrange("p (a c) -> p a c", a=KD),
                               ACT.Copy).then_inc(h_hi, 1)
            act.wait_ge(tab_in, 16 * 6)
            freed(act, "tables")
            act.activation(negA[:], negA[:], ACT.Exp).then_inc(a_exp, 1)

            def bc_taps(q, b, src, ct, looped):
                dst = (BT, CT)[q]
                tap(dst[:, b * S:(b + 1) * S], src, ct, looped).then_inc(btap_ok, 1)

            def bc_silu(q, b):
                dst = (BT, CT)[q][:, b * S:(b + 1) * S]
                act.activation(dst, dst, ACT.Silu).then_inc(bc_ok, 1)

            def first_taps(q, b):
                full(act, f"bc{q}{b}")
                bc_taps(q, b, bank(f"bc{q}{b}"), TILES + G * q, False)

            first_taps(0, 0)
            for b in range(NB):
                freed(act, f"dt{b}")
            act.activation(dtS[1][:], dtS[0][:], ACT.Abs).then_inc(dt_act, 1)
            act.wait_ge(dt_act, 1)
            act.activation(dtS[3][:], dtS[1][:], ACT.Exp, scale=-1.0).then_inc(dt_act, 1)
            act.wait_ge(dt_act, 2)
            act.wait_ge(xr_ok, NT)
            act.activation(dtS[4][:], dtS[3][:], ACT.Ln, bias=1.0).then_inc(dt_act, 1)
            first_taps(0, 1)
            for b in range(NB):
                first_taps(1, b)
            act.wait_ge(cs_ok, 1)
            for k in range(NT):
                e = act.activation(dtS[5][:, k * P:(k + 1) * P], dtS[4][:, k * P:(k + 1) * P], ACT.Exp,
                                   scale=-1.0, bias=dtS[4][:, (k + 1) * P - 1:(k + 1) * P])
            e.then_inc(dt_act, 1)
            act.activation(dtS[6][:, 0:NT], dtS[4][:, P - 1::P], ACT.Exp).then_inc(dt_act, 1)
            for b in range(NB):
                full(act, f"h{b}")
                tap(hidT[:, b * S:(b + 1) * S], bank(f"h{b}"), 0).then_inc(tap_ok, 1)
            hi("hW1", WTh, wth_hi)
            for q in range(2):
                for b in range(NB):
                    freed(act, f"bc{q}{b}")
                    bc_silu(q, b)
            for b in range(NB):
                freed(act, f"h{b}")
                act.activation(hidT[:, b * S:(b + 1) * S], hidT[:, b * S:(b + 1) * S], ACT.Silu).then_inc(hid_ok, 1)
            act.wait_ge(last_in, 16)
            act.wait_ge(scratch_out, 16 * (1 + 2 * NB))
            freed(act, "dttok1")
            freed(act, "cstok1")
            freed(act, "dctok1")

            def share_hi(g, m, hf, last):
                if m and hf == 0:
                    act.wait_ge(ys_used, NT * g + m)
                if m and hf == 1:
                    k = (m - 1) // 2 + (1 if m - 1 >= 4 and not last else 0)
                    act.wait_ge(l_full["D"][(m - 1) % 2], 5 * g + k + 1)
                act.activation(YS[:, hf, 0], YG[:, 4 * hf:4 * hf + 4, m * P:(m + 1) * P], ACT.Copy
                               ).then_inc(ys_hi, 1)

            def tile(t, s, g, first, end, last):
                act.wait_ge(hid_ok, 2 * t + 2)
                act.wait_ge(ys_ok, YS0 + 2 * NT * g)
                apart(act)
                act.activation(YG[:, bass.ds(s, 1), :].rearrange("p a t -> p (a t)"), hidT[:], ACT.Copy,
                               scale=Dc[:, bass.ds(t, 1)]).then_inc(dh_ok, 1)

                def tap_next(b):
                    if not last:
                        act.wait_ge(dh_ok, t + 1)
                        act.wait_ge(t_full["R"][b], BASE["R"][b] + t + 1)
                        act.wait_ge(t_full["P"][b], BASE["P"][b] + 3 * t + 1)
                        tap(hidT[:, b * S:(b + 1) * S], psP[:, b], t + 1, True).then_inc(tap_ok, 1)

                def decay_exp(h, b):
                    act.wait_ge(dif_ok, 4 * t + 2 * h + b + 1)
                    act.activation(flat(LM[:, h, b]), flat(LM[:, h, b]), ACT.Exp).then_inc(exp_ok, 1)

                def decay_in(h):
                    act.wait_ge(cs_in, 16 * (2 * t + h + 1))
                    act.wait_ge(pool_y, Y0 + 4 * t - 3)
                    rows = slice(h * HP, (h + 1) * HP)
                    cs = CSB[rows].rearrange("p (b c) i -> p b c i", b=NB)
                    act.activation(E[rows, :, 1:NCH], cs[:, :, 1:NCH], ACT.Exp).then_inc(e_ok, 1)

                gk = 0 if last else 1

                def gate(b):
                    act.wait_ge(t_full["P"][b], BASE["P"][b] + 3 * t + gk + 1)
                    act.activation(sg[:, b * S:(b + 1) * S], psP[:, b], ACT.Silu).then_inc(t_free["P"][b], 1)

                decay_exp(0, 0)
                tap_next(0)
                act.wait_ge(t_full["X"][0], BASE["X"][0] + 3 * t + 1)
                apart(act)
                act.activation(WOh[:, bass.ds(s, 1), :].rearrange("p a t -> p (a t)"), psX[:, 0], ACT.Copy,
                               scale=gw[:, bass.ds(t, 1)]).then_inc(wo_hi, 1)
                decay_in(0)
                tap_next(1)
                decay_exp(0, 1)
                decay_in(1)
                decay_exp(1, 0)
                decay_exp(1, 1)
                if end or last:
                    share_hi(g, 0, 0, last)
                act.wait_ge(pool_y, Y0 + 4 * t - 2)
                gate(0)
                gate(1)
                if not last:
                    for b in range(NB):
                        act.wait_ge(t_free["P"][b], BASE["P"][b] + 3 * t + 1)
                        act.activation(hidT[:, b * S:(b + 1) * S], hidT[:, b * S:(b + 1) * S], ACT.Silu
                                       ).then_inc(hid_ok, 1)
                if not last:
                    act.wait_ge(t_full["P"][0], BASE["P"][0] + 3 * t + 3)
                    act.activation(flat(WTh[:, 0]), psP[:, 0], ACT.Copy).then_inc(wth_hi, 1)
                    act.wait_ge(t_full["P"][1], BASE["P"][1] + 3 * t + 3)
                    act.activation(flat(WTg[:, 0]), psP[:, 1], ACT.Copy).then_inc(wtg_hi, 1)

            def tail(g, last):
                def taps(q, b):
                    act.wait_ge(l_full["P"][b], 2 * g + q + 1)
                    bc_taps(q, b, psP[:, b], TILES + G * q + g + 1, True)

                def silus(q):
                    for b in range(NB):
                        act.wait_ge(l_free["P"][b], 2 * g + q + 1)
                        bc_silu(q, b)

                if not last:
                    act.wait_ge(t_full["D"][1], BASE["D"][1] + TPG * (g + 1))
                    for i in range(2):
                        act.wait_ge(l_full["R"][i], PL["R"][i] * g + 1)
                        act.activation(flat(WTbc[:, i, 0]), psR[:, i], ACT.Copy).then_inc(wtb_hi, 1)
                act.wait_ge(pool_y, Y0 + 4 * TPG * (g + 1) - 2)
                share_hi(g, 0, 1, last)
                if not last:
                    taps(0, 0)
                share_hi(g, 1, 0, last)
                if not last:
                    taps(0, 1)
                    act.wait_ge(t_full["X"][1], BASE["X"][1] + 2 * TPG * (g + 1))
                    taps(1, 0)
                share_hi(g, 1, 1, last)
                if not last:
                    taps(1, 1)
                if not last:
                    silus(0)
                    silus(1)
                for m in range(2, NT):
                    share_hi(g, m, 0, last)
                    share_hi(g, m, 1, last)
                    if m == 4 and last:
                        ffn_weights(1)

            every(act, tile, tail)
            ffn(1)

        @block.vector
        def _(dve):
            steps = [0]

            def link(ins):
                steps[0] += 1
                ins.then_inc(dve_link, 1)
                dve.wait_ge(dve_link, steps[0])

            def stats(k):
                return dve.bn_stats(bst[:, k], XR[:, k])

            def variance(i):
                h4 = slice(4 * i, 4 * i + 4)
                for k in range(4 * i, 4 * i + 4):
                    last = dve.bn_aggr(bag[:, k], bst[:, k])
                link(last)
                dve.tensor_scalar(rv[:, h4], bag[:, h4, 1], LN_EPS, None, ALU.add).then_inc(ln_var, 1)

            def normed(n, i):
                dve.wait_ge(ln_fac, (0, 2, 6)[n] + i + 1)
                for k in range(4 * i, 4 * i + 4):
                    dve.tensor_scalar(MX[n // 2].XH[:, k], XR[:, k], bag[:, k, 0:1], rs[:, k:k + 1], ALU.subtract,
                                      ALU.mult).then_inc(xh_ok, 1)

            def ffn(f):
                def low_out(k):
                    full(dve, f"low{f}{k}")
                    dve.tensor_copy(low[:, k], bank(f"low{f}{k}")[:, 0:HR + FH]).then_inc(free_sem(f"low{f}{k}"), 1)

                def logits(i):
                    h4 = slice(4 * i, 4 * i + 4)
                    for k in (4 * i + 2, 4 * i + 3):
                        freed(dve, f"low{f}{k}")
                    dve.wait_ge(ffw_in, 16 * (3 + KD) * (f + 1))
                    link(dve.tensor_tensor(lg[:, h4], low[:, h4, HR:], brb[:].unsqueeze(1).to_broadcast([P, 4, FH]),
                                           ALU.add))
                    link(dve.tensor_reduce(mx[:, h4], lg[:, h4], AX.X, ALU.max))
                    dve.tensor_tensor(lg[:, h4], lg[:, h4], mx[:, h4].unsqueeze(2).to_broadcast([P, 4, FH]),
                                      ALU.subtract).then_inc(smx_in, 1)

                def scored(i):
                    h4 = slice(4 * i, 4 * i + 4)
                    dve.wait_ge(smx_exp, 2 * f + i + 1)
                    link(dve.tensor_reduce(sm[:, h4], pe_[:, h4], AX.X, ALU.add))
                    link(dve.reciprocal(mx[:, h4], sm[:, h4]))
                    link(dve.scalar_tensor_tensor(out=pw[:, h4], in0=pe_[:, h4], scalar=FFN_SCALE,
                                                  in1=mx[:, h4].unsqueeze(2).to_broadcast([P, 4, FH]),
                                                  op0=ALU.mult, op1=ALU.mult))
                    for k in range(4 * i, 4 * i + 4):
                        last = dve.tensor_tensor(LS[:, k].rearrange("p (h r) -> p h r", h=FH),
                                                 low[:, k, 0:HR].rearrange("p (h r) -> p h r", h=FH),
                                                 pw[:, k].unsqueeze(2).to_broadcast([P, FH, FR]), ALU.mult)
                    last.then_inc(ls_ok, 1)

                for k in range(6):
                    low_out(k)
                    if k == 3:
                        logits(0)
                scored(0)
                low_out(6)
                low_out(7)
                logits(1)
                scored(1)
                for k in range(NT + 1):
                    if k < NT:
                        full(dve, f"ffn{f}{k}")
                        dve.tensor_tensor(XR[:, k], XR[:, k], bank(f"ffn{f}{k}"), ALU.add
                                          ).then_inc(free_sem(f"ffn{f}{k}"), 1)
                    if k and f == 0:
                        freed(dve, f"ffn{f}{k - 1}")
                        last = stats(k - 1)
                        if k % 4 == 0:
                            link(last)
                            variance(k // 4 - 1)

            def conv_tap(step, n, dst, src, ct, done, d):
                if d > 1:
                    dve.wait_ge(step, n + d - 1)
                dve.scalar_tensor_tensor(out=dst[:, d:S], in0=src[:, 0:S - d],
                                         scalar=cw[:, bass.ds(ct, 1), TAPS - 1 - d], in1=dst[:, d:S],
                                         op0=ALU.mult, op1=ALU.add
                                         ).then_inc(done if d == TAPS - 1 else step, 1)

            def conv(step, n, dst, src, ct, done):
                for d in range(1, TAPS):
                    conv_tap(step, n, dst, src, ct, done, d)

            def split_lo(dst, src, hi, done):
                dve.tensor_tensor(dst.rearrange("p a c -> p (a c)"), src,
                                  hi.rearrange("p a c -> p (a c)").bitcast(F32), ALU.subtract).then_inc(done, 1)

            dve.memset(mx[:], 0.0).then_inc(ys_ok, 1)
            for i in range(2):
                dve.wait_ge(x_in[i], 32)
                for k in range(4 * i, 4 * i + 4):
                    last = stats(k)
                link(last)
                variance(i)

            def lo(name, wt, made, n):
                full(dve, name)
                dve.wait_ge(made, n)
                split_lo(wt[:, 1], bank(name), wt[:, 0], free_sem(name))

            lo("WdT", WTd, wd_hi, 1)
            for q in range(2):
                lo(f"bcW{q}", WTf[q], wtb_hi, q + 1)
            for i in range(2):
                normed(0, i)
            full(dve, "tables")
            n = TAPS * CT_ALL
            dve.tensor_copy(cw[:].rearrange("p t k -> p k t"), bank("tables")[:, 0:n].rearrange("p (k t) -> p k t", k=TAPS))
            for dst in (cb, gw):
                last = dve.tensor_copy(dst[:], bank("tables")[:, n:n + dst.shape[1]])
                n += dst.shape[1]
            for h in range(2):
                last = dve.tensor_copy(Dc[h * HP:(h + 1) * HP, :], Drow[h * HP:(h + 1) * HP, h::2])
            last.then_inc(free_sem("tables"), 1)
            ffn(0)
            lo("hW0", WTh, wth_hi, 1)
            for i in range(2):
                normed(1, i)
            lo("gW0", WTg, wtg_hi, 1)
            for i in range(2):
                h4 = slice(4 * i, 4 * i + 4)
                dve.wait_ge(xn_sq, 4 * i + 4)
                dve.tensor_scalar(rv[:, h4], s2[:, h4], 1.0 / DM, RMS_EPS, ALU.mult, ALU.add).then_inc(ln_var, 1)
            dve.wait_ge(nw_in, 16)
            freed(dve, "tables")
            for k in range(NT + 2):
                if k < NT:
                    dve.wait_ge(ln_fac, 5 + k // 4)
                    dve.wait_ge(xh_ok, 2 * NT)
                    dve.scalar_tensor_tensor(out=HN[:, k], in0=MX[0].XH[:, k], scalar=rs[:, k:k + 1], in1=nwB[:],
                                             op0=ALU.mult, op1=ALU.mult).then_inc(h_ok, 1)
                if k >= 2:
                    j = k - 2
                    dve.wait_ge(h_hi, j + 1)
                    full(dve, f"hT{j}")
                    dve.tensor_tensor(HTl[:, :, j * P:(j + 1) * P], bank(f"hT{j}").rearrange("p (a c) -> p a c", a=KD),
                                      HTh[:, :, j * P:(j + 1) * P].bitcast(F32), ALU.subtract
                                      ).then_inc(free_sem(f"hT{j}"), 1)

            def dt_biased(b):
                full(dve, f"dt{b}")
                dve.tensor_scalar(dtS[0][:, b * S:(b + 1) * S], bank(f"dt{b}"), dtb[:], None, ALU.add
                                  ).then_inc(free_sem(f"dt{b}"), 1)

            def bc_conv_first(q, b):
                dve.wait_ge(btap_ok, 2 * q + b + 1)
                conv(bconv_st, 2 * (2 * q + b), (BT, CT)[q][:, b * S:(b + 1) * S], bank(f"bc{q}{b}"),
                     TILES + G * q, free_sem(f"bc{q}{b}"))

            dve.wait_ge(tab_in, 16 * 6)
            dt_biased(0)
            bc_conv_first(0, 0)
            dt_biased(1)
            dve.wait_ge(dt_act, 3)
            dve.wait_ge(a_exp, 1)
            link(dve.tensor_scalar(negA[:], negA[:], -1.0, None, ALU.mult))
            for b in range(NB):
                freed(dve, f"dt{b}")
            dve.scalar_tensor_tensor(out=dtS[2][:], in0=dtS[0][:], scalar=0.0, in1=dtS[4][:], op0=ALU.max,
                                     op1=ALU.add).then_inc(tok_ok, 1)
            dve.wait_ge(tok_ok, 1)
            link(dve.tensor_scalar(dtS[1][:], dtS[2][:], negA[:], EXP_FLOOR, ALU.mult, ALU.max))
            link(dve.memset(dtS[3][:], 1.0))
            link(dve.memset(dtS[3][:, 0::P], 0.0))
            dve.tensor_tensor_scan(dtS[4][:], dtS[3][:], dtS[1][:], 0.0, ALU.mult, ALU.add).then_inc(cs_ok, 1)
            for q, b in ((0, 1), (1, 0), (1, 1)):
                bc_conv_first(q, b)
            for b in range(NB):
                dve.wait_ge(tap_ok, b + 1)
                conv(conv_st, 2 * b, hidT[:, b * S:(b + 1) * S], bank(f"h{b}"), 0, free_sem(f"h{b}"))
            lo("hW1", WTh, wth_hi, 2)
            for name, dst in (("dttok", dtk), ("cstok", ctk), ("dctok", dck)):
                for i in range(2):
                    full(dve, f"{name}{i}")
                    dve.tensor_copy(dst[:, 4 * i:4 * i + 4], bank(f"{name}{i}").rearrange("p (c h) -> p c h", c=4)
                                    ).then_inc(free_sem(f"{name}{i}"), 1)

            def mask_cb(psum, i, done):
                dve.tensor_tensor(GM[:, 4 * i:4 * i + 4], psum.rearrange("p (c i) -> p c i", c=NCH),
                                  causal[:].unsqueeze(1).to_broadcast([P, NCH, P]), ALU.mult).then_inc(done, 1)

            def copy_b(psum, i, done):
                dve.tensor_copy(BTok[:, 4 * i:4 * i + 4], psum.rearrange("p (c i) -> p c i", c=NCH)
                                ).then_inc(done, 1)

            dve.wait_ge(const_ok, 1)
            for i in range(2):
                full(dve, f"CB{i}")
                mask_cb(bank(f"CB{i}"), i, free_sem(f"CB{i}"))
                full(dve, f"Bt{i}")
                copy_b(bank(f"Bt{i}"), i, free_sem(f"Bt{i}"))
            dve.wait_ge(last_in, 16)
            dve.wait_ge(xr_ok, NT)

            def share_lo(g, m, hf):
                dve.wait_ge(ys_hi, 2 * NT * g + 2 * m + hf + 1)
                dve.tensor_tensor(YS[:, hf, 1], YG[:, 4 * hf:4 * hf + 4, m * P:(m + 1) * P],
                                  YS[:, hf, 0].bitcast(F32), ALU.subtract).then_inc(ys_ok, 1)

            def tile(t, s, g, first, end, last):
                def exponents(h, b, chunks=range(NCH)):
                    if b == 0:
                        dve.wait_ge(cs_in, 16 * (2 * t + h + 1))
                    for c in chunks:
                        k = b * NCH + c
                        last_i = dve.tensor_scalar(LM[:, h, b, c], CSB[:, k], ctk[:, k, bass.ds(2 * t + h, 1)], 0.0,
                                                   ALU.subtract, ALU.min)
                    if c == NCH - 1:
                        last_i.then_inc(dif_ok, 1)

                def conv_next(b, d):
                    if not last:
                        if d == 1:
                            dve.wait_ge(tap_ok, 2 * t + b + 3)
                        conv_tap(conv_st, 4 * t + 4 + 2 * b, hidT[:, b * S:(b + 1) * S], psP[:, b], t + 1,
                                 t_free["P"][b], d)

                def score(b):
                    dve.wait_ge(exp_ok, 4 * t + b + 3)
                    dve.tensor_tensor(LM[:, 1, b], LM[:, 1, b], GM[:, b * NCH:(b + 1) * NCH], ALU.mult
                                      ).then_inc(m_ok[1], 1)

                for b in range(NB):
                    dve.wait_ge(t_full["D"][b], BASE["D"][b] + t)
                exponents(0, 0)
                by_head = lambda a: a.rearrange("p c (h q) -> p c h q", h=2)
                dve.wait_ge(xd_ok, XD0 + 2 * t)
                for b in range(NB):
                    dve.wait_ge(t_full["R"][b], BASE["R"][b] + t + 1)
                    ch = slice(b * NCH, (b + 1) * NCH)
                    dve.tensor_tensor(by_head(HC[:, ch]), by_head(psR[:, b].rearrange("p (c i) -> p c i", c=NCH)),
                                      dtk[:, ch, bass.ds(2 * t, 2)].unsqueeze(3).to_broadcast([P, NCH, 2, HP]),
                                      ALU.mult).then_inc(t_free["R"][b], 1)
                exponents(0, 1, range(NCH - 1))
                conv_next(0, 1)
                dve.wait_ge(wo_hi, t + 1)
                dve.scalar_tensor_tensor(out=WOl[:, bass.ds(s, 1), :].rearrange("p a t -> p (a t)"), in0=psX[:, 0],
                                         scalar=gw[:, bass.ds(t, 1)],
                                         in1=WOh[:, bass.ds(s, 1), :].rearrange("p a t -> p (a t)").bitcast(F32),
                                         op0=ALU.mult, op1=ALU.subtract).then_inc(t_free["X"][0], 1)
                conv_next(0, 2)
                exponents(0, 1, [NCH - 1])
                conv_next(0, 3)
                halves = lambda a: a.rearrange("p b (h q) -> p b h q", h=2)

                def decayed(c):
                    dve.wait_ge(st_step, 4 * t + 2 * c - 1)
                    dve.tensor_tensor(halves(ST[:, :, c]), halves(ST[:, :, c - 1]),
                                      EL[:, :, c - 1, bass.ds(2 * t, 2)].unsqueeze(3).to_broadcast([P, NB, 2, HP]),
                                      ALU.mult).then_inc(st_step, 1)

                conv_next(1, 1)
                dve.wait_ge(t_full["X"][0], BASE["X"][0] + 3 * t + 2)
                dve.wait_ge(t_full["X"][1], BASE["X"][1] + 2 * t + 1)
                dve.tensor_copy(ST[:, :, 0], psX[:, :, 0:P]).then_inc(st_step, 1)
                conv_next(1, 2)
                decayed(1)
                conv_next(1, 3)
                exponents(1, 0)
                exponents(1, 1)
                score(0)
                dve.wait_ge(st_step, 4 * t + 2)
                dve.tensor_tensor(ST[:, :, 1], ST[:, :, 1], psX[:, :, P:2 * P], ALU.add).then_inc(st_step, 1)
                score(1)
                decayed(2)
                dve.wait_ge(st_step, 4 * t + 4)
                for b in range(NB):
                    dve.tensor_tensor(ST[:, b, 2], ST[:, b, 2], psX[:, b, 2 * P:3 * P], ALU.add
                                      ).then_inc(t_free["X"][b], 1)
                if end or last:
                    share_lo(g, 0, 0)
                dve.wait_ge(dh_ok, t + 1)
                for b in range(NB):
                    dve.wait_ge(t_full["D"][b], BASE["D"][b] + t + 1)
                    y = YG[:, bass.ds(s, 1), b * S:(b + 1) * S].rearrange("p a t -> p (a t)")
                    dve.tensor_tensor(y, y, psD[:, b], ALU.add).then_inc(t_free["D"][b], 1)
                if not last:
                    for w, made, n, b in ((WTh, wth_hi, t + 3, 0), (WTg, wtg_hi, t + 2, 1)):
                        dve.wait_ge(made, n)
                        split_lo(w[:, 1], psP[:, b], w[:, 0], t_free["P"][b])
                for b in range(NB):
                    dve.wait_ge(t_full["X"][b], BASE["X"][b] + PT["X"][b] * t + 3 - b)
                    dve.wait_ge(e_ok, 2 * t + 2)
                    dve.tensor_tensor(E[:, b, 1:NCH], E[:, b, 1:NCH],
                                      psX[:, b, 0:(NCH - 1) * P].rearrange("p (c i) -> p c i", c=NCH - 1), ALU.mult
                                      ).then_inc(t_free["X"][b], 1)

            def tail(g, last):
                def bc_conv(q, b):
                    dve.wait_ge(btap_ok, 4 * (g + 1) + 2 * q + b + 1)
                    for d in range(1, TAPS):
                        conv_tap(bconv_st, 8 * (g + 1) + 2 * (2 * q + b), (BT, CT)[q][:, b * S:(b + 1) * S],
                                 psP[:, b], TILES + G * q + g + 1, l_free["P"][b], d)

                def mean_squares():
                    k = PL["R"][1] * g + (1 if last else 2)
                    dve.wait_ge(l_full["R"][1], k)
                    dve.tensor_scalar(vs[:], psR[:, 1, 0:NT], float(G) / DI, RMS_EPS, ALU.mult, ALU.add
                                      ).then_inc(l_free["R"][1], 1)

                def add(m):
                    k = m // 2 + (1 if m >= 4 and not last else 0)
                    dve.wait_ge(l_full["D"][m % 2], 5 * g + k + 1)
                    dve.scalar_tensor_tensor(out=XR[:, m], in0=psD[:, m % 2], scalar=rg[:, m:m + 1], in1=XR[:, m],
                                             op0=ALU.mult, op1=ALU.add).then_inc(l_free["D"][m % 2], 1)

                def added(m):
                    dve.wait_ge(l_free["D"][m % 2], 5 * g + m // 2 + 1)

                if not last:
                    for q in range(2):
                        dve.wait_ge(wtb_hi, 2 * g + q + 3)
                        split_lo(WTbc[:, q, 1], psR[:, q], WTbc[:, q, 0], l_free["R"][q])
                share_lo(g, 0, 1)
                if not last:
                    bc_conv(0, 0)
                share_lo(g, 1, 0)
                if not last:
                    bc_conv(0, 1)
                    bc_conv(1, 0)
                share_lo(g, 1, 1)
                mean_squares()
                if not last:
                    bc_conv(1, 1)
                dve.wait_ge(r_ok, g + 1)
                add(0)
                for m in range(2, NT):
                    share_lo(g, m, 0)
                    add(m - 1)
                    share_lo(g, m, 1)
                    if last:
                        added(m - 2)
                        stat = stats(m - 2)
                        if m == 5:
                            link(stat)
                            variance(0)
                        if m == 6:
                            normed(2, 0)
                    if m == 4 and not last:
                        dve.wait_ge(l_full["D"][0], 5 * g + 3)
                        mask_cb(psD[:, 0], 0, l_free["D"][0])
                        for i in range(2):
                            dve.wait_ge(l_full["X"][i], g + 1)
                            copy_b(psX[:, i], i, l_free["X"][i])
                        dve.wait_ge(l_full["D"][1], 5 * g + 3)
                        mask_cb(psD[:, 1], 1, l_free["D"][1])
                add(NT - 1)
                if last:
                    for m in (NT - 2, NT - 1):
                        added(m)
                        stat = stats(m)
                    link(stat)
                    variance(1)
                    normed(2, 1)

            every(dve, tile, tail)
            ffn(1)

        @block.gpsimd
        def _(pool):
            steps = [0]

            def link(ins):
                steps[0] += 1
                ins.then_inc(pool_link, 1)
                pool.wait_ge(pool_link, steps[0])

            link(pool.memset(ident[:], 0.0))
            pool.affine_select(out=ident[:], in_=ident[:], compare_op=ALU.not_equal, fill=1.0, base=0,
                               pattern=[[-1, P]], channel_multiplier=1).then_inc(ident_ok, 1)
            link(pool.memset(half[:], -0.5))

            def inv_sqrt(dst, src, n, var, made):
                pool.wait_ge(var, n)
                pool.tensor_tensor(dst, src, half[:, 0:dst.shape[1]], ALU.pow).then_inc(made, 1)

            def ln_factor(n):
                h4 = slice(4 * (n % 2), 4 * (n % 2) + 4)
                inv_sqrt(rs[:, h4], rv[:, h4], n + 1, ln_var, ln_fac)

            ln_factor(0)
            ln_factor(1)
            pool.memset(ones[:], 1.0)
            link(pool.memset(causal[:], 1.0))
            link(pool.affine_select(out=causal[:], in_=causal[:], compare_op=ALU.is_ge, fill=0.0, base=0,
                                    pattern=[[1, P]], channel_multiplier=-1))
            pool.memset(SQ[:], 0.0).then_inc(sq_zero, 1)
            pool.wait_ge(sq_zero, 1)
            for k in range(Y0):
                pool.memset(rg[:, k:k + 1], 1.0).then_inc(pool_y, 1)
            pool.memset(rg[:, Y0:Y0 + 1], 1.0).then_inc(xd_ok, 1)
            pool.memset(vs[:], 1.0).then_inc(const_ok, 1)
            for n in range(2, 6):
                ln_factor(n)
            pool.wait_ge(xh_ok, 2 * NT)
            for k in range(NT):
                pool.tensor_tensor(XR[:, k], XR[:, k], MX[0].XH[:, k], ALU.add).then_inc(xr_ok, 1)

            def state_part(t, s):
                y4 = YG[:, bass.ds(s, 1), :].rearrange("p a (b c i) -> p (a b) c i", b=NB, c=NCH)
                for b in range(NB):
                    pool.wait_ge(t_free["X"][b], BASE["X"][b] + PT["X"][b] * (t + 1))
                    pool.wait_ge(t_free["D"][b], BASE["D"][b] + t + 1)
                apart(pool)
                pool.tensor_tensor(y4[:, :, 1:NCH], y4[:, :, 1:NCH], E[:, :, 1:NCH], ALU.add).then_inc(pool_y, 1)

            def gated(t, s, last):
                y = YG[:, bass.ds(s, 1), :].rearrange("p a t -> p (a t)")
                for b in range(NB):
                    pool.wait_ge(t_free["P"][b], BASE["P"][b] + 3 * t + (1 if last else 2))
                pool.wait_ge(pool_y, Y0 + 4 * t + 1)
                apart(pool)
                pool.tensor_tensor(y, y, sg[:], ALU.mult).then_inc(pool_y, 1)

            def squared(t, s, g):
                y = YG[:, bass.ds(s, 1), :].rearrange("p a t -> p (a t)")
                pool.wait_ge(pool_y, Y0 + 4 * t + 2)
                apart(pool)
                pool.tensor_tensor(YQ[:], y, y, ALU.mult).then_inc(pool_y, 1)
                pool.wait_ge(pool_y, Y0 + 4 * t + 3)
                pool.wait_ge(sq_zero, g + 1)
                pool.tensor_tensor(SQ[:], SQ[:], YQ[:], ALU.add).then_inc(pool_y, 1)

            def tile(t, s, g, first, end, last):
                if not first:
                    state_part(t - 1, s - 1)
                for b in range(NB):
                    pool.wait_ge(t_full["X"][b], BASE["X"][b] + PT["X"][b] * t)
                    pool.wait_ge(t_free["R"][b], BASE["R"][b] + t + 1)
                    apart(pool)
                    ch = slice(b * NCH, b * NCH + NCH - 1)
                    by_head = lambda a: a.rearrange("p c (h q) -> p c h q", h=2)
                    pool.tensor_tensor(by_head(XD[:, b]), by_head(HC[:, ch]),
                                       dck[:, ch, bass.ds(2 * t, 2)].unsqueeze(3).to_broadcast([P, NCH - 1, 2, HP]),
                                       ALU.mult).then_inc(xd_ok, 1)
                if not first:
                    gated(t - 1, s - 1, False)
                for b in range(NB):
                    pool.wait_ge(exp_ok, 4 * t + b + 1)
                    apart(pool)
                    pool.tensor_tensor(LM[:, 0, b], LM[:, 0, b], GM[:, b * NCH:(b + 1) * NCH], ALU.mult
                                       ).then_inc(m_ok[0], 1)
                if not first:
                    squared(t - 1, s - 1, g)

            def tail(g, last):
                t = TPG * g + TPG - 1
                state_part(t, TPG - 1)
                gated(t, TPG - 1, last)
                squared(t, TPG - 1, g)
                k = PL["R"][1] * g + (1 if last else 2)
                pool.wait_ge(l_full["R"][1], k)
                inv_sqrt(rg[:], vs[:], k, l_free["R"][1], r_ok)
                apart(pool)
                pool.memset(SQ[:], 0.0).then_inc(sq_zero, 1)

            every(pool, tile, tail)
            ln_factor(6)
            ln_factor(7)


_ORDER = ["x", "norm_w", "in_proj_w", "conv_w", "conv_b", "dt_bias", "A_log", "Dp", "gnorm_w", "out_proj_w",
          "A", "B", "Wr", "br"]


def kernel(L0_attn_x, L0_attn_norm_w, L0_attn_in_proj_w, L0_attn_conv_w, L0_attn_conv_b, L0_attn_dt_bias,
           L0_attn_A_log, L0_attn_Dp, L0_attn_gnorm_w, L0_attn_out_proj_w, L0_ffn_A, L0_ffn_B, L0_ffn_Wr,
           L0_ffn_br):
    import numpy as np
    import concourse.bacc as bacc
    from concourse.bass_utils import run_bass_kernel_spmd

    given = [L0_attn_x, L0_attn_norm_w, L0_attn_in_proj_w, L0_attn_conv_w, L0_attn_conv_b, L0_attn_dt_bias,
             L0_attn_A_log, L0_attn_Dp, L0_attn_gnorm_w, L0_attn_out_proj_w, L0_ffn_A, L0_ffn_B, L0_ffn_Wr,
             L0_ffn_br]
    nc = bacc.Bacc("TRN2", target_bir_lowering=False, num_devices=1)
    arrays, args = {}, []
    for name, a in zip(_ORDER, given):
        a = np.ascontiguousarray(a)
        arrays[f"in_{name}"] = a
        args.append(nc.dram_tensor(f"in_{name}", a.shape, mybir.dt.from_np(a.dtype), kind="ExternalInput").ap())
    y = nc.dram_tensor("out_y", given[0].shape, F32, kind="ExternalOutput").ap()
    macaron(nc, *args, y)
    r = run_bass_kernel_spmd(nc, [arrays], core_ids=[0])
    return r.results[0]["out_y"]
```
